# Optimizing a Trainium2 kernel written in Bass

```python
import numpy as np
import jax
import jax.numpy as jnp

def _softmax(x, axis=-1):
    return jax.nn.softmax(x, axis=axis)

def _gelu(x):
    return jax.nn.gelu(x, approximate=True)

def _silu(x):
    return jax.nn.silu(x)

def _sigmoid(x):
    return jax.nn.sigmoid(x)

def _layernorm(x, axis=-1, eps=1e-05):
    m = jnp.mean(x, axis=axis, keepdims=True)
    v = jnp.var(x, axis=axis, keepdims=True)
    return (x - m) / jnp.sqrt(v + eps)

def _scatter_add(tgt, idx, src, axis=0):
    return tgt.at[idx].add(src)

def _segment_sum(src, seg, n):
    return jax.ops.segment_sum(src, seg, n)
kernel_name = 'mk_seq_preln_d2_jaxref_r4_1acac3'

def setup_inputs(seed: int=0):
    np.random.seed(seed)
    _w = jnp.asarray

    def _L0_attn_setup():
        import jax, jax.numpy as jnp
        import numpy as np
        EPS_RMS = 1e-06
        EPS_GN = 1e-05

        def rms_norm(x, w, eps=EPS_RMS):
            var = jnp.mean(x * x, axis=-1, keepdims=True)
            return w * (x * jax.lax.rsqrt(var + eps))
        key = jax.random.key(seed)
        B, T, D, H, LORA, F = (4, 512, 256, 16, 64, 1024)
        dk = D // H
        ks = jax.random.split(key, 20)
        s = 0.02

        def n(k, shape, scale=s):
            return jax.random.normal(k, shape, dtype=jnp.float32) * scale
        return {'x': n(ks[0], (B, T, D), 1.0), 'ln1_w': jnp.ones((D,), jnp.float32), 'mu_r': jax.random.uniform(ks[1], (D,), jnp.float32), 'mu_k': jax.random.uniform(ks[2], (D,), jnp.float32), 'mu_v': jax.random.uniform(ks[3], (D,), jnp.float32), 'mu_w': jax.random.uniform(ks[4], (D,), jnp.float32), 'mu_g': jax.random.uniform(ks[5], (D,), jnp.float32), 'Wr': n(ks[6], (D, D)), 'Wk': n(ks[7], (D, D)), 'Wv': n(ks[8], (D, D)), 'Wg': n(ks[9], (D, D)), 'Wo': n(ks[10], (D, D)), 'w0': n(ks[11], (D,), 0.5), 'wA': n(ks[12], (D, LORA)), 'wB': n(ks[13], (LORA, D)), 'u': n(ks[14], (H, dk), 0.5), 'gn_w': jnp.ones((H, dk), jnp.float32), 'gn_b': jnp.zeros((H, dk), jnp.float32), 'ln2_w': jnp.ones((D,), jnp.float32), 'ffn_w1': n(ks[15], (D, F)), 'ffn_w2': n(ks[16], (F, D))}
    _L0_attn_in = _L0_attn_setup()

    def _L0_ffn_setup():
        import jax, jax.numpy as jnp
        import numpy as np
        H_DIM, E_DIM = (256, 128)
        N_SHARED, N_ROUTED, TOP_K = (2, 16, 4)
        B, S = (4, 512)
        key = jax.random.key(seed)
        ks = jax.random.split(key, 6)
        sc = 1.0 / np.sqrt(H_DIM)
        ec = 1.0 / np.sqrt(E_DIM)
        return {'x': jax.random.normal(ks[0], (B, S, H_DIM), dtype=jnp.float32), 'shared_up': jax.random.uniform(ks[1], (N_SHARED, E_DIM, H_DIM), jnp.float32, -sc, sc), 'shared_down': jax.random.uniform(ks[2], (N_SHARED, H_DIM, E_DIM), jnp.float32, -ec, ec), 'routed_up': jax.random.uniform(ks[3], (N_ROUTED, E_DIM, H_DIM), jnp.float32, -sc, sc), 'routed_down': jax.random.uniform(ks[4], (N_ROUTED, H_DIM, E_DIM), jnp.float32, -ec, ec), 'router_w': jax.random.uniform(ks[5], (N_ROUTED, H_DIM), jnp.float32, -sc, sc)}
    _L0_ffn_in = _L0_ffn_setup()

    def _L1_attn_setup():
        import jax, jax.numpy as jnp
        import numpy as np
        from jax import lax
        D_MODEL = 256
        D_STATE = 16
        D_CONV = 4
        EXPAND = 2
        D_INNER = D_MODEL * EXPAND
        BATCH = 4
        SEQ = 512

        def _selective_scan(x, dt, A, B, D):
            b, L, d_inner = x.shape
            h0 = jnp.zeros((b, d_inner, A.shape[1]), x.dtype)

            def step(h, inp):
                x_t, dt_t, B_t = inp
                dA = jnp.exp(dt_t[:, :, None] * A[None])
                h = dA * h + dt_t[:, :, None] * B_t[:, None, :] * x_t[:, :, None]
                y_t = h.sum(-1) + D[None, :] * x_t
                return (h, y_t)
            xs = (jnp.swapaxes(x, 0, 1), jnp.swapaxes(dt, 0, 1), jnp.swapaxes(B, 0, 1))
            _, ys = lax.scan(step, h0, xs)
            return jnp.swapaxes(ys, 0, 1)
        key = jax.random.key(seed)
        ks = jax.random.split(key, 10)

        def lin(k, out_f, in_f):
            return jax.random.normal(k, (out_f, in_f), jnp.float32) / np.sqrt(in_f)
        x = jax.random.normal(ks[0], (BATCH, SEQ, D_MODEL), jnp.float32)
        W_in = lin(ks[1], 2 * D_INNER, D_MODEL)
        W_conv = jax.random.normal(ks[2], (D_INNER, 1, D_CONV), jnp.float32) / np.sqrt(D_CONV)
        b_conv = jax.random.normal(ks[3], (D_INNER,), jnp.float32) * 0.02
        W_x = lin(ks[4], 2 * D_STATE, D_INNER)
        W_dt = lin(ks[5], D_INNER, D_INNER)
        b_dt = jax.random.normal(ks[6], (D_INNER,), jnp.float32) * 0.02
        W_out = lin(ks[7], D_MODEL, D_INNER)
        A_log = jax.random.normal(ks[8], (D_INNER, D_STATE), jnp.float32)
        D = jnp.ones((D_INNER,), jnp.float32)
        return {'x': x, 'W_in': W_in, 'W_conv': W_conv, 'b_conv': b_conv, 'W_x': W_x, 'W_dt': W_dt, 'b_dt': b_dt, 'W_out': W_out, 'A_log': A_log, 'D': D}
    _L1_attn_in = _L1_attn_setup()

    def _L1_ffn_setup():
        import jax, jax.numpy as jnp
        from jax import lax
        import numpy as np
        D_MODEL = 256
        HIDDEN = 128
        N_EXPERTS = 32
        TOP_K = 2
        B, S = (1, 1024)

        def _moe_group(x2, router_w, wg, wu, wd, top_k):
            T = x2.shape[0]
            n_experts = router_w.shape[1]
            logits = x2 @ router_w
            scores = jax.nn.softmax(logits, axis=-1)
            expert_weights, expert_indices = lax.top_k(scores, top_k)
            flat_e = expert_indices.reshape(-1)
            flat_w = expert_weights.reshape(-1)
            flat_t = jnp.repeat(jnp.arange(T), top_k)
            order = jnp.argsort(flat_e)
            tok = flat_t[order]
            xs = x2[tok]
            group_sizes = jnp.bincount(flat_e, length=n_experts).astype(jnp.int32)
            gate = lax.ragged_dot(xs, wg, group_sizes)
            up = lax.ragged_dot(xs, wu, group_sizes)
            ys = lax.ragged_dot(jax.nn.silu(gate) * up, wd, group_sizes)
            ys = ys * flat_w[order][:, None]
            return jnp.zeros_like(x2).at[tok].add(ys)
        key = jax.random.key(seed)
        ks = jax.random.split(key, 9)
        w = lambda k, shape: jax.random.normal(k, shape, dtype=jnp.float32) * 0.02
        return {'x': jax.random.normal(ks[0], (B, S, D_MODEL), dtype=jnp.float32), 'router_w0': w(ks[1], (D_MODEL, N_EXPERTS)), 'wg0': w(ks[2], (N_EXPERTS, D_MODEL, HIDDEN)), 'wu0': w(ks[3], (N_EXPERTS, D_MODEL, HIDDEN)), 'wd0': w(ks[4], (N_EXPERTS, HIDDEN, D_MODEL)), 'router_w1': w(ks[5], (D_MODEL, N_EXPERTS)), 'wg1': w(ks[6], (N_EXPERTS, D_MODEL, HIDDEN)), 'wu1': w(ks[7], (N_EXPERTS, D_MODEL, HIDDEN)), 'wd1': w(ks[8], (N_EXPERTS, HIDDEN, D_MODEL))}
    _L1_ffn_in = _L1_ffn_setup()
    _d = {'L0_attn_x': _L0_attn_in['x'], 'L0_attn_ln1_w': _L0_attn_in['ln1_w'], 'L0_attn_mu_r': _L0_attn_in['mu_r'], 'L0_attn_mu_k': _L0_attn_in['mu_k'], 'L0_attn_mu_v': _L0_attn_in['mu_v'], 'L0_attn_mu_w': _L0_attn_in['mu_w'], 'L0_attn_mu_g': _L0_attn_in['mu_g'], 'L0_attn_Wr': _L0_attn_in['Wr'], 'L0_attn_Wk': _L0_attn_in['Wk'], 'L0_attn_Wv': _L0_attn_in['Wv'], 'L0_attn_Wg': _L0_attn_in['Wg'], 'L0_attn_Wo': _L0_attn_in['Wo'], 'L0_attn_w0': _L0_attn_in['w0'], 'L0_attn_wA': _L0_attn_in['wA'], 'L0_attn_wB': _L0_attn_in['wB'], 'L0_attn_u': _L0_attn_in['u'], 'L0_attn_gn_w': _L0_attn_in['gn_w'], 'L0_attn_gn_b': _L0_attn_in['gn_b'], 'L0_attn_ln2_w': _L0_attn_in['ln2_w'], 'L0_attn_ffn_w1': _L0_attn_in['ffn_w1'], 'L0_attn_ffn_w2': _L0_attn_in['ffn_w2'], 'L0_ffn_shared_up': _L0_ffn_in['shared_up'], 'L0_ffn_shared_down': _L0_ffn_in['shared_down'], 'L0_ffn_routed_up': _L0_ffn_in['routed_up'], 'L0_ffn_routed_down': _L0_ffn_in['routed_down'], 'L0_ffn_router_w': _L0_ffn_in['router_w'], 'L1_attn_W_in': _L1_attn_in['W_in'], 'L1_attn_W_conv': _L1_attn_in['W_conv'], 'L1_attn_b_conv': _L1_attn_in['b_conv'], 'L1_attn_W_x': _L1_attn_in['W_x'], 'L1_attn_W_dt': _L1_attn_in['W_dt'], 'L1_attn_b_dt': _L1_attn_in['b_dt'], 'L1_attn_W_out': _L1_attn_in['W_out'], 'L1_attn_A_log': _L1_attn_in['A_log'], 'L1_attn_D': _L1_attn_in['D'], 'L1_ffn_router_w0': _L1_ffn_in['router_w0'], 'L1_ffn_wg0': _L1_ffn_in['wg0'], 'L1_ffn_wu0': _L1_ffn_in['wu0'], 'L1_ffn_wd0': _L1_ffn_in['wd0'], 'L1_ffn_router_w1': _L1_ffn_in['router_w1'], 'L1_ffn_wg1': _L1_ffn_in['wg1'], 'L1_ffn_wu1': _L1_ffn_in['wu1'], 'L1_ffn_wd1': _L1_ffn_in['wd1']}
    _x0 = _d['L0_attn_x']
    _d['L0_attn_x'] = jax.random.normal(jax.random.fold_in(jax.random.key(seed), 1), (4, 2048, 256), dtype=_x0.dtype)
    del _x0
    return _d

def reference(L0_attn_x, L0_attn_ln1_w, L0_attn_mu_r, L0_attn_mu_k, L0_attn_mu_v, L0_attn_mu_w, L0_attn_mu_g, L0_attn_Wr, L0_attn_Wk, L0_attn_Wv, L0_attn_Wg, L0_attn_Wo, L0_attn_w0, L0_attn_wA, L0_attn_wB, L0_attn_u, L0_attn_gn_w, L0_attn_gn_b, L0_attn_ln2_w, L0_attn_ffn_w1, L0_attn_ffn_w2, L0_ffn_shared_up, L0_ffn_shared_down, L0_ffn_routed_up, L0_ffn_routed_down, L0_ffn_router_w, L1_attn_W_in, L1_attn_W_conv, L1_attn_b_conv, L1_attn_W_x, L1_attn_W_dt, L1_attn_b_dt, L1_attn_W_out, L1_attn_A_log, L1_attn_D, L1_ffn_router_w0, L1_ffn_wg0, L1_ffn_wu0, L1_ffn_wd0, L1_ffn_router_w1, L1_ffn_wg1, L1_ffn_wu1, L1_ffn_wd1):

    def _L0_attn_ref(x, ln1_w, mu_r, mu_k, mu_v, mu_w, mu_g, Wr, Wk, Wv, Wg, Wo, w0, wA, wB, u, gn_w, gn_b, ln2_w, ffn_w1, ffn_w2):
        import jax, jax.numpy as jnp
        import numpy as np
        EPS_RMS = 1e-06
        EPS_GN = 1e-05

        def rms_norm(x, w, eps=EPS_RMS):
            var = jnp.mean(x * x, axis=-1, keepdims=True)
            return w * (x * jax.lax.rsqrt(var + eps))
        B, T, D = x.shape
        H, dk = u.shape
        h = rms_norm(x, ln1_w)
        xx = jnp.pad(h[:, :-1], ((0, 0), (1, 0), (0, 0))) - h
        xr = h + xx * mu_r
        xk = h + xx * mu_k
        xv = h + xx * mu_v
        xw = h + xx * mu_w
        xg = h + xx * mu_g
        r = (xr @ Wr).reshape(B, T, H, dk)
        k = (xk @ Wk).reshape(B, T, H, dk)
        v = (xv @ Wv).reshape(B, T, H, dk)
        g = jax.nn.silu(xg @ Wg)
        w = w0 + jnp.tanh(xw @ wA) @ wB
        decay = jnp.exp(-jnp.exp(w)).reshape(B, T, H, dk)
        rT = jnp.moveaxis(r, 1, 0)
        kT = jnp.moveaxis(k, 1, 0)
        vT = jnp.moveaxis(v, 1, 0)
        dT = jnp.moveaxis(decay, 1, 0)

        def step(S, inps):
            rt, kt, vt, dt = inps
            kv = kt[..., :, None] * vt[..., None, :]
            o = jnp.einsum('bhk,bhkv->bhv', rt, S + u[None, :, :, None] * kv)
            S = dt[..., None] * S + kv
            return (S, o)
        S0 = jnp.zeros((B, H, dk, dk), x.dtype)
        _, oT = jax.lax.scan(step, S0, (rT, kT, vT, dT))
        o = jnp.moveaxis(oT, 0, 1)
        mean = jnp.mean(o, axis=-1, keepdims=True)
        var = jnp.var(o, axis=-1, keepdims=True)
        o = (o - mean) * jax.lax.rsqrt(var + EPS_GN) * gn_w + gn_b
        o = (o * g.reshape(B, T, H, dk)).reshape(B, T, D)
        x = x + o @ Wo
        h2 = rms_norm(x, ln2_w)
        x = x + jax.nn.gelu(h2 @ ffn_w1, approximate=False) @ ffn_w2
        return x

    def _L0_ffn_ref(x, shared_up, shared_down, routed_up, routed_down, router_w):
        import jax, jax.numpy as jnp
        import numpy as np
        H_DIM, E_DIM = (256, 128)
        N_SHARED, N_ROUTED, TOP_K = (2, 16, 4)
        B, S = (4, 512)
        b, s, h = x.shape
        xt = x.reshape(-1, h)
        up_s = jnp.einsum('th,seh->tse', xt, shared_up)
        shared = jnp.einsum('tse,she->th', jax.nn.gelu(up_s, approximate=False), shared_down)
        probs = jax.nn.softmax(xt @ router_w.T, axis=-1)
        topk_p, topk_i = jax.lax.top_k(probs, TOP_K)
        gate = jnp.zeros_like(probs).at[jnp.arange(xt.shape[0])[:, None], topk_i].add(topk_p)
        up_r = jnp.einsum('th,reh->tre', xt, routed_up)
        act = jax.nn.gelu(up_r, approximate=False) * gate[:, :, None]
        routed = jnp.einsum('tre,rhe->th', act, routed_down)
        return (shared + routed).reshape(b, s, h)

    def _L1_attn_ref(x, W_in, W_conv, b_conv, W_x, W_dt, b_dt, W_out, A_log, D):
        import jax, jax.numpy as jnp
        import numpy as np
        from jax import lax
        D_MODEL = 256
        D_STATE = 16
        D_CONV = 4
        EXPAND = 2
        D_INNER = D_MODEL * EXPAND
        BATCH = 4
        SEQ = 512

        def _selective_scan(x, dt, A, B, D):
            b, L, d_inner = x.shape
            h0 = jnp.zeros((b, d_inner, A.shape[1]), x.dtype)

            def step(h, inp):
                x_t, dt_t, B_t = inp
                dA = jnp.exp(dt_t[:, :, None] * A[None])
                h = dA * h + dt_t[:, :, None] * B_t[:, None, :] * x_t[:, :, None]
                y_t = h.sum(-1) + D[None, :] * x_t
                return (h, y_t)
            xs = (jnp.swapaxes(x, 0, 1), jnp.swapaxes(dt, 0, 1), jnp.swapaxes(B, 0, 1))
            _, ys = lax.scan(step, h0, xs)
            return jnp.swapaxes(ys, 0, 1)
        seq_len = x.shape[1]
        x_and_res = x @ W_in.T
        x_ssm, res = jnp.split(x_and_res, 2, axis=-1)
        xc = jnp.swapaxes(x_ssm, 1, 2)
        xc = lax.conv_general_dilated(xc, W_conv, window_strides=(1,), padding=[(D_CONV - 1, 0)], feature_group_count=W_conv.shape[0], dimension_numbers=('NCH', 'OIH', 'NCH'))
        xc = xc + b_conv[None, :, None]
        x_ssm = jax.nn.silu(jnp.swapaxes(xc, 1, 2))
        A = -jnp.exp(A_log)
        deltaBC = x_ssm @ W_x.T
        _delta, B_C = jnp.split(deltaBC, 2, axis=-1)
        dt = jax.nn.softplus(x_ssm @ W_dt.T + b_dt)
        y = _selective_scan(x_ssm, dt, A, B_C, D)
        y = y * jax.nn.silu(res)
        return y @ W_out.T

    def _L1_ffn_ref(x, router_w0, wg0, wu0, wd0, router_w1, wg1, wu1, wd1):
        import jax, jax.numpy as jnp
        from jax import lax
        import numpy as np
        D_MODEL = 256
        HIDDEN = 128
        N_EXPERTS = 32
        TOP_K = 2
        B, S = (1, 1024)

        def _moe_group(x2, router_w, wg, wu, wd, top_k):
            T = x2.shape[0]
            n_experts = router_w.shape[1]
            logits = x2 @ router_w
            scores = jax.nn.softmax(logits, axis=-1)
            expert_weights, expert_indices = lax.top_k(scores, top_k)
            flat_e = expert_indices.reshape(-1)
            flat_w = expert_weights.reshape(-1)
            flat_t = jnp.repeat(jnp.arange(T), top_k)
            order = jnp.argsort(flat_e)
            tok = flat_t[order]
            xs = x2[tok]
            group_sizes = jnp.bincount(flat_e, length=n_experts).astype(jnp.int32)
            gate = lax.ragged_dot(xs, wg, group_sizes)
            up = lax.ragged_dot(xs, wu, group_sizes)
            ys = lax.ragged_dot(jax.nn.silu(gate) * up, wd, group_sizes)
            ys = ys * flat_w[order][:, None]
            return jnp.zeros_like(x2).at[tok].add(ys)
        b, s, d = x.shape
        x2 = x.reshape(-1, d)
        out0 = _moe_group(x2, router_w0, wg0, wu0, wd0, TOP_K)
        out1 = _moe_group(x2, router_w1, wg1, wu1, wd1, TOP_K)
        out = (out0 * TOP_K + out1 * TOP_K) / (TOP_K + TOP_K)
        return out.reshape(b, s, d)
    x = L0_attn_x
    x = x + _L0_attn_ref(_layernorm(x, axis=-1), L0_attn_ln1_w, L0_attn_mu_r, L0_attn_mu_k, L0_attn_mu_v, L0_attn_mu_w, L0_attn_mu_g, L0_attn_Wr, L0_attn_Wk, L0_attn_Wv, L0_attn_Wg, L0_attn_Wo, L0_attn_w0, L0_attn_wA, L0_attn_wB, L0_attn_u, L0_attn_gn_w, L0_attn_gn_b, L0_attn_ln2_w, L0_attn_ffn_w1, L0_attn_ffn_w2)
    x = x + _L0_ffn_ref(_layernorm(x, axis=-1), L0_ffn_shared_up, L0_ffn_shared_down, L0_ffn_routed_up, L0_ffn_routed_down, L0_ffn_router_w)
    x = x + _L1_attn_ref(_layernorm(x, axis=-1), L1_attn_W_in, L1_attn_W_conv, L1_attn_b_conv, L1_attn_W_x, L1_attn_W_dt, L1_attn_b_dt, L1_attn_W_out, L1_attn_A_log, L1_attn_D)
    x = x + _L1_ffn_ref(_layernorm(x, axis=-1), L1_ffn_router_w0, L1_ffn_wg0, L1_ffn_wu0, L1_ffn_wd0, L1_ffn_router_w1, L1_ffn_wg1, L1_ffn_wu1, L1_ffn_wd1)
    return x

_drawn_inputs = setup_inputs


def setup_inputs(seed=0):
    import zlib

    import numpy as np

    out = dict(_drawn_inputs(seed))
    spreads = {'L0_attn_ln1_w': (1.0, 0.6),
     'L0_attn_gn_w': (1.0, 0.6),
     'L0_attn_gn_b': (0.0, 0.8),
     'L0_attn_ln2_w': (1.0, 0.6),
     'L1_attn_D': (1.0, 0.2)}
    factors = {'L0_attn_mu_r': 3.328,
     'L0_attn_mu_k': 3.42,
     'L0_attn_mu_v': 4.052,
     'L0_attn_mu_w': 8.0,
     'L0_attn_mu_g': 3.818,
     'L0_attn_w0': 6.496,
     'L0_attn_wA': 8.0,
     'L0_attn_wB': 8.0,
     'L0_attn_u': 4.146,
     'L1_attn_b_conv': 3.631,
     'L1_attn_b_dt': 8.0,
     'L1_ffn_router_w0': 8.0,
     'L1_ffn_wg0': 8.0,
     'L1_ffn_wu0': 8.0,
     'L1_ffn_wd0': 8.0,
     'L1_ffn_router_w1': 8.0,
     'L1_ffn_wg1': 8.0,
     'L1_ffn_wu1': 8.0,
     'L1_ffn_wd1': 8.0}
    for name, (base, spread) in spreads.items():
        noise = np.random.default_rng([zlib.crc32(name.encode()), seed]).standard_normal(out[name].shape)
        drawn = base * np.exp(spread * noise) if base else spread * noise
        out[name] = jnp.asarray(drawn.astype(out[name].dtype))
    for name, factor in factors.items():
        out[name] = (out[name] * factor).astype(out[name].dtype)
    return out
```

```python
from contextlib import ExitStack

import concourse.bass as bass
from concourse import mybir

P = 128
ALU = mybir.AluOpType
ACT = mybir.ActivationFunctionType
F32 = mybir.dt.float32
EPS_LN = 1e-5
EPS_RMS = 1e-6
EPS_GN = 1e-5
LANE_STEP = 1024


A_COLS = ("mu_r", "mu_k", "mu_v", "mu_w", "mu_g", "ln1_w", "ln2_w", "w0", "u", "gn_w", "gn_b")


class Mark:

    def __init__(self, lane, ordinal):
        self.lane, self.ordinal = lane, ordinal


class Lane:

    def __init__(self, nc, engine, name, stack):
        self.engine = engine
        self.sem = stack.enter_context(nc.semaphore(name))
        self.pause = stack.enter_context(nc.semaphore(name + "_pause"))
        self.base, self.count, self.waited = 0, 0, {}

    def begin(self, base):
        self.base, self.count, self.waited = base, 0, {}

    def mark(self, instruction):
        self.count += 1
        instruction.then_inc(self.sem, 1)
        return Mark(self, self.count)

    def after(self, *marks):
        for m in marks:
            if m is None or self.waited.get(m.lane, 0) >= m.ordinal:
                continue
            self.waited[m.lane] = m.ordinal
            self.engine.wait_ge(m.lane.sem, m.lane.base + m.ordinal)

    def after_alone(self, *marks):
        self.after(*marks)
        self.engine.sem_inc(self.pause, 1)

    def finish(self):
        assert self.count < LANE_STEP
        if self.count:
            self.engine.wait_ge(self.sem, self.base + self.count)
        self.engine.sem_inc(self.sem, LANE_STEP - self.count)


class Lanes:

    def __init__(self, nc, phase, stack):
        self.pe = Lane(nc, nc.tensor, f"{phase}_pe", stack)
        self.act = Lane(nc, nc.scalar, f"{phase}_act", stack)
        self.dve = Lane(nc, nc.vector, f"{phase}_dve", stack)
        self.pool = Lane(nc, nc.gpsimd, f"{phase}_pool", stack)
        self.sp = Lane(nc, nc.sync, f"{phase}_sp", stack)
        self.all = [self.pe, self.act, self.dve, self.pool, self.sp]

    def begin(self, iteration):
        for lane in self.all:
            lane.begin(iteration * LANE_STEP + 1)
        for lane in self.all:
            for other in self.all:
                if other is not lane:
                    lane.engine.wait_ge(other.sem, other.base)

    def prime(self):
        for lane in self.all:
            lane.engine.sem_inc(lane.sem, 1)

    def finish(self):
        for lane in self.all:
            lane.finish()


class Banks:

    def __init__(self, tensor, first, count):
        self.tensor, self.first, self.count, self.turn = tensor, first, count, 0
        self.freed = [None] * count

    def begin(self):
        self.turn, self.freed = 0, [None] * self.count

    def take(self, pe):
        i = self.turn % self.count
        self.turn += 1
        pe.after(self.freed[i])
        return i, self.tensor[:, self.first + i, :]


def load(nc, sem, pairs):
    for dst, src in pairs:
        nc.sync.dma_start(dst, src).then_inc(sem, 16)
    return 16 * len(pairs)


def column(v):
    return v.rearrange("(k p) -> p k", p=P)


def normalise_stats(nc, L, src, stats, mv, tiles, eps_tile_cols, eps):
    for t in range(tiles):
        last = L.dve.mark(nc.vector.bn_stats(stats[:, t, :], src(t)))
    L.dve.after_alone(last)
    for t in range(tiles):
        last = L.dve.mark(nc.vector.bn_aggr(mv[:, t, :], stats[:, t, :]))
    L.dve.after(last)
    return L.dve.mark(nc.vector.tensor_scalar(eps_tile_cols, mv[:, 0:tiles, 1], eps, None, ALU.add))


def transpose_tiles(nc, L, G, src, ident, tiles, blocks, evacuate):
    for kb in range(blocks):
        i, bank = G.take(L.pe)
        for t in range(tiles):
            last = nc.tensor.transpose(bank[:, t * P:(t + 1) * P], src(t, kb), ident[:, :])
        done = L.pe.mark(last)
        G.freed[i] = evacuate(kb, bank, done)


def matmuls(nc, out, pairs):
    for n, (lhsT, rhs) in enumerate(pairs):
        last = nc.tensor.matmul(out, lhsT, rhs, start=(n == 0), stop=(n == len(pairs) - 1))
    return last


def time_mix_phase(nc, psum, X, consts, I, x_dram):
    C, D, H, DK, LORA, F = 512, 256, 16, 16, 64, 1024
    KB, TL, NCH, HP = D // P, C // P, X.shape[1] * P // C, P // DK
    FB = F // P
    with ExitStack() as st:
        sb = lambda name, shape: st.enter_context(nc.sbuf_tensor("a_" + name, shape, F32))
        L = Lanes(nc, "a", st)
        s_load = st.enter_context(nc.semaphore("a_load"))
        W = {n: sb(n, [P, KB, D]) for n in ("Wr", "Wk", "Wv", "Wg", "Wo")}
        wA, wB = sb("wA", [P, KB, LORA]), sb("wB", [LORA, D])
        w1, w2 = sb("w1", [P, KB, F]), sb("w2", [P, FB, D])
        spread, gather = sb("spread", [P, DK, P]), sb("gather", [P, DK, P])
        head_sum = sb("head_sum", [P, P])
        chunk_mask = sb("chunk_mask", [P, NCH])
        col_pack = sb("cols", [P, len(A_COLS), KB])
        cols = {n: col_pack[:, i, :] for i, n in enumerate(A_COLS)}
        head_mean = sb("head_mean", [P, P])
        eps_gn = sb("eps_gn", [P, 1])

        stats, mv = sb("stats", [P, TL, 6]), sb("mv", [P, TL, 2])
        ve, rstd, ms, rms, sc, ssq = (sb(n, [P, TL]) for n in ("ve", "rstd", "ms", "rms", "sc", "ssq"))
        xn, hn = sb("xn", [P, TL, D]), sb("hn", [P, TL, D])
        hT, xx = sb("hT", [P, KB, C + 1]), sb("xx", [P, KB, C])
        xm = [sb(f"xm{i}", [P, KB, C]) for i in range(2)]
        rkvd = sb("rkvd", [P, 4, KB, C])
        rT, kT, vT, dT = (rkvd[:, i] for i in range(4))
        up = rkvd[:, :, :, :].rearrange("p a k c -> p (a k) c")
        gT, zg = sb("gT", [P, KB, C]), sb("zg", [P, KB, C])
        lora = sb("lora", [LORA, C])
        NR = 3
        vrep, kv, prod = (sb(n, [P, NR, C]) for n in ("vrep", "kv", "prod"))
        S = sb("S", [P, NR, C + 1])
        carry = sb("carry", [P, KB, DK])
        ruk, o, oc = sb("ruk", [P, C]), sb("o", [P, KB, C]), sb("oc", [P, C])
        act1 = sb("act1", [P, C])
        h2T = xx
        ident, neghalf = consts["ident"], consts["neghalf"]

        x_view = x_dram.rearrange("b (t p) d -> p (b t) d", p=P)
        TT = X.shape[1]
        pairs = [(X[:, i:i + 8, :], x_view[:, i:i + 8, :]) for i in range(0, TT, 8)]
        pairs += [(W[n][:, :, :], I["a_" + n]) for n in W]
        pairs += [(wA[:, :, :], I["a_wA"]), (wB[:, :], I["L0_attn_wB"]), (w1[:, :, :], I["a_w1"]), (w2[:, :, :], I["a_w2"]),
                  (spread[:, :, :], I["spread"]), (gather[:, :, :], I["gather"]), (head_sum[:, :], I["head_sum"]),
                  (chunk_mask[:, :], I["chunk_mask"]), (ident[:, :], I["ident"]), (col_pack[:, :, :], I["a_cols"])]
        loaded = load(nc, s_load, pairs)
        nc.vector.memset(neghalf[:, :], -0.5)
        nc.vector.memset(eps_gn[:, :], EPS_GN)
        nc.vector.memset(carry[:, :, :], 0.0)
        nc.vector.memset(hT[:, :, C], 0.0)
        nc.vector.wait_ge(s_load, loaded)
        nc.vector.tensor_scalar(head_mean[:, :], head_sum[:, :], 1.0 / DK, None, ALU.mult)
        nc.sync.wait_ge(s_load, loaded)
        L.prime()
        nc.all_engine_barrier()

        G = Banks(psum, 0, 4)
        VR = Banks(psum, 4, 2)
        OB = 6
        with nc.Fori(0, NCH) as c:
            L.begin(c)
            pe, act, dve, pool = L.pe, L.act, L.dve, L.pool
            G.begin(); VR.begin()
            mask = chunk_mask[:, bass.ds(c, 1)]
            tile = lambda t: X[:, bass.ds(c * TL + t, 1), :].rearrange("p a d -> p (a d)")
            prev = dve.mark(nc.vector.tensor_scalar(hT[:, :, 0], hT[:, :, C], mask, None, ALU.mult))
            m = normalise_stats(nc, L, tile, stats, mv, TL, ve[:, :], EPS_LN)
            pool.after(m)
            m_rstd = pool.mark(nc.gpsimd.tensor_tensor(rstd[:, :], ve[:, :], neghalf[:, 0:TL], ALU.pow))
            dve.after(m_rstd)
            m = dve.mark(nc.vector.tensor_tensor(ms[:, :], rstd[:, :], rstd[:, :], ALU.mult))
            for t in range(TL):
                m_xn = dve.mark(nc.vector.tensor_scalar(xn[:, t, :], tile(t), mv[:, t, 0:1], rstd[:, t:t + 1], ALU.subtract, ALU.mult))
            dve.after(m)
            m = dve.mark(nc.vector.tensor_tensor(ms[:, :], ms[:, :], mv[:, :, 1], ALU.mult))
            dve.after(m)
            m = dve.mark(nc.vector.tensor_scalar(ms[:, :], ms[:, :], EPS_RMS, None, ALU.add))
            pool.after(m)
            m = pool.mark(nc.gpsimd.tensor_tensor(rms[:, :], ms[:, :], neghalf[:, 0:TL], ALU.pow))
            dve.after(m, m_xn)
            for t in range(TL):
                m_hn = dve.mark(nc.vector.tensor_scalar(hn[:, t, :], xn[:, t, :], rms[:, t:t + 1], None, ALU.mult))
            pe.after(m_hn)

            def out_h(kb, bank, done):
                act.after(done, prev)
                nonlocal_m[kb] = act.mark(nc.scalar.activation(hT[:, kb, 1:C + 1], bank, ACT.Copy, scale=cols["ln1_w"][:, kb:kb + 1]))
                return nonlocal_m[kb]
            nonlocal_m = {}
            transpose_tiles(nc, L, G, lambda t, kb: hn[:, t, kb * P:(kb + 1) * P], ident, TL, KB, out_h)
            dve.after(prev)
            for kb in range(KB):
                dve.after(nonlocal_m[kb])
                m_xx = dve.mark(nc.vector.tensor_tensor(xx[:, kb, :], hT[:, kb, 0:C], hT[:, kb, 1:C + 1], ALU.subtract))
            used = [None, None]
            m_proj = {}
            dve.after(m_xx)
            for n, (mu, w) in enumerate((("mu_w", wA), ("mu_g", W["Wg"]), ("mu_k", W["Wk"]), ("mu_v", W["Wv"]), ("mu_r", W["Wr"]))):
                buf = xm[n % 2]
                dve.after(used[n % 2])
                for kb in range(KB):
                    m = dve.mark(nc.vector.scalar_tensor_tensor(out=buf[:, kb, :], in0=xx[:, kb, :], scalar=cols[mu][:, kb:kb + 1],
                                                                in1=hT[:, kb, 1:C + 1], op0=ALU.mult, op1=ALU.add))
                pe.after(m)
                if mu == "mu_w":
                    i, bank = G.take(pe)
                    m = pe.mark(matmuls(nc, bank[0:LORA, :], [(wA[:, kb, :], buf[:, kb, :]) for kb in range(KB)]))
                    used[n % 2] = m
                    act.after(m)
                    m = act.mark(nc.scalar.activation(lora[:, :], bank[0:LORA, :], ACT.Tanh))
                    G.freed[i] = m
                    pe.after(m)
                    for ob in range(KB):
                        i, bank = G.take(pe)
                        m = pe.mark(matmuls(nc, bank, [(wB[:, ob * P:(ob + 1) * P], lora[:, :])]))
                        act.after(m)
                        m = act.mark(nc.scalar.activation(dT[:, ob, :], bank, ACT.Exp, bias=cols["w0"][:, ob:ob + 1]))
                        G.freed[i] = m
                        act.after(m)
                        m_proj["d", ob] = act.mark(nc.scalar.activation(dT[:, ob, :], dT[:, ob, :], ACT.Exp, scale=-1.0))
                    continue
                for ob in range(KB):
                    i, bank = G.take(pe)
                    m = pe.mark(matmuls(nc, bank, [(w[:, kb, ob * P:(ob + 1) * P], buf[:, kb, :]) for kb in range(KB)]))
                    act.after(m)
                    if mu == "mu_g":
                        m = act.mark(nc.scalar.activation(zg[:, ob, :], bank, ACT.Tanh, scale=0.5))
                        dve.after(m)
                        m_proj["g", ob] = dve.mark(nc.vector.scalar_tensor_tensor(out=gT[:, ob, :], in0=zg[:, ob, :], scalar=1.0, in1=bank,
                                                                                  op0=ALU.add, op1=ALU.mult))
                        G.freed[i] = m_proj["g", ob]
                    else:
                        dst = {"mu_k": kT, "mu_v": vT, "mu_r": rT}[mu]
                        m_proj[mu[-1], ob] = act.mark(nc.scalar.copy(dst[:, ob, :], bank))
                        G.freed[i] = m_proj[mu[-1], ob]
                used[n % 2] = m if mu != "mu_g" else used[n % 2]
                if mu == "mu_g":
                    used[n % 2] = m_proj["g", KB - 1]
            steps = KB * DK
            m_rep, m_kv, m_scan, m_prod, m_sum, m_cr = {}, {}, {}, {}, {}, {}
            pool.after(m_proj["k", KB - 1])
            dve.after(m_proj["d", KB - 1], m_proj["r", KB - 1])
            for s in range(steps + 3):
                if s < steps:
                    hb, v = divmod(s, DK)
                    i, bank = VR.take(pe)
                    pe.after(m_proj["v", hb])
                    m = pe.mark(matmuls(nc, bank, [(spread[:, v, :], vT[:, hb, :])]))
                    act.after(m, m_kv.get(s - NR))
                    m_rep[s] = act.mark(nc.scalar.copy(vrep[:, s % NR, :], bank))
                    VR.freed[i] = m_rep[s]
                    pool.after(m_rep[s], m_scan.get(s - NR))
                    m_kv[s] = pool.mark(nc.gpsimd.tensor_tensor(kv[:, s % NR, :], kT[:, hb, :], vrep[:, s % NR, :], ALU.mult))
                q = s - 1
                if 0 <= q < steps:
                    hb, v = divmod(q, DK)
                    dve.after(m_prod.get(q - NR))
                    m = dve.mark(nc.vector.tensor_scalar(S[:, q % NR, 0:1], carry[:, hb, v:v + 1], mask, None, ALU.mult))
                    dve.after(m, m_kv[q])
                    m_scan[q] = dve.mark(nc.vector.tensor_tensor_scan(S[:, q % NR, 1:C + 1], dT[:, hb, :], kv[:, q % NR, :],
                                                                      S[:, q % NR, 0:1], ALU.mult, ALU.add))
                    dve.after(m_scan[q], m_sum.get(q - NR))
                    m_prod[q] = dve.mark(nc.vector.tensor_tensor(prod[:, q % NR, :], rT[:, hb, :], S[:, q % NR, 0:C], ALU.mult))
                    m_cr[q] = dve.mark(nc.vector.tensor_copy(carry[:, hb, v:v + 1], S[:, q % NR, C:C + 1]))
                q = s - 2
                if 0 <= q < steps:
                    hb, v = divmod(q, DK)
                    pe.after(m_prod[q])
                    m_sum[q] = pe.mark(nc.tensor.matmul(psum[:, OB + hb, :], gather[:, v, :], prod[:, q % NR, :], start=(v == 0), stop=(v == DK - 1)))
            m_gate = {}
            dve.after(m_proj["k", KB - 1], m_proj["v", KB - 1])
            prev_r = None
            for hb in range(KB):
                dve.after(prev_r)
                m = dve.mark(nc.vector.scalar_tensor_tensor(out=ruk[:, :], in0=rT[:, hb, :], scalar=cols["u"][:, hb:hb + 1], in1=kT[:, hb, :],
                                                            op0=ALU.mult, op1=ALU.mult))
                i, bank = G.take(pe)
                pe.after(m)
                m = pe.mark(matmuls(nc, bank, [(head_sum[:, :], ruk[:, :])]))
                prev_r = m
                dve.after(m)
                m = dve.mark(nc.vector.tensor_tensor(o[:, hb, :], bank, vT[:, hb, :], ALU.mult))
                G.freed[i] = m
                dve.after(m, m_sum[hb * DK + DK - 1])
                m = dve.mark(nc.vector.tensor_tensor(o[:, hb, :], psum[:, OB + hb, :], o[:, hb, :], ALU.add))
                i, bank = G.take(pe)
                pe.after(m)
                m = pe.mark(matmuls(nc, bank, [(head_mean[:, :], o[:, hb, :])]))
                dve.after(m)
                m = dve.mark(nc.vector.tensor_tensor(o[:, hb, :], o[:, hb, :], bank, ALU.subtract))
                G.freed[i] = m
                act.after(m)
                m = act.mark(nc.scalar.activation(act1[:, :], o[:, hb, :], ACT.Square))
                i, bank = G.take(pe)
                pe.after(m)
                m = pe.mark(matmuls(nc, bank, [(head_mean[:, :], act1[:, :])]))
                if hb == 0:
                    nc.scalar.preload_act_table_set("natural_log_exp_and_others")
                act.after(m)
                m = act.mark(nc.scalar.activation(zg[:, hb, :], bank, ACT.Ln, bias=eps_gn[:, 0:1]))
                G.freed[i] = m
                act.after(m)
                m = act.mark(nc.scalar.activation(zg[:, hb, :], zg[:, hb, :], ACT.Exp, scale=-0.5))
                dve.after(m)
                m = dve.mark(nc.vector.tensor_tensor(o[:, hb, :], o[:, hb, :], zg[:, hb, :], ALU.mult))
                dve.after(m)
                m = dve.mark(nc.vector.tensor_scalar(o[:, hb, :], o[:, hb, :], cols["gn_w"][:, hb:hb + 1], cols["gn_b"][:, hb:hb + 1],
                                                     ALU.mult, ALU.add))
                dve.after(m)
                m_gate[hb] = dve.mark(nc.vector.scalar_tensor_tensor(out=o[:, hb, :], in0=o[:, hb, :], scalar=0.5, in1=gT[:, hb, :],
                                                                     op0=ALU.mult, op1=ALU.mult))
            pe.after(m_gate[KB - 1])
            for t in range(TL):
                i, bank = G.take(pe)
                m = pe.mark(matmuls(nc, bank[:, 0:D], [(o[:, kb, t * P:(t + 1) * P], W["Wo"][:, kb, :]) for kb in range(KB)]))
                dve.after(m)
                m_x1 = dve.mark(nc.vector.tensor_tensor(xn[:, t, :], xn[:, t, :], bank[:, 0:D], ALU.add))
                G.freed[i] = m_x1
                act.after(m_x1)
                m_sq = act.mark(nc.scalar.activation(hn[:, t, :], xn[:, t, :], ACT.Square, accum_out=ssq[:, t:t + 1]))
            dve.after(m_sq)
            m = dve.mark(nc.vector.tensor_scalar(ms[:, :], ssq[:, :], 1.0 / D, EPS_RMS, ALU.mult, ALU.add))
            pool.after(m)
            m = pool.mark(nc.gpsimd.tensor_tensor(rms[:, :], ms[:, :], neghalf[:, 0:TL], ALU.pow))
            dve.after(m, m_x1)
            for t in range(TL):
                m_hn = dve.mark(nc.vector.tensor_scalar(hn[:, t, :], xn[:, t, :], rms[:, t:t + 1], None, ALU.mult))
            pe.after(m_hn)
            m_h2 = {}

            def out_h2(kb, bank, done):
                act.after(done)
                m_h2[kb] = act.mark(nc.scalar.activation(h2T[:, kb, :], bank, ACT.Copy, scale=cols["ln2_w"][:, kb:kb + 1]))
                return m_h2[kb]
            transpose_tiles(nc, L, G, lambda t, kb: hn[:, t, kb * P:(kb + 1) * P], ident, TL, KB, out_h2)
            for t in range(TL):
                m_res = dve.mark(nc.vector.tensor_tensor(tile(t), tile(t), xn[:, t, :], ALU.add))
            pe.after(m_h2[KB - 1])
            for f in range(FB):
                i, bank = G.take(pe)
                m = pe.mark(matmuls(nc, bank, [(w1[:, kb, f * P:(f + 1) * P], h2T[:, kb, :]) for kb in range(KB)]))
                act.after(m)
                m_up = act.mark(nc.scalar.activation(up[:, f, :], bank, ACT.Gelu))
                G.freed[i] = m_up
            pe.after(m_up)
            dve.after(m_res)
            for t in range(TL):
                i, bank = G.take(pe)
                m = pe.mark(matmuls(nc, bank[:, 0:D], [(up[:, f, t * P:(t + 1) * P], w2[:, f, :]) for f in range(FB)]))
                dve.after(m)
                G.freed[i] = dve.mark(nc.vector.tensor_tensor(tile(t), tile(t), bank[:, 0:D], ALU.add))
            L.finish()
        nc.all_engine_barrier()


def selective_scan_phase(nc, psum, X, consts, I):
    C, D, E, N, KC = 512, 256, 512, 16, 4
    KB, EB, TL, NCH = D // P, E // P, C // P, X.shape[1] * P // C
    with ExitStack() as st:
        sb = lambda name, shape: st.enter_context(nc.sbuf_tensor("c_" + name, shape, F32))
        L = Lanes(nc, "c", st)
        s_load = st.enter_context(nc.semaphore("c_load"))
        W_in, W_dt, W_out = sb("W_in", [P, KB, 2 * E]), sb("W_dt", [P, EB, E]), sb("W_out", [P, EB, D])
        W_B = sb("W_B", [P, EB, N])
        spread = sb("spread", [N, N, P])
        chunk_mask = sb("chunk_mask", [P, NCH])
        col_pack = sb("cols", [P, EB, N + KC + 3])
        A = col_pack[:, :, 0:N]
        conv_w = col_pack[:, :, N:N + KC]
        b_conv, b_dt, skip = (col_pack[:, :, N + KC + i:N + KC + i + 1] for i in range(3))

        stats, mv = sb("stats", [P, TL, 6]), sb("mv", [P, TL, 2])
        ve, rstd = sb("ve", [P, TL]), sb("rstd", [P, TL])
        hn, xT = sb("hn", [P, TL, D]), sb("xT", [P, KB, C])
        pre = sb("pre", [P, EB, C + KC - 1])
        xs, dt, dtx = (sb(n, [P, EB, C]) for n in ("xs", "dt", "dtx"))
        gate = sb("gate", [P, TL, E])
        B = sb("B", [N, C])
        Brep = sb("Brep", [P, N, C])
        tmp = sb("tmp", [P, 2, C])
        NR = 3
        dbx, hs = sb("dbx", [P, NR, C]), sb("hs", [P, NR, C])
        carry = sb("carry", [P, EB, N])
        ident, neghalf = consts["ident"], consts["neghalf"]
        y, yT = dtx, dt

        loaded = load(nc, s_load, [(W_in[:, :, :], I["c_W_in"]), (W_dt[:, :, :], I["c_W_dt"]), (W_out[:, :, :], I["c_W_out"]),
                                   (W_B[:, :, :], I["c_W_B"]), (spread[:, :, :], I["state_spread"]), (chunk_mask[:, :], I["chunk_mask"]),
                                   (col_pack[:, :, :], I["c_cols"])])
        nc.vector.memset(carry[:, :, :], 0.0)
        nc.vector.memset(pre[:, :, C:C + KC - 1], 0.0)
        nc.sync.wait_ge(s_load, loaded)
        nc.all_engine_barrier()
        with nc.semaphore("c_setup") as s_setup:
            nc.scalar.activation(A, A, ACT.Exp).then_inc(s_setup, 1)
            nc.vector.wait_ge(s_setup, 1)
            nc.vector.tensor_scalar(A, A, -1.0, None, ALU.mult)
            nc.vector.tensor_scalar(col_pack[:, :, N:N + KC + 1], col_pack[:, :, N:N + KC + 1], 0.5, None, ALU.mult)
            L.prime()
            nc.all_engine_barrier()

        G = Banks(psum, 0, 3)
        DA = Banks(psum, 3, 3)
        YB = 6
        pe, act, dve, pool = L.pe, L.act, L.dve, L.pool
        with nc.Fori(0, NCH) as c:
            L.begin(c)
            G.begin(); DA.begin()
            mask = chunk_mask[:, bass.ds(c, 1)]
            tile = lambda t: X[:, bass.ds(c * TL + t, 1), :].rearrange("p a d -> p (a d)")
            m_pre = dve.mark(nc.vector.tensor_scalar(pre[:, :, 0:KC - 1], pre[:, :, C:C + KC - 1], mask, None, ALU.mult))
            m_carry = dve.mark(nc.vector.tensor_scalar(carry[:, :, :], carry[:, :, :], mask, None, ALU.mult))
            m = normalise_stats(nc, L, tile, stats, mv, TL, ve[:, :], EPS_LN)
            pool.after(m)
            m = pool.mark(nc.gpsimd.tensor_tensor(rstd[:, :], ve[:, :], neghalf[:, 0:TL], ALU.pow))
            dve.after(m)
            for t in range(TL):
                m_hn = dve.mark(nc.vector.tensor_scalar(hn[:, t, :], tile(t), mv[:, t, 0:1], rstd[:, t:t + 1], ALU.subtract, ALU.mult))
            pe.after(m_hn)
            m_x = {}

            def out_x(kb, bank, done):
                act.after(done)
                m_x[kb] = act.mark(nc.scalar.copy(xT[:, kb, :], bank))
                return m_x[kb]
            transpose_tiles(nc, L, G, lambda t, kb: hn[:, t, kb * P:(kb + 1) * P], ident, TL, KB, out_x)
            pe.after(m_x[KB - 1])
            m_xs = {}
            for e in range(EB):
                i, bank = G.take(pe)
                m = pe.mark(matmuls(nc, bank, [(W_in[:, kb, e * P:(e + 1) * P], xT[:, kb, :]) for kb in range(KB)]))
                act.after(m, m_pre)
                m = act.mark(nc.scalar.copy(pre[:, e, KC - 1:KC - 1 + C], bank))
                G.freed[i] = m
                dve.after(m, m_pre)
                m = dve.mark(nc.vector.tensor_scalar(dtx[:, e, :], pre[:, e, KC - 1:KC - 1 + C], conv_w[:, e, KC - 1:KC], b_conv[:, e, :], ALU.mult, ALU.add))
                for j in range(KC - 1):
                    dve.after(m)
                    m = dve.mark(nc.vector.scalar_tensor_tensor(out=dtx[:, e, :], in0=pre[:, e, j:j + C], scalar=conv_w[:, e, j:j + 1],
                                                                in1=dtx[:, e, :], op0=ALU.mult, op1=ALU.add))
                act.after(m, m_xs.get(e - 2))
                m = act.mark(nc.scalar.activation(tmp[:, e % 2, :], dtx[:, e, :], ACT.Tanh))
                dve.after(m)
                m_xs[e] = dve.mark(nc.vector.scalar_tensor_tensor(out=xs[:, e, :], in0=tmp[:, e % 2, :], scalar=1.0, in1=dtx[:, e, :],
                                                                  op0=ALU.add, op1=ALU.mult))
            for t in range(TL):
                i, bank = G.take(pe)
                m = pe.mark(matmuls(nc, bank, [(xT[:, kb, t * P:(t + 1) * P], W_in[:, kb, E:2 * E]) for kb in range(KB)]))
                act.after(m)
                m = act.mark(nc.scalar.activation(gate[:, t, :], bank, ACT.Tanh, scale=0.5))
                dve.after(m)
                m_gate = dve.mark(nc.vector.scalar_tensor_tensor(out=gate[:, t, :], in0=gate[:, t, :], scalar=1.0, in1=bank,
                                                                 op0=ALU.add, op1=ALU.mult))
                G.freed[i] = m_gate
            nc.scalar.preload_act_table_set("natural_log_exp_and_others")
            pe.after(m_xs[EB - 1])
            i, bank = G.take(pe)
            m = pe.mark(matmuls(nc, bank[0:N, :], [(W_B[:, e, :], xs[:, e, :]) for e in range(EB)]))
            act.after(m)
            m_B = act.mark(nc.scalar.copy(B[:, :], bank[0:N, :]))
            G.freed[i] = m_B
            m_dtx = {}
            m_l = {}
            for e in range(EB):
                i, bank = G.take(pe)
                m = pe.mark(matmuls(nc, bank, [(W_dt[:, k, e * P:(e + 1) * P], xs[:, k, :]) for k in range(EB)]))
                act.after(m)
                m_z = act.mark(nc.scalar.activation(dt[:, e, :], bank, ACT.Identity, bias=b_dt[:, e, :]))
                G.freed[i] = m_z
                act.after(m_z, m_l.get(e - 2))
                m = act.mark(nc.scalar.activation(tmp[:, e % 2, :], dt[:, e, :], ACT.Abs))
                act.after(m)
                m = act.mark(nc.scalar.activation(tmp[:, e % 2, :], tmp[:, e % 2, :], ACT.Exp, scale=-1.0))
                act.after(m)
                m = act.mark(nc.scalar.activation(tmp[:, e % 2, :], tmp[:, e % 2, :], ACT.Ln, bias=1.0))
                dve.after(m)
                m_l[e] = dve.mark(nc.vector.scalar_tensor_tensor(out=dt[:, e, :], in0=dt[:, e, :], scalar=0.0, in1=tmp[:, e % 2, :],
                                                                 op0=ALU.max, op1=ALU.add))
                dve.after(m_l[e])
                m_dtx[e] = dve.mark(nc.vector.tensor_tensor(dtx[:, e, :], dt[:, e, :], xs[:, e, :], ALU.mult))
            m_skip = {}
            for e in range(EB):
                dve.after(m_dtx[e])
                m_skip[e] = dve.mark(nc.vector.tensor_scalar(xs[:, e, :], xs[:, e, :], skip[:, e, :], None, ALU.mult))
            steps = EB * N
            m_rep, m_da, m_dbx, m_scan, m_sum, m_carried = {}, {}, {}, {}, {}, {}
            m_y = {}
            for s in range(steps + 3):
                if s < steps:
                    e, n = divmod(s, N)
                    if e == 0:
                        i, bank = G.take(pe)
                        pe.after(m_B)
                        m = pe.mark(matmuls(nc, bank, [(spread[:, n, :], B[:, :])]))
                        act.after(m)
                        m_rep[n] = act.mark(nc.scalar.copy(Brep[:, n, :], bank))
                        G.freed[i] = m_rep[n]
                    act.after(m_l[e])
                    i, bank = DA.take(act)
                    m_da[s] = act.mark(nc.scalar.activation(bank, dt[:, e, :], ACT.Exp, scale=A[:, e, n:n + 1]))
                    pool.after(m_rep[n], m_dtx[e], m_scan.get(s - NR))
                    m_dbx[s] = pool.mark(nc.gpsimd.tensor_tensor(dbx[:, s % NR, :], dtx[:, e, :], Brep[:, n, :], ALU.mult))
                    dve.after(m_da[s], m_dbx[s], m_sum.get(s - NR), m_carried.get(s - NR), m_carry)
                    m_scan[s] = dve.mark(nc.vector.tensor_tensor_scan(hs[:, s % NR, :], bank, dbx[:, s % NR, :], carry[:, e, n:n + 1],
                                                                      ALU.mult, ALU.add))
                    DA.freed[i] = m_scan[s]
                q = s - 1
                if 0 <= q < steps:
                    e, n = divmod(q, N)
                    dve.after(m_scan[q])
                    m_carried[q] = dve.mark(nc.vector.tensor_copy(carry[:, e, n:n + 1], hs[:, q % NR, C - 1:C]))
                    pe.after(m_scan[q])
                    if n == 0:
                        pe.after(m_y.get(e - 2), m_skip[e])
                        for t in range(TL):
                            nc.tensor.matmul(psum[:, YB + e % 2, t * P:(t + 1) * P], xs[:, e, t * P:(t + 1) * P], ident[:, :],
                                             is_transpose=True, start=(t == 0), stop=False, skip_group_check=True)
                    for t in range(TL):
                        last = nc.tensor.matmul(psum[:, YB + e % 2, t * P:(t + 1) * P], hs[:, q % NR, t * P:(t + 1) * P], ident[:, :],
                                                is_transpose=True, start=False, stop=(n == N - 1 and t == TL - 1), skip_group_check=True)
                    m_sum[q] = pe.mark(last)
                    if n == N - 1:
                        dve.after(m_sum[q], m_gate)
                        m_y[e] = dve.mark(nc.vector.scalar_tensor_tensor(
                            out=gate[:, :, e * P:(e + 1) * P], in0=psum[:, YB + e % 2, :].rearrange("p (t d) -> p t d", t=TL), scalar=0.5,
                            in1=gate[:, :, e * P:(e + 1) * P], op0=ALU.mult, op1=ALU.mult))
            m_yT = {}

            def out_y(e, bank, done):
                act.after(done)
                m_yT[e] = act.mark(nc.scalar.copy(yT[:, e, :], bank))
                return m_yT[e]
            pe.after(m_y[EB - 1])
            act.after(m_scan[steps - 1])
            transpose_tiles(nc, L, G, lambda t, e: gate[:, t, e * P:(e + 1) * P], ident, TL, EB, out_y)
            pe.after(m_yT[EB - 1])
            for t in range(TL):
                i, bank = G.take(pe)
                m = pe.mark(matmuls(nc, bank[:, 0:D], [(yT[:, e, t * P:(t + 1) * P], W_out[:, e, :]) for e in range(EB)]))
                dve.after(m)
                G.freed[i] = dve.mark(nc.vector.tensor_tensor(tile(t), tile(t), bank[:, 0:D], ALU.add))
            L.finish()
        nc.all_engine_barrier()


def router(nc, L, G, xT, W_router, R, iota, groups, experts, top):
    TL, KB = 4, 2
    NE = groups * experts
    pe, act, dve = L.pe, L.act, L.dve
    rows = TL * groups
    i, bank = G.take(pe)
    for t in range(TL):
        m = matmuls(nc, bank[:, t * NE:(t + 1) * NE], [(xT[:, kb, t * P:(t + 1) * P], W_router[:, kb, :]) for kb in range(KB)])
    m = pe.mark(m)
    logits = bank[:, 0:TL * NE].rearrange("p (r e) -> p r e", r=rows)
    dve.after(m)
    m = dve.mark(nc.vector.tensor_reduce(R["peak"][:, :], logits, mybir.AxisListType.X, ALU.max))
    dve.after(m)
    m = dve.mark(nc.vector.tensor_tensor(R["prob"][:, :, :], logits, R["peak"][:, :].unsqueeze(2).broadcast_to([P, rows, experts]), ALU.subtract))
    G.freed[i] = m
    act.after(m)
    m = act.mark(nc.scalar.activation(R["prob"][:, :, :], R["prob"][:, :, :], ACT.Exp))
    dve.after(m)
    m = dve.mark(nc.vector.tensor_reduce(R["total"][:, :], R["prob"][:, :, :], mybir.AxisListType.X, ALU.add))
    dve.after(m)
    m = dve.mark(nc.vector.reciprocal(R["total"][:, :], R["total"][:, :]))
    dve.after(m)
    m = dve.mark(nc.vector.tensor_tensor(R["prob"][:, :, :], R["prob"][:, :, :], R["total"][:, :].unsqueeze(2).broadcast_to([P, rows, experts]), ALU.mult))
    dve.after_alone(m)
    for r in range(rows):
        m = dve.mark(nc.vector.max(R["best"][:, r, :], R["prob"][:, r, :]))
    dve.after_alone(m)
    for r in range(rows):
        m = dve.mark(nc.vector.max_index(R["index"][:, r, :], R["best"][:, r, :], R["prob"][:, r, :]))
    dve.after(m)
    m = dve.mark(nc.vector.tensor_copy(R["index_f"][:, :, :], R["index"][:, :, 0:top]))
    dve.after(m)
    m = dve.mark(nc.vector.tensor_tensor(R["onehot"][:, :, :, :], iota[:, 0:experts].unsqueeze(1).unsqueeze(1).broadcast_to([P, rows, top, experts]),
                                         R["index_f"][:, :, :].unsqueeze(3).broadcast_to([P, rows, top, experts]), ALU.is_equal))
    dve.after(m)
    return dve.mark(nc.vector.tensor_reduce(R["chosen"][:, :, :], R["onehot"][:, :, :, :].rearrange("p r s e -> p r e s"), mybir.AxisListType.X, ALU.add))


def router_buffers(nc, st, name, groups, experts, top):
    rows = 4 * groups
    shapes = {"peak": [P, rows], "total": [P, rows], "prob": [P, rows, experts], "best": [P, rows, 8], "index_f": [P, rows, top],
              "onehot": [P, rows, top, experts], "chosen": [P, rows, experts]}
    R = {n: st.enter_context(nc.sbuf_tensor(f"{name}_{n}", s, F32)) for n, s in shapes.items()}
    R["index"] = st.enter_context(nc.sbuf_tensor(f"{name}_index", [P, rows, 8], mybir.dt.uint32))
    return R


def normalised_chunk(nc, L, G, tile, stats, mv, ve, rstd, hn, xT, consts, KB, TL):
    m = normalise_stats(nc, L, tile, stats, mv, TL, ve[:, :], EPS_LN)
    L.pool.after(m)
    m = L.pool.mark(nc.gpsimd.tensor_tensor(rstd[:, :], ve[:, :], consts["neghalf"][:, 0:TL], ALU.pow))
    L.dve.after(m)
    for t in range(TL):
        m_hn = L.dve.mark(nc.vector.tensor_scalar(hn[:, t, :], tile(t), mv[:, t, 0:1], rstd[:, t:t + 1], ALU.subtract, ALU.mult))
    L.pe.after(m_hn)
    m_x = {}

    def out_x(kb, bank, done):
        L.act.after(done)
        m_x[kb] = L.act.mark(nc.scalar.copy(xT[:, kb, :], bank))
        return m_x[kb]
    transpose_tiles(nc, L, G, lambda t, kb: hn[:, t, kb * P:(kb + 1) * P], consts["ident"], TL, KB, out_x)
    L.pe.after(m_x[KB - 1])
    return m_x[KB - 1]


def dense_experts_phase(nc, psum, X, consts, I):
    C, D, E, S, TOP = 512, 256, 16, 2, 4
    KB, TL, NCH = D // P, C // P, X.shape[1] * P // C
    with ExitStack() as st:
        sb = lambda name, shape: st.enter_context(nc.sbuf_tensor("b_" + name, shape, F32))
        L = Lanes(nc, "b", st)
        s_load = st.enter_context(nc.semaphore("b_load"))
        W_up, W_down = sb("W_up", [P, S + E, KB, P]), sb("W_down", [P, S + E, D])
        W_router, iota = sb("W_router", [P, KB, E]), sb("iota", [P, 32])
        stats, mv = sb("stats", [P, TL, 6]), sb("mv", [P, TL, 2])
        ve, rstd = sb("ve", [P, TL]), sb("rstd", [P, TL])
        hn, xT = sb("hn", [P, TL, D]), sb("xT", [P, KB, C])
        NH = 3
        hidden = sb("hidden", [P, NH, C])
        gates = sb("gates", [P, TL, E])
        R = router_buffers(nc, st, "b", 1, E, TOP)
        loaded = load(nc, s_load, [(W_up[:, :, :, :], I["b_up"]), (W_down[:, :, :], I["b_down"]), (W_router[:, :, :], I["b_router"]), (iota[:, :], I["iota"])])
        nc.sync.wait_ge(s_load, loaded)
        L.prime()
        nc.all_engine_barrier()
        G = Banks(psum, 0, 4)
        DN = Banks(psum, 4, 4)
        pe, act, dve, pool = L.pe, L.act, L.dve, L.pool
        with nc.Fori(0, NCH) as c:
            L.begin(c)
            G.begin(); DN.begin()
            tile = lambda t: X[:, bass.ds(c * TL + t, 1), :].rearrange("p a d -> p (a d)")
            normalised_chunk(nc, L, G, tile, stats, mv, ve, rstd, hn, xT, consts, KB, TL)
            m = router(nc, L, G, xT, W_router, R, iota, 1, E, TOP)
            dve.after(m)
            m_gates = dve.mark(nc.vector.tensor_tensor(gates[:, :, :], R["chosen"][:, :, :], R["prob"][:, :, :], ALU.mult))
            nc.scalar.preload_act_table(ACT.Gelu)
            m_hidden, m_down = {}, {}
            m_acc = {}
            for e in range(S + E + 1):
                if e < S + E:
                    i, bank = G.take(pe)
                    m = pe.mark(matmuls(nc, bank, [(W_up[:, e, kb, :], xT[:, kb, :]) for kb in range(KB)]))
                    act.after(m, m_down.get(e - NH))
                    m_hidden[e] = act.mark(nc.scalar.activation(hidden[:, e % NH, :], bank, ACT.Gelu))
                    G.freed[i] = m_hidden[e]
                q = e - 1
                if q < 0:
                    continue
                pe.after(m_hidden[q])
                for half in range(2):
                    i, bank = DN.take(pe)
                    for t in (2 * half, 2 * half + 1):
                        m = nc.tensor.matmul(bank[:, (t % 2) * D:(t % 2 + 1) * D], hidden[:, q % NH, t * P:(t + 1) * P], W_down[:, q, :], start=True, stop=True)
                    m_down[q] = pe.mark(m)
                    dve.after(m_down[q])
                    for t in (2 * half, 2 * half + 1):
                        part = bank[:, (t % 2) * D:(t % 2 + 1) * D]
                        dve.after(m_acc.get(t))
                        if q < S:
                            m_acc[t] = dve.mark(nc.vector.tensor_tensor(tile(t), tile(t), part, ALU.add))
                        else:
                            dve.after(m_gates)
                            m_acc[t] = dve.mark(nc.vector.scalar_tensor_tensor(out=tile(t), in0=part, scalar=gates[:, t, q - S:q - S + 1], in1=tile(t),
                                                                               op0=ALU.mult, op1=ALU.add))
                    DN.freed[i] = m_acc[2 * half + 1]
            L.finish()
        nc.all_engine_barrier()


class SortedExperts:
    GROUPS, EXPERTS, TOP, SLOTS, UNROLL, RING = 2, 32, 2, 256, 8, 4

    def __init__(self, tokens):
        self.picks = self.GROUPS * self.TOP
        self.ne = self.GROUPS * self.EXPERTS
        self.tiles = tokens * self.picks // self.SLOTS + self.ne
        assert self.tiles % self.UNROLL == 0 and self.tiles + self.RING <= 2 * P and self.UNROLL % self.RING == 0
        self.rows = (self.tiles + self.RING) * self.SLOTS


def clear_sorted_rows(nc, zeros, sorted_x, sem):
    per = zeros.shape[1]
    dst = sorted_x.rearrange("(a n p r) d -> a p n (r d)", p=P, r=per // sorted_x.shape[1], n=14)
    for a in range(dst.shape[0]):
        nc.sync.dma_start(dst[a], zeros[:, :].unsqueeze(1).broadcast_to([P, 14, per])).then_inc(sem, 16)
    return 16 * dst.shape[0]


def sorted_experts_phase(nc, psum, X, consts, I, out, sorted_x, sorted_y, expert_list):
    Z = SortedExperts(X.shape[1] * P)
    C, D = 512, 256
    KB, TL, TT = D // P, C // P, X.shape[1]
    NCH, PK, NE, E, TOP, GR, SL = TT // TL, Z.picks, Z.ne, Z.EXPERTS, Z.TOP, Z.GROUPS, Z.SLOTS
    U32, I32, AX = mybir.dt.uint32, mybir.dt.int32, mybir.AxisListType.X
    tile_of = lambda c: (lambda t: X[:, bass.ds(c * TL + t, 1), :].rearrange("p a d -> p (a d)"))
    flat = lambda ap: ap.rearrange("p a b -> p (a b)")
    with ExitStack() as st:
        sb = lambda name, shape, dt=F32: st.enter_context(nc.sbuf_tensor("d_" + name, shape, dt))
        s_load = st.enter_context(nc.semaphore("d_load"))
        W_router, iota, tri, ones = sb("W_router", [P, KB, NE]), sb("iota", [P, 32]), sb("tri", [P, P]), sb("ones", [P, P])
        tile_no = sb("tile_no", [P, 2])
        picks, weights, ranks, rows = (sb(n, [P, TT, PK]) for n in ("picks", "weights", "ranks", "rows"))
        means, rstds = sb("means", [P, TT]), sb("rstds", [P, TT])
        before = sb("before", [P, NE])
        base, ends, in_tiles, work = (sb(n, [P, NE]) for n in ("base", "ends", "in_tiles", "work"))
        whole = sb("whole", [P, NE], I32)
        e_col, e_int = sb("e_col", [P, 2]), sb("e_int", [P, 2], I32)
        e_row = sb("e_row", [1, 2 * P], I32)
        loaded = load(nc, s_load, [(W_router[:, :, :], I["d_router"]), (iota[:, :], I["iota"]), (tri[:, :], I["tri"]), (tile_no[:, :], I["tile_no"])])
        nc.vector.memset(before[:, :], 0.0)
        nc.vector.memset(ones[:, :], 1.0)
        nc.sync.wait_ge(s_load, loaded)
        nc.all_engine_barrier()

        with ExitStack() as s1:
            sb1 = lambda name, shape: s1.enter_context(nc.sbuf_tensor("d1_" + name, shape, F32))
            L = Lanes(nc, "d1", s1)
            stats, mv = sb1("stats", [P, TL, 6]), sb1("mv", [P, TL, 2])
            ve, rstd = sb1("ve", [P, TL]), sb1("rstd", [P, TL])
            hn, xT = sb1("hn", [P, TL, D]), sb1("xT", [P, KB, C])
            at_pick = sb1("at_pick", [P, TL * GR, TOP, E])
            total = sb1("chunk_total", [P, NE])
            R = router_buffers(nc, s1, "d1", GR, E, TOP)
            L.prime()
            nc.all_engine_barrier()
            G = Banks(psum, 0, 6)
            pe, act, dve, pool = L.pe, L.act, L.dve, L.pool
            with nc.Fori(0, NCH) as c:
                L.begin(c)
                G.begin()
                part = bass.ds(c * TL, TL)
                normalised_chunk(nc, L, G, tile_of(c), stats, mv, ve, rstd, hn, xT, consts, KB, TL)
                nc.vector.tensor_copy(means[:, part], mv[:, :, 0])
                nc.vector.tensor_copy(rstds[:, part], rstd[:, :])
                m = router(nc, L, G, xT, W_router, R, iota, GR, E, TOP)
                chosen = R["chosen"][:, :, :].rearrange("p (t g) e -> p t (g e)", t=TL)
                dve.mark(nc.vector.tensor_copy(picks[:, part, :].rearrange("p t k -> p (t k)"), flat(R["index_f"][:, :, :])))
                dve.mark(nc.vector.tensor_scalar(weights[:, part, :].rearrange("p t (g k) -> p (t g) k", g=GR), R["best"][:, :, 0:TOP], 0.5, None, ALU.mult))
                pe.after(m)
                i, bank = G.take(pe)
                for t in range(TL):
                    m = matmuls(nc, bank[:, t * NE:(t + 1) * NE], [(tri[:, :], chosen[:, t, :])] + [(ones[:, :], chosen[:, q, :]) for q in range(t)]
                                + [(ones[:, :], before[:, :])])
                m_rank = pe.mark(m)
                dve.after(m_rank)
                m = dve.mark(nc.vector.tensor_tensor(
                    at_pick[:, :, :, :], R["onehot"][:, :, :, :],
                    bank[:, 0:TL * NE].rearrange("p (r e) -> p r e", e=E).unsqueeze(2).broadcast_to([P, TL * GR, TOP, E]), ALU.mult))
                G.freed[i] = m
                dve.after(m)
                dve.mark(nc.vector.tensor_reduce(ranks[:, part, :].rearrange("p t k -> p (t k)"), at_pick[:, :, :, :].rearrange("p r s e -> p (r s) e"), AX, ALU.add))
                m = dve.mark(nc.vector.tensor_reduce(total[:, :], chosen.rearrange("p t x -> p x t"), AX, ALU.add))
                dve.after(m)
                dve.mark(nc.vector.tensor_tensor(before[:, :], before[:, :], total[:, :], ALU.add))
                L.finish()
            nc.all_engine_barrier()

        with nc.semaphore("d_place") as s_place, nc.semaphore("d_list") as s_list:
            steps = [0]

            def then(instruction):
                steps[0] += 1
                instruction.then_inc(s_place, 1)
                nc.vector.wait_ge(s_place, steps[0])
            counts = psum[:, 0, 0:NE]
            then(nc.tensor.matmul(counts, ones[:, :], before[:, :], start=True, stop=True))
            then(nc.vector.tensor_scalar(work[:, :], counts, float(SL - 1), None, ALU.add))
            then(nc.vector.tensor_copy(whole[:, :], work[:, :]))
            then(nc.vector.tensor_scalar(whole[:, :], whole[:, :], SL.bit_length() - 1, None, ALU.arith_shift_right))
            then(nc.vector.tensor_copy(in_tiles[:, :], whole[:, :]))
            then(nc.vector.tensor_tensor_scan(ends[:, :], ones[:, 0:NE], in_tiles[:, :], 0.0, ALU.mult, ALU.add))
            then(nc.vector.tensor_tensor(base[:, :], ends[:, :], in_tiles[:, :], ALU.subtract))
            then(nc.vector.tensor_scalar(base[:, :], base[:, :], float(SL), None, ALU.mult))
            for j in range(2):
                then(nc.vector.tensor_scalar(work[:, :], ends[:, :], tile_no[:, j:j + 1], None, ALU.is_le))
                then(nc.vector.tensor_reduce(e_col[:, j:j + 1], work[:, :], AX, ALU.add))
            then(nc.vector.tensor_scalar(e_col[:, :], e_col[:, :], float(NE - 1), None, ALU.min))
            then(nc.vector.tensor_copy(e_int[:, :], e_col[:, :]))
            nc.sync.wait_ge(s_place, steps[0])
            with nc.allow_non_contiguous_dma(reason="256 expert numbers, once"):
                for j in range(2):
                    nc.sync.dma_start(expert_list[j * P:(j + 1) * P].rearrange("(p a) -> p a", a=1), e_int[:, j:j + 1]).then_inc(s_list, 16)
            nc.sync.wait_ge(s_list, 32)
            nc.sync.dma_start(e_row[:, :], expert_list.rearrange("(a n) -> a n", a=1)).then_inc(s_list, 16)
            nc.sync.wait_ge(s_list, 48)
            nc.all_engine_barrier()

        with ExitStack() as s2:
            sb2 = lambda name, shape, dt=F32: s2.enter_context(nc.sbuf_tensor("d2_" + name, shape, dt))
            L = Lanes(nc, "d2", s2)
            s_sent = s2.enter_context(nc.semaphore("d2_sent"))
            hn = sb2("hn", [P, TL, D])
            onehot = sb2("onehot", [P, GR, TL, TOP, E])
            start = sb2("start", [P, TL, PK])
            to_row = sb2("to_row", [P, TL * PK], U32)
            L.prime()
            nc.all_engine_barrier()
            pe, act, dve, pool = L.pe, L.act, L.dve, L.pool
            per_chunk = 16 * TL * PK
            with nc.Fori(0, NCH) as c:
                L.begin(c)
                tile, part = tile_of(c), bass.ds(c * TL, TL)
                for g in range(GR):
                    mine = onehot[:, g, :, :, :]
                    m = dve.mark(nc.vector.tensor_tensor(
                        mine, iota[:, 0:E].unsqueeze(1).unsqueeze(1).broadcast_to([P, TL, TOP, E]),
                        picks[:, part, g * TOP:(g + 1) * TOP].unsqueeze(3).broadcast_to([P, TL, TOP, E]), ALU.is_equal))
                    dve.after(m)
                    m = dve.mark(nc.vector.tensor_tensor(
                        mine, mine, base[:, g * E:(g + 1) * E].unsqueeze(1).unsqueeze(1).broadcast_to([P, TL, TOP, E]), ALU.mult))
                    dve.after(m)
                    m = dve.mark(nc.vector.tensor_reduce(start[:, :, g * TOP:(g + 1) * TOP], mine, AX, ALU.add))
                dve.after(m)
                m = dve.mark(nc.vector.tensor_tensor(start[:, :, :], start[:, :, :], ranks[:, part, :], ALU.add))
                dve.after(m)
                dve.mark(nc.vector.tensor_copy(rows[:, part, :].rearrange("p t k -> p (t k)"), flat(start[:, :, :])))
                m_row = dve.mark(nc.vector.tensor_copy(to_row[:, :], flat(start[:, :, :])))
                for t in range(TL):
                    m = dve.mark(nc.vector.tensor_scalar(hn[:, t, :], tile(t), means[:, bass.ds(c * TL + t, 1)], rstds[:, bass.ds(c * TL + t, 1)],
                                                         ALU.subtract, ALU.mult))
                    pool.after_alone(m_row, m)
                    for k in range(PK):
                        nc.gpsimd.indirect_dma_start(out=sorted_x, out_offset=bass.IndirectOffsetOnAxis(ap=to_row[:, t * PK + k:t * PK + k + 1], axis=0),
                                                     in_=hn[:, t, :], in_offset=None, bounds_check=Z.rows - 1).then_inc(s_sent, 16)
                nc.gpsimd.wait_ge(s_sent, c * per_chunk + per_chunk)
                L.finish()
            nc.all_engine_barrier()

        with ExitStack() as s3:
            sb3 = lambda name, shape: s3.enter_context(nc.sbuf_tensor("d3_" + name, shape, F32))
            L = Lanes(nc, "d3", s3)
            RN, UN, HB = Z.RING, Z.UNROLL, SL // P
            xs, w, ys = sb3("xs", [P, RN, HB, D]), sb3("w", [P, RN, 2 * KB * P + D]), sb3("ys", [P, RN, HB, D])
            xT, hg = sb3("xT", [P, 3, KB, SL]), sb3("hg", [P, 3, SL])
            s_x, s_w, s_y = ([s3.enter_context(nc.semaphore(f"d3_{n}{i}")) for i in range(RN)] for n in "xwy")
            rows_in = sorted_x.rearrange("(j h p) d -> j p h d", p=P, h=HB)
            rows_out = sorted_y.rearrange("(j h p) d -> j p h d", p=P, h=HB)
            weights_in = I["d_experts"]

            def fetch(j, slot):
                e = nc.sync.value_load(e_row[0:1, bass.ds(j, 1)], min_val=0, max_val=NE - 1)
                nc.sync.dma_start(w[:, slot, :], weights_in[bass.ds(e, 1), :, :].rearrange("a p n -> p (a n)")).then_inc(s_w[slot], 16)
                nc.sync.dma_start(xs[:, slot, :, :], rows_in[bass.ds(j, 1), :, :, :].rearrange("a p h d -> p (a h) d")).then_inc(s_x[slot], 16)
            L.prime()
            for slot in range(RN):
                fetch(slot, slot)
                nc.sync.sem_inc(s_y[slot], 16)
            nc.all_engine_barrier()
            TB, GU, DN = Banks(psum, 0, 2), Banks(psum, 2, 3), Banks(psum, 5, 3)
            pe, act, dve, pool, sp = L.pe, L.act, L.dve, L.pool, L.sp
            w_gate = lambda slot, kb: w[:, slot, kb * P:(kb + 1) * P]
            w_up = lambda slot, kb: w[:, slot, (KB + kb) * P:(KB + kb + 1) * P]
            w_down = lambda slot: w[:, slot, 2 * KB * P:]
            with nc.Fori(0, Z.tiles // UN) as i:
                L.begin(i)
                for b in (TB, GU, DN):
                    b.begin()
                m_xT, m_gu, m_h, m_dn = {}, {}, {}, {}
                uses = UN // RN
                for s in range(UN + 2):
                    if s < UN:
                        slot, use = s % RN, s // RN
                        pe.engine.wait_ge(s_x[slot], i * (16 * uses) + 16 * (use + 1))
                        b, bank = TB.take(pe)
                        for kb in range(KB):
                            for h in range(HB):
                                m = nc.tensor.transpose(bank[:, kb * SL + h * P:kb * SL + (h + 1) * P], xs[:, slot, h, kb * P:(kb + 1) * P], consts["ident"][:, :])
                        m = pe.mark(m)
                        act.after(m, m_gu.get(s - 3))
                        m_xT[s] = act.mark(nc.scalar.copy(xT[:, s % 3, :, :].rearrange("p k c -> p (k c)"), bank))
                        TB.freed[b] = m_xT[s]
                    q = s - 1
                    if 0 <= q < UN:
                        slot, use = q % RN, q // RN
                        pe.engine.wait_ge(s_w[slot], i * (16 * uses) + 16 * (use + 1))
                        b, bank = GU.take(pe)
                        pe.after(m_xT[q])
                        for half, wt in enumerate((w_gate, w_up)):
                            m = matmuls(nc, bank[:, half * SL:(half + 1) * SL], [(wt(slot, kb), xT[:, q % 3, kb, :]) for kb in range(KB)])
                        m_gu[q] = pe.mark(m)
                        act.after(m_gu[q], m_dn.get(q - 3))
                        m = act.mark(nc.scalar.activation(hg[:, q % 3, :], bank[:, 0:SL], ACT.Silu))
                        dve.after(m)
                        m_h[q] = dve.mark(nc.vector.tensor_tensor(hg[:, q % 3, :], hg[:, q % 3, :], bank[:, SL:2 * SL], ALU.mult))
                        GU.freed[b] = m_h[q]
                    q = s - 2
                    if 0 <= q < UN:
                        slot, use = q % RN, q // RN
                        b, bank = DN.take(pe)
                        pe.after(m_h[q])
                        for h in range(HB):
                            m = nc.tensor.matmul(bank[:, h * D:(h + 1) * D], hg[:, q % 3, h * P:(h + 1) * P], w_down(slot), start=True, stop=True)
                        m_dn[q] = pe.mark(m)
                        dve.after(m_dn[q])
                        dve.engine.wait_ge(s_y[slot], i * (16 * uses) + 16 * (use + 1))
                        m = dve.mark(nc.vector.tensor_copy(ys[:, slot, :, :].rearrange("p h d -> p (h d)"), bank))
                        DN.freed[b] = m
                        sp.after(m_dn[q])
                        fetch(i * UN + q + RN, slot)
                        sp.after(m)
                        nc.sync.dma_start(rows_out[bass.ds(i * UN + q, 1), :, :, :].rearrange("a p h d -> p (a h) d"), ys[:, slot, :, :]).then_inc(s_y[slot], 16)
                L.finish()
            for slot in range(RN):
                nc.sync.wait_ge(s_y[slot], 16 * (Z.tiles // RN + 1))
                nc.sync.wait_ge(s_x[slot], 16 * (Z.tiles // RN + 1))
                nc.sync.wait_ge(s_w[slot], 16 * (Z.tiles // RN + 1))
            nc.all_engine_barrier()

        with ExitStack() as s4:
            L = Lanes(nc, "d4", s4)
            got = s4.enter_context(nc.sbuf_tensor("d4_got", [P, TL * PK, D], F32))
            from_row = s4.enter_context(nc.sbuf_tensor("d4_from_row", [P, TL * PK], U32))
            s_got = [s4.enter_context(nc.semaphore(f"d4_got{t}")) for t in range(TL)]
            s_out = s4.enter_context(nc.semaphore("d4_out"))
            out_view = out.rearrange("b (t p) d -> p (b t) d", p=P)
            L.prime()
            nc.all_engine_barrier()
            pe, act, dve, pool, sp = L.pe, L.act, L.dve, L.pool, L.sp
            with nc.Fori(0, NCH) as c:
                L.begin(c)
                tile, part = tile_of(c), bass.ds(c * TL, TL)
                m = dve.mark(nc.vector.tensor_copy(from_row[:, :], rows[:, part, :].rearrange("p t k -> p (t k)")))
                pool.after_alone(m)
                for t in range(TL):
                    for k in range(PK):
                        nc.gpsimd.indirect_dma_start(out=got[:, t * PK + k, :], out_offset=None, in_=sorted_y,
                                                     in_offset=bass.IndirectOffsetOnAxis(ap=from_row[:, t * PK + k:t * PK + k + 1], axis=0),
                                                     bounds_check=Z.tiles * SL - 1).then_inc(s_got[t], 16)
                for t in range(TL):
                    dve.engine.wait_ge(s_got[t], c * (16 * PK) + 16 * PK)
                    for k in range(PK):
                        m = dve.mark(nc.vector.scalar_tensor_tensor(out=tile(t), in0=got[:, t * PK + k, :],
                                                                    scalar=weights[:, bass.ds(c * TL + t, 1), k:k + 1].rearrange("p a b -> p (a b)"),
                                                                    in1=tile(t), op0=ALU.mult, op1=ALU.add))
                        dve.after(m)
                sp.after(m)
                nc.sync.dma_start(out_view[:, part, :], X[:, part, :]).then_inc(s_out, 16)
                L.finish()
            nc.sync.wait_ge(s_out, 16 * NCH)
            nc.all_engine_barrier()


def store_x(nc, X, out):
    with nc.semaphore("s_out") as s_out:
        TT = X.shape[1]
        view = out.rearrange("b (t p) d -> p (b t) d", p=P)
        n = 0
        for i in range(0, TT, 8):
            nc.sync.dma_start(view[:, i:i + 8, :], X[:, i:i + 8, :]).then_inc(s_out, 16)
            n += 16
        nc.sync.wait_ge(s_out, n)


def build(nc, I, out, phases="ABCD"):
    with ExitStack() as st:
        T = out.shape[0] * out.shape[1]
        X = st.enter_context(nc.sbuf_tensor("X", [P, T // P, out.shape[2]], F32))
        consts = {"ident": st.enter_context(nc.sbuf_tensor("ident", [P, P], F32)),
                  "neghalf": st.enter_context(nc.sbuf_tensor("neghalf", [P, 4], F32))}
        psum = st.enter_context(nc.psum_tensor("psum", [P, 8, 512], F32))
        if "L" in phases:
            with nc.semaphore("ld") as q:
                v = I["L0_attn_x"].rearrange("b (t p) d -> p (b t) d", p=P)
                nc.sync.dma_start(X[:, :, :], v).then_inc(q, 16)
                nc.sync.dma_start(consts["ident"][:, :], I["ident"]).then_inc(q, 16)
                nc.sync.wait_ge(q, 32)
                nc.vector.memset(consts["neghalf"][:, :], -0.5)
                nc.all_engine_barrier()
        if "A" in phases:
            time_mix_phase(nc, psum, X, consts, I, I["L0_attn_x"])
        if "B" in phases:
            dense_experts_phase(nc, psum, X, consts, I)
        if "C" in phases:
            selective_scan_phase(nc, psum, X, consts, I)
        if "D" in phases:
            Z = SortedExperts(T)
            D = out.shape[2]
            sorted_x = nc.dram_tensor("sorted_x", (Z.rows, D), F32).ap()
            sorted_y = nc.dram_tensor("sorted_y", (Z.tiles * Z.SLOTS, D), F32).ap()
            expert_list = nc.dram_tensor("expert_list", (2 * P,), mybir.dt.int32).ap()
            with nc.sbuf_tensor("zeros", [P, 2 * D], F32) as zeros, nc.semaphore("s_clear") as s_clear:
                nc.vector.memset(zeros[:, :], 0.0)
                nc.all_engine_barrier()
                nc.sync.wait_ge(s_clear, clear_sorted_rows(nc, zeros, sorted_x, s_clear))
                nc.all_engine_barrier()
            sorted_experts_phase(nc, psum, X, consts, I, out, sorted_x, sorted_y, expert_list)
        else:
            store_x(nc, X, out)


def shape_constants():
    import numpy as np
    dk, per_seq, chunks = 16, 4, 16
    p = np.arange(P)
    same = (p[:, None] // dk == p[None, :] // dk)
    spread = np.stack([same & (p[:, None] % dk == v) for v in range(dk)], axis=1)
    gather = np.stack([same & (p[None, :] % dk == v) for v in range(dk)], axis=1)
    mask = np.tile((np.arange(chunks) % per_seq != 0)[None, :], (P, 1))
    state_spread = np.repeat(np.eye(dk, dtype=np.float32)[:, :, None], P, axis=2)
    tile_no = p[:, None] + P * np.arange(2)[None, :]
    return {"tri": (p[:, None] < p[None, :]).astype(np.float32), "tile_no": tile_no.astype(np.float32),
            "iota": np.tile(np.arange(32, dtype=np.float32), (P, 1)), "state_spread": state_spread, "ident": np.eye(P, dtype=np.float32), "spread": spread.astype(np.float32), "gather": gather.astype(np.float32),
            "head_sum": same.astype(np.float32), "chunk_mask": mask.astype(np.float32)}


def by_rows(w):
    return w.reshape(-1, P, w.shape[-1]).transpose(1, 0, 2)


def layouts(i):
    import numpy as np
    i = {k: np.asarray(v) for k, v in i.items()}
    a = {n: i["L0_attn_" + n] for n in ("Wr", "Wk", "Wv", "Wg", "Wo", "wA")}
    a["w1"], a["w2"] = i["L0_attn_ffn_w1"], i["L0_attn_ffn_w2"]
    d = {"a_" + k: by_rows(v) for k, v in a.items()}
    d["a_cols"] = np.stack([i["L0_attn_" + n].reshape(-1, P).T for n in A_COLS], axis=1)
    c = {n: i["L1_attn_" + n] for n in ("W_in", "W_dt", "W_out", "W_x", "W_conv", "A_log", "b_conv", "b_dt", "D")}
    d["c_W_in"], d["c_W_dt"], d["c_W_out"] = (by_rows(c[n].T) for n in ("W_in", "W_dt", "W_out"))
    d["c_W_B"] = by_rows(c["W_x"][c["W_x"].shape[0] // 2:].T)
    rows = np.concatenate([c["A_log"], c["W_conv"][:, 0, :]] + [c[n][:, None] for n in ("b_conv", "b_dt", "D")], axis=1)
    d["c_cols"] = by_rows(rows)
    experts = []
    for g in "01":
        for n in ("wg", "wu"):
            a = i[f"L1_ffn_{n}{g}"]
            experts.append(a.reshape(a.shape[0], -1, P, P).transpose(0, 2, 1, 3).reshape(a.shape[0], P, -1))
        experts.append(i[f"L1_ffn_wd{g}"])
    d["d_experts"] = np.concatenate([np.concatenate(experts[0:3], axis=2), np.concatenate(experts[3:6], axis=2)])
    d["d_router"] = by_rows(np.concatenate([i["L1_ffn_router_w0"], i["L1_ffn_router_w1"]], axis=1))
    up = np.concatenate([i["L0_ffn_shared_up"], i["L0_ffn_routed_up"]])
    down = np.concatenate([i["L0_ffn_shared_down"], i["L0_ffn_routed_down"]])
    d["b_up"] = up.reshape(up.shape[0], P, -1, P).transpose(3, 0, 2, 1)
    d["b_down"] = down.transpose(2, 0, 1)
    d["b_router"] = by_rows(i["L0_ffn_router_w"].T)
    d["L0_attn_wB"] = i["L0_attn_wB"]
    d["L0_attn_x"] = i["L0_attn_x"]
    return d


def kernel(**inputs):
    import numpy as _np
    import concourse.bacc as _bacc
    from concourse import mybir as _mybir
    from concourse.bass_utils import run_bass_kernel_spmd as _run

    nc = _bacc.Bacc("TRN2", target_bir_lowering=False, num_devices=1)
    nc.disable_value_cache = True
    arrays, aps = {}, {}
    for name, a in list(layouts(inputs).items()) + list(shape_constants().items()):
        a = _np.ascontiguousarray(a)
        arrays[f"in_{name}"] = a
        aps[name] = nc.dram_tensor(f"in_{name}", a.shape, _mybir.dt.from_np(a.dtype), kind="ExternalInput").ap()
    out = nc.dram_tensor("out_x", inputs["L0_attn_x"].shape, _mybir.dt.float32, kind="ExternalOutput").ap()
    build(nc, aps, out)
    r = _run(nc, [arrays], core_ids=[0])
    return r.results[0]["out_x"]
```

```python
from contextlib import ExitStack

import concourse.bass as bass
from concourse import mybir

P = 128
ALU = mybir.AluOpType
ACT = mybir.ActivationFunctionType
F32, BF16 = mybir.dt.float32, mybir.dt.bfloat16
EPS_LN = 1e-5
EPS_RMS = 1e-6
EPS_GN = 1e-5
LANE_STEP = 2048


A_COLS = ("mu_r", "mu_k", "mu_v", "mu_w", "mu_g", "ln1_w", "ln2_w", "w0", "u", "gn_w", "gn_b")


class Mark:

    def __init__(self, lane, ordinal, body):
        self.lane, self.ordinal, self.body = lane, ordinal, body


class Lane:

    def __init__(self, nc, engine, name, stack):
        self.engine = engine
        self.sem = stack.enter_context(nc.semaphore(name))
        self.pause = stack.enter_context(nc.semaphore(name + "_pause"))
        self.base, self.count, self.waited, self.body = 0, 0, {}, 0

    def begin(self, base, body):
        self.base, self.count, self.waited, self.body = base, 0, {}, body

    def mark(self, instruction):
        self.count += 1
        instruction.then_inc(self.sem, 1)
        return Mark(self, self.count, self.body)

    def after(self, *marks):
        for m in marks:
            if m is None or m.body != self.body or self.waited.get(m.lane, 0) >= m.ordinal:
                continue
            self.waited[m.lane] = m.ordinal
            self.engine.wait_ge(m.lane.sem, m.lane.base + m.ordinal)

    def after_alone(self, *marks):
        self.after(*marks)
        self.engine.sem_inc(self.pause, 1)

    def finish(self):
        assert self.count < LANE_STEP
        if self.count:
            self.engine.wait_ge(self.sem, self.base + self.count)
        self.engine.sem_inc(self.sem, LANE_STEP - self.count)


class Lanes:

    def __init__(self, nc, phase, stack):
        self.pe = Lane(nc, nc.tensor, f"{phase}_pe", stack)
        self.act = Lane(nc, nc.scalar, f"{phase}_act", stack)
        self.dve = Lane(nc, nc.vector, f"{phase}_dve", stack)
        self.pool = Lane(nc, nc.gpsimd, f"{phase}_pool", stack)
        self.sp = Lane(nc, nc.sync, f"{phase}_sp", stack)
        self.all = [self.pe, self.act, self.dve, self.pool, self.sp]
        self.bodies = 0

    def begin(self, index):
        self.bodies += 1
        for lane in self.all:
            lane.begin(index * LANE_STEP + 1, self.bodies)
        for lane in self.all:
            for other in self.all:
                if other is not lane:
                    lane.engine.wait_ge(other.sem, other.base)
        self.sp.engine.sem_inc(self.sp.pause, 1)

    def prime(self):
        for lane in self.all:
            lane.engine.sem_inc(lane.sem, 1)

    def finish(self):
        for lane in self.all:
            lane.finish()


class Banks:

    def __init__(self, tensor, first, count):
        self.tensor, self.first, self.count, self.turn = tensor, first, count, 0
        self.freed = [None] * count

    def begin(self):
        self.turn, self.freed = 0, [None] * self.count

    def take(self, lane):
        i = self.turn % self.count
        self.turn += 1
        lane.after(self.freed[i])
        return i, self.tensor[:, self.first + i, :]


class Shared:

    def __init__(self, tensor):
        self.tensor, self.readers = tensor, []

    def claim(self, *lanes):
        for lane in lanes:
            lane.after(*self.readers)
        self.readers = []


class Background:

    def __init__(self, *stages):
        self.stages, self.due = list(stages), 0.0

    def pull(self, pieces):
        self.due += pieces
        while self.due >= 1 and self.stages:
            try:
                next(self.stages[0])
                self.due -= 1
            except StopIteration:
                self.stages.pop(0)

    def drain(self):
        self.pull(1 << 30)


def load(nc, sem, pairs):
    for dst, src in pairs:
        nc.sync.dma_start(dst, src).then_inc(sem, 16)
    return 16 * len(pairs)


def column(v):
    return v.rearrange("(k p) -> p k", p=P)


def matmuls(nc, out, pairs):
    for n, (lhsT, rhs) in enumerate(pairs):
        last = nc.tensor.matmul(out, lhsT, rhs, start=(n == 0), stop=(n == len(pairs) - 1))
    return last


def layer0_phase(nc, psum, consts, I, x_in, x_out, clear):
    C, D, H, DK, LORA, F = 512, 256, 16, 16, 64, 1024
    E, SH, TOP = 16, 2, 4
    KB, TL, HP, FB = D // P, C // P, P // DK, F // P
    NCH = x_in.shape[0] * x_in.shape[1] // C
    AX = mybir.AxisListType.X
    with ExitStack() as st:
        sb = lambda name, shape, dt=F32: st.enter_context(nc.sbuf_tensor("a_" + name, shape, dt))
        sem = lambda name: st.enter_context(nc.semaphore("a_" + name))
        L = Lanes(nc, "a", st)
        pe, act, dve, pool, sp = L.pe, L.act, L.dve, L.pool, L.sp
        s_load, s_xa, s_xb, s_store = sem("load"), sem("xa"), sem("xb"), sem("store")
        W = {n: sb(n, [P, KB, D]) for n in ("Wr", "Wk", "Wv", "Wg", "Wo")}
        wA, wB = sb("wA", [P, KB, LORA]), sb("wB", [LORA, D])
        w1, w2 = sb("w1", [P, KB, F]), sb("w2", [P, FB, D])
        spread = sb("spread", [P, DK, P])
        head_of = sb("head_of", [P, HP])
        chunk_mask = sb("chunk_mask", [P, NCH + 1])
        col_pack = sb("cols", [P, len(A_COLS), KB])
        cols = {n: col_pack[:, i, :] for i, n in enumerate(A_COLS)}
        gn_w, gn_b = sb("gn_w", [P, D]), sb("gn_b", [P, D])
        eps_gn = sb("eps_gn", [P, 1])
        W_up, W_down = sb("W_up", [P, SH + E, KB, P]), sb("W_down", [P, SH + E, D])
        W_router, iota = sb("W_router", [P, KB, E]), sb("iota", [P, 32])
        ident, neghalf = consts["ident"], consts["neghalf"]

        rkvd = [sb(f"rkvd{i}", [P, 4, KB, C]) for i in range(2)]
        gate, bonus = ([sb(f"{n}{i}", [P, TL, D]) for i in range(2)] for n in ("gate", "bonus"))
        mv = [sb(f"mv{i}", [P, TL, 2]) for i in range(2)]
        rstd = [sb(f"rstd{i}", [P, TL]) for i in range(2)]
        NR = 3
        vrep, kv, prod = (sb(n, [P, NR, C]) for n in ("vrep", "kv", "prod"))
        S = sb("S", [P, NR, C + 1])
        carry = sb("carry", [P, KB * DK])
        o = Shared(sb("o", [P, TL, D]))
        xa, xb, x1 = sb("xa", [P, TL, D]), sb("xb", [P, TL, D]), sb("x1", [P, TL, D])
        hn, bgT = Shared(sb("hn", [P, TL, D])), Shared(sb("bgT", [P, KB, C]))
        hT = Shared(sb("hT", [P, KB, C + 1]))
        xm = [Shared(sb(f"xm{i}", [P, KB, C])) for i in range(2)]
        NH = 3
        hidden = sb("hidden", [P, NH, C])
        lora = hidden[0:LORA, 0, :]
        stats = sb("stats", [P, TL, 6])
        ve, ms, rms, ssq = (sb(n, [P, TL]) for n in ("ve", "ms", "rms", "ssq"))
        heads = sb("heads", [P, TL * H])
        bon = sb("bon", [P, TL * H])
        gates = sb("gates", [P, TL, E])
        R = router_buffers(nc, st, "a", 1, E, TOP)

        pairs = [(W[n][:, :, :], I["a_" + n]) for n in W]
        pairs += [(wA[:, :, :], I["a_wA"]), (wB[:, :], I["L0_attn_wB"]), (w1[:, :, :], I["a_w1"]), (w2[:, :, :], I["a_w2"]),
                  (spread[:, :, :], I["spread"]), (head_of[:, :], I["head_of"]), (chunk_mask[:, :], I["chunk_mask"]),
                  (ident[:, :], I["ident"]), (col_pack[:, :, :], I["a_cols"]), (gn_w[:, :], I["a_gn_w"].partition_broadcast(P)),
                  (gn_b[:, :], I["a_gn_b"].partition_broadcast(P)), (W_up[:, :, :, :], I["b_up"]), (W_down[:, :, :], I["b_down"]),
                  (W_router[:, :, :], I["b_router"]), (iota[:, :], I["iota"])]
        loaded = load(nc, s_load, pairs)
        nc.vector.memset(neghalf[:, :], -0.5)
        nc.vector.memset(eps_gn[:, :], EPS_GN)
        nc.vector.memset(carry[:, :], 0.0)
        nc.vector.memset(hT.tensor[:, :, C], 0.0)
        nc.vector.wait_ge(s_load, loaded)
        nc.vector.tensor_scalar(gn_w[:, :], gn_w[:, :], 0.5, None, ALU.mult)
        nc.vector.tensor_scalar(gn_b[:, :], gn_b[:, :], 0.5, None, ALU.mult)
        nc.sync.wait_ge(s_load, loaded)
        nc.sync.sem_inc(s_store, 16)
        L.prime()
        nc.all_engine_barrier()

        chunks_in = x_in.rearrange("b (c t p) d -> p (b c) t d", p=P, t=TL)
        chunks_out = x_out.rearrange("(c t p) d -> p c t d", p=P, t=TL)
        chunk_of = lambda view, c: view[:, bass.ds(c, 1), :, :].rearrange("p a t d -> p (a t) d")
        VR, OB, DN, G = Banks(psum, 0, 2), 2, Banks(psum, 4, 2), Banks(psum, 6, 2)
        o_free, o_parts = [None], {}
        scan_done = [[], []]
        post_done = [[], []]
        xa_read, hid_read, hid_turn = [None], {}, [0]
        xb_read = [None]
        flat = lambda ap: ap.rearrange("p a b -> p (a b)")

        def transposed(src, dst, scale=None, rows=(0, TL)):
            marks = []
            for kb in range(KB):
                i, bank = G.take(pe)
                for t in range(TL):
                    m = nc.tensor.transpose(bank[:, t * P:(t + 1) * P], src[:, t, kb * P:(kb + 1) * P], ident[:, :])
                m = pe.mark(m)
                yield
                act.after(m)
                if scale is None:
                    m = act.mark(nc.scalar.copy(dst(kb), bank))
                else:
                    m = act.mark(nc.scalar.activation(dst(kb), bank, ACT.Copy, scale=scale(kb)))
                G.freed[i] = m
                marks.append(m)
            return marks

        def variance(src, mvb):
            for t in range(TL):
                m = dve.mark(nc.vector.bn_stats(stats[:, t, :], src[:, t, :]))
            dve.after_alone(m)
            for t in range(TL):
                m = dve.mark(nc.vector.bn_aggr(mvb[:, t, :], stats[:, t, :]))
            yield
            dve.after(m)
            return dve.mark(nc.vector.tensor_scalar(ve[:, :], mvb[:, :, 1], EPS_LN, None, ALU.add))

        def inverse_root(dst, src, m):
            pool.after(m)
            return pool.mark(nc.gpsimd.tensor_tensor(dst, src, neghalf[:, 0:TL], ALU.pow))

        def load_xa(c, n):
            sp.after(xa_read[0])
            nc.sync.dma_start(xa[:, :, :], chunk_of(chunks_in, c)).then_inc(s_xa, 16)

        def load_xb(c):
            sp.engine.wait_ge(s_store, c * 16 + 16)
            nc.sync.dma_start(xb[:, :, :], chunk_of(chunks_in, c)).then_inc(s_xb, 16)

        def before(c, slot):
            rT, kT, vT, dT = (rkvd[slot][:, i] for i in range(4))
            done = {}
            h = hT.tensor
            hT.claim(dve, act)
            prev = dve.mark(nc.vector.tensor_scalar(h[:, :, 0], h[:, :, C], chunk_mask[:, bass.ds(c, 1)], None, ALU.mult))
            dve.engine.wait_ge(s_xa, c * 16 + 16)
            dve.after(*post_done[slot])
            m = yield from variance(xa, mv[slot])
            m = inverse_root(rstd[slot][:, :], ve[:, :], m)
            yield
            dve.after(m)
            m = dve.mark(nc.vector.tensor_tensor(ms[:, :], rstd[slot][:, :], rstd[slot][:, :], ALU.mult))
            dve.after(m)
            m = dve.mark(nc.vector.tensor_tensor(ms[:, :], ms[:, :], mv[slot][:, :, 1], ALU.mult))
            dve.after(m)
            m = dve.mark(nc.vector.tensor_scalar(ms[:, :], ms[:, :], EPS_RMS, None, ALU.add))
            m = inverse_root(rms[:, :], ms[:, :], m)
            yield
            dve.after(m)
            m = dve.mark(nc.vector.tensor_tensor(ms[:, :], rms[:, :], rstd[slot][:, :], ALU.mult))
            dve.after(m)
            hn.claim(dve)
            for t in range(TL):
                m = dve.mark(nc.vector.tensor_scalar(hn.tensor[:, t, :], xa[:, t, :], mv[slot][:, t, 0:1], ms[:, t:t + 1], ALU.subtract, ALU.mult))
            xa_read[0] = m
            yield
            pe.after(m)
            act.after(prev)
            marks = yield from transposed(hn.tensor, lambda kb: h[:, kb, 1:C + 1], lambda kb: cols["ln1_w"][:, kb:kb + 1])
            hn.readers = marks
            yield
            xx = bgT.tensor
            bgT.claim(dve)
            for kb in range(KB):
                dve.after(marks[kb])
                m = dve.mark(nc.vector.tensor_tensor(xx[:, kb, :], h[:, kb, 0:C], h[:, kb, 1:C + 1], ALU.subtract))
            yield
            dve.after(m)
            act.after(*scan_done[slot])
            for n, mu in enumerate(("mu_w", "mu_g", "mu_v", "mu_k", "mu_r")):
                buf = xm[n % 2]
                buf.claim(dve)
                for kb in range(KB):
                    m = dve.mark(nc.vector.scalar_tensor_tensor(out=buf.tensor[:, kb, :], in0=xx[:, kb, :], scalar=cols[mu][:, kb:kb + 1],
                                                                in1=h[:, kb, 1:C + 1], op0=ALU.mult, op1=ALU.add))
                if mu == "mu_r":
                    hT.readers = [m]
                    bgT.readers = [m]
                yield
                pe.after(m)
                if mu == "mu_w":
                    i, bank = G.take(pe)
                    m = pe.mark(matmuls(nc, bank[0:LORA, :], [(wA[:, kb, :], buf.tensor[:, kb, :]) for kb in range(KB)]))
                    buf.readers = [m]
                    yield
                    act.after(m, *hid_read.values())
                    m = act.mark(nc.scalar.activation(lora, bank[0:LORA, :], ACT.Tanh))
                    G.freed[i] = m
                    yield
                    pe.after(m)
                    for ob in range(KB):
                        i, bank = G.take(pe)
                        m = pe.mark(matmuls(nc, bank, [(wB[:, ob * P:(ob + 1) * P], lora)]))
                        hid_read[0] = m
                        yield
                        act.after(m)
                        m = act.mark(nc.scalar.activation(dT[:, ob, :], bank, ACT.Exp, bias=cols["w0"][:, ob:ob + 1]))
                        G.freed[i] = m
                        act.after(m)
                        done["d"] = act.mark(nc.scalar.activation(dT[:, ob, :], dT[:, ob, :], ACT.Exp, scale=-1.0))
                    continue
                if mu == "mu_g":
                    for half in range(2):
                        i, bank = G.take(pe)
                        for t in range(2):
                            at = (2 * half + t) * P
                            m = matmuls(nc, bank[:, t * D:(t + 1) * D], [(buf.tensor[:, kb, at:at + P], W["Wg"][:, kb, :]) for kb in range(KB)])
                        m = pe.mark(m)
                        buf.readers = [m]
                        yield
                        act.after(m, *post_done[slot])
                        part = flat(gate[slot][:, 2 * half:2 * half + 2, :])
                        m = act.mark(nc.scalar.activation(part, bank, ACT.Tanh, scale=0.5))
                        yield
                        dve.after(m)
                        done["g"] = dve.mark(nc.vector.scalar_tensor_tensor(out=part, in0=part, scalar=1.0, in1=bank, op0=ALU.add, op1=ALU.mult))
                        G.freed[i] = done["g"]
                    continue
                dst, w = {"mu_k": (kT, W["Wk"]), "mu_v": (vT, W["Wv"]), "mu_r": (rT, W["Wr"])}[mu]
                for ob in range(KB):
                    i, bank = G.take(pe)
                    m = pe.mark(matmuls(nc, bank, [(w[:, kb, ob * P:(ob + 1) * P], buf.tensor[:, kb, :]) for kb in range(KB)]))
                    buf.readers = [m]
                    yield
                    act.after(m)
                    done[mu[-1]] = act.mark(nc.scalar.copy(dst[:, ob, :], bank))
                    G.freed[i] = done[mu[-1]]
            ruk = xm[1]
            ruk.claim(dve)
            dve.after(done["r"], done["k"])
            for kb in range(KB):
                m = dve.mark(nc.vector.scalar_tensor_tensor(out=ruk.tensor[:, kb, :], in0=rT[:, kb, :], scalar=cols["u"][:, kb:kb + 1],
                                                            in1=kT[:, kb, :], op0=ALU.mult, op1=ALU.mult))
            yield
            pe.after(m)
            i, bank = G.take(pe)
            for t in range(TL):
                for kb in range(KB):
                    m = matmuls(nc, bank[:, (t * KB + kb) * HP:(t * KB + kb + 1) * HP], [(ruk.tensor[:, kb, t * P:(t + 1) * P], head_of[:, :])])
            m = pe.mark(m)
            ruk.readers = [m]
            yield
            act.after(m)
            m_bon = act.mark(nc.scalar.copy(bon[:, :], bank[:, 0:TL * H]))
            G.freed[i] = m_bon
            pe.after(done["v"])
            for half in range(2):
                i, bank = G.take(pe)
                for t in range(2):
                    for kb in range(KB):
                        at = (2 * half + t) * P
                        m = nc.tensor.transpose(bank[:, t * D + kb * P:t * D + (kb + 1) * P], vT[:, kb, at:at + P], ident[:, :])
                m = pe.mark(m)
                yield
                dve.after(m, m_bon)
                HH = TL * H // 2
                m = dve.mark(nc.vector.tensor_tensor(
                    flat(bonus[slot][:, 2 * half:2 * half + 2, :]).rearrange("p (h v) -> p h v", v=DK), bank.rearrange("p (h v) -> p h v", v=DK),
                    bon[:, half * HH:(half + 1) * HH].unsqueeze(2).broadcast_to([P, HH, DK]), ALU.mult))
                G.freed[i] = m
            done["b"] = m
            ready[slot] = done

        def two_layer(blocks, up_pairs, down):
            banks = [DN.take(pe) for _ in range(2)]
            m_hidden = {}
            for f in range(blocks + 1):
                if f < blocks:
                    i, bank = G.take(pe)
                    m = pe.mark(matmuls(nc, bank, up_pairs(f)))
                    yield
                    r = hid_turn[0] % NH
                    act.after(m, hid_read.get(r))
                    m_hidden[f] = (act.mark(nc.scalar.activation(hidden[:, r, :], bank, ACT.Gelu)), r)
                    hid_turn[0] += 1
                    G.freed[i] = m_hidden[f][0]
                q = f - 1
                if q >= 0:
                    mh, r = m_hidden[q]
                    pe.after(mh)
                    for t in range(TL):
                        m = nc.tensor.matmul(banks[t // 2][1][:, (t % 2) * D:(t % 2 + 1) * D], hidden[:, r, t * P:(t + 1) * P], down(q),
                                             start=(q == 0 and t % 2 == 0), stop=(q == blocks - 1 and t % 2 == 1), skip_group_check=True)
                    hid_read[r] = pe.mark(m)
                    yield
            return banks, hid_read[r]

        def add_sums(banks, m):
            dve.after(m)
            for half, (i, bank) in enumerate(banks):
                part = flat(xb[:, 2 * half:2 * half + 2, :])
                m = dve.mark(nc.vector.tensor_tensor(part, part, bank, ALU.add))
                DN.freed[i] = m
            return m

        def after_scan(c, slot):
            ot = o.tensor
            by_head = flat(ot[:, :, :]).rearrange("p (h v) -> p h v", v=DK)
            wide = lambda ap: ap.unsqueeze(2).broadcast_to([P, TL * H, DK])
            dve.after(o_ready[0])
            m = dve.mark(nc.vector.tensor_tensor(flat(ot[:, :, :]), flat(ot[:, :, :]), flat(bonus[slot][:, :, :]), ALU.add))
            dve.after(m)
            m = dve.mark(nc.vector.tensor_reduce(heads[:, :], by_head, AX, ALU.add))
            dve.after(m)
            m = dve.mark(nc.vector.tensor_scalar(heads[:, :], heads[:, :], 1.0 / DK, None, ALU.mult))
            dve.after(m)
            m = dve.mark(nc.vector.tensor_tensor(by_head, by_head, wide(heads[:, :]), ALU.subtract))
            yield
            hn.claim(act)
            act.after(m)
            m = act.mark(nc.scalar.activation(flat(hn.tensor[:, :, :]), flat(ot[:, :, :]), ACT.Square))
            yield
            dve.after(m)
            m = dve.mark(nc.vector.tensor_reduce(heads[:, :], flat(hn.tensor[:, :, :]).rearrange("p (h v) -> p h v", v=DK), AX, ALU.add))
            hn.readers = [m]
            yield
            nc.scalar.preload_act_table_set("natural_log_exp_and_others")
            act.after(m)
            m = act.mark(nc.scalar.activation(heads[:, :], heads[:, :], ACT.Ln, scale=1.0 / DK, bias=eps_gn[:, 0:1]))
            act.after(m)
            m = act.mark(nc.scalar.activation(heads[:, :], heads[:, :], ACT.Exp, scale=-0.5))
            yield
            dve.after(m)
            m = dve.mark(nc.vector.tensor_tensor(by_head, by_head, wide(heads[:, :]), ALU.mult))
            over_tiles = lambda row: row[:, :].unsqueeze(1).broadcast_to([P, TL, D])
            for operand, op in ((over_tiles(gn_w), ALU.mult), (over_tiles(gn_b), ALU.add), (gate[slot][:, :, :], ALU.mult)):
                pool.after(m)
                m = pool.mark(nc.gpsimd.tensor_tensor(ot[:, :, :], ot[:, :, :], operand, op))
                yield
            m_gated = m
            dve.engine.wait_ge(s_xb, c * 16 + 16)
            for t in range(TL):
                m_xn = dve.mark(nc.vector.tensor_scalar(x1[:, t, :], xb[:, t, :], mv[slot][:, t, 0:1], rstd[slot][:, t:t + 1], ALU.subtract, ALU.mult))
            yield
            pe.after(m_gated)
            bgT.claim(act)
            oT = bgT.tensor
            marks = yield from transposed(ot, lambda kb: oT[:, kb, :])
            o.readers = marks
            post_done[slot] = marks + [m_xn]
            pe.after(*marks)
            dve.after(m_xn)
            for half in range(2):
                i, bank = G.take(pe)
                for t in range(2):
                    at = (2 * half + t) * P
                    m = matmuls(nc, bank[:, t * D:(t + 1) * D], [(oT[:, kb, at:at + P], W["Wo"][:, kb, :]) for kb in range(KB)])
                m = pe.mark(m)
                bgT.readers = [m]
                yield
                dve.after(m)
                part = flat(x1[:, 2 * half:2 * half + 2, :])
                m_x1 = dve.mark(nc.vector.tensor_tensor(part, part, bank, ALU.add))
                G.freed[i] = m_x1
            yield
            hn.claim(act)
            act.after(m_x1)
            for t in range(TL):
                m = act.mark(nc.scalar.activation(hn.tensor[:, t, :], x1[:, t, :], ACT.Square, accum_out=ssq[:, t:t + 1]))
            hn.readers = [m]
            yield
            dve.after(m)
            m = dve.mark(nc.vector.tensor_scalar(ms[:, :], ssq[:, :], 1.0 / D, EPS_RMS, ALU.mult, ALU.add))
            m = inverse_root(rms[:, :], ms[:, :], m)
            m_res = dve.mark(nc.vector.tensor_tensor(flat(xb[:, :, :]), flat(xb[:, :, :]), flat(x1[:, :, :]), ALU.add))
            yield
            hn.claim(dve)
            dve.after(m)
            for t in range(TL):
                m = dve.mark(nc.vector.tensor_scalar(hn.tensor[:, t, :], x1[:, t, :], rms[:, t:t + 1], None, ALU.mult))
            yield
            pe.after(m)
            bgT.claim(act)
            h2T = bgT.tensor
            marks = yield from transposed(hn.tensor, lambda kb: h2T[:, kb, :], lambda kb: cols["ln2_w"][:, kb:kb + 1])
            hn.readers = marks
            pe.after(*marks)
            yield
            banks, m = yield from two_layer(FB, lambda f: [(w1[:, kb, f * P:(f + 1) * P], h2T[:, kb, :]) for kb in range(KB)], lambda f: w2[:, f, :])
            bgT.readers = [m]
            dve.after(m_res)
            m = add_sums(banks, m)
            yield
            dve.after(m)
            m = yield from variance(xb, R["mv"])
            m = inverse_root(R["rstd"][:, :], ve[:, :], m)
            yield
            dve.after(m)
            hn.claim(dve)
            for t in range(TL):
                m = dve.mark(nc.vector.tensor_scalar(hn.tensor[:, t, :], xb[:, t, :], R["mv"][:, t, 0:1], R["rstd"][:, t:t + 1], ALU.subtract, ALU.mult))
            yield
            pe.after(m)
            bgT.claim(act)
            xT = bgT.tensor
            marks = yield from transposed(hn.tensor, lambda kb: xT[:, kb, :])
            hn.readers = marks
            pe.after(*marks)
            yield
            m = yield from router(nc, L, G, xT, W_router, R, iota, 1, E, TOP)
            dve.after(m)
            m_gates = dve.mark(nc.vector.tensor_tensor(gates[:, :, :], R["chosen"][:, :, :], R["prob"][:, :, :], ALU.mult))
            yield
            up_of = lambda e: [(W_up[:, e, kb, :], xT[:, kb, :]) for kb in range(KB)]
            banks, m = yield from two_layer(SH, up_of, lambda e: W_down[:, e, :])
            m = add_sums(banks, m)
            m_acc = {t: m for t in range(TL)}
            dve.after(m_gates)
            m_hidden = {}
            for e in range(E + 1):
                if e < E:
                    i, bank = G.take(pe)
                    m = pe.mark(matmuls(nc, bank, up_of(SH + e)))
                    yield
                    r = hid_turn[0] % NH
                    act.after(m, hid_read.get(r))
                    m_hidden[e] = (act.mark(nc.scalar.activation(hidden[:, r, :], bank, ACT.Gelu)), r)
                    hid_turn[0] += 1
                    G.freed[i] = m_hidden[e][0]
                q = e - 1
                if q < 0:
                    continue
                mh, r = m_hidden[q]
                pe.after(mh)
                for half in range(2):
                    i, bank = DN.take(pe)
                    for t in (2 * half, 2 * half + 1):
                        m = nc.tensor.matmul(bank[:, (t % 2) * D:(t % 2 + 1) * D], hidden[:, r, t * P:(t + 1) * P], W_down[:, SH + q, :], start=True, stop=True)
                    hid_read[r] = pe.mark(m)
                    yield
                    dve.after(hid_read[r])
                    for t in (2 * half, 2 * half + 1):
                        dve.after(m_acc[t])
                        m_acc[t] = dve.mark(nc.vector.scalar_tensor_tensor(out=xb[:, t, :], in0=bank[:, (t % 2) * D:(t % 2 + 1) * D],
                                                                           scalar=gates[:, t, q:q + 1], in1=xb[:, t, :], op0=ALU.mult, op1=ALU.add))
                    DN.freed[i] = m_acc[2 * half + 1]
            bgT.readers = [hid_read[r]]
            sp.after(m_acc[TL - 1])
            nc.sync.dma_start(chunk_of(chunks_out, c), xb[:, :, :]).then_inc(s_store, 16)

        def scan(c, slot, bg, pieces):
            rT, kT, vT, dT = (rkvd[slot][:, i] for i in range(4))
            done = ready.get(slot, {})
            steps = KB * DK
            m_start = dve.mark(nc.vector.tensor_scalar(carry[:, :], carry[:, :], chunk_mask[:, bass.ds(c, 1)], None, ALU.mult))
            m_rep, m_kv, m_scan, m_prod, m_sum, m_kept, m_first = {}, {}, {}, {}, {}, {}, {}
            pool.after(done.get("k"))
            dve.after(done.get("d"), done.get("r"))
            act.after(m_start)
            pe.after(done.get("v"), *o_free)
            for s in range(steps + 3):
                if s < steps:
                    hb, v = divmod(s, DK)
                    i, bank = VR.take(pe)
                    m = pe.mark(matmuls(nc, bank, [(spread[:, v, :], vT[:, hb, :])]))
                    act.after(m, m_kv.get(s - NR))
                    m_rep[s] = act.mark(nc.scalar.copy(vrep[:, s % NR, :], bank))
                    VR.freed[i] = m_rep[s]
                    act.after(m_prod.get(s - NR), m_kept.get(s - NR))
                    m_first[s] = act.mark(nc.scalar.copy(S[:, s % NR, 0:1], carry[:, s:s + 1]))
                    pool.after(m_rep[s], m_scan.get(s - NR))
                    m_kv[s] = pool.mark(nc.gpsimd.tensor_tensor(kv[:, s % NR, :], kT[:, hb, :], vrep[:, s % NR, :], ALU.mult))
                q = s - 1
                if 0 <= q < steps:
                    hb, v = divmod(q, DK)
                    dve.after(m_kv[q], m_first[q], m_prod.get(q - NR))
                    m_scan[q] = dve.mark(nc.vector.tensor_tensor_scan(S[:, q % NR, 1:C + 1], dT[:, hb, :], kv[:, q % NR, :],
                                                                      S[:, q % NR, 0:1], ALU.mult, ALU.add))
                    act.after(m_scan[q])
                    m_kept[q] = act.mark(nc.scalar.copy(carry[:, q:q + 1], S[:, q % NR, C:C + 1]))
                    dve.after(m_scan[q], m_sum.get(q - NR))
                    m_prod[q] = dve.mark(nc.vector.tensor_tensor(prod[:, q % NR, :], rT[:, hb, :], S[:, q % NR, 0:C], ALU.mult))
                q = s - 2
                if 0 <= q < steps:
                    hb, v = divmod(q, DK)
                    pe.after(m_prod[q])
                    for t in range(TL):
                        at = (t % 2) * D + hb * P + v
                        m = nc.tensor.matmul(psum[:, OB + t // 2, at:at + (HP - 1) * DK + 1:DK], prod[:, q % NR, t * P:(t + 1) * P], head_of[:, :],
                                             start=True, stop=True)
                    m_sum[q] = pe.mark(m)
                bg.pull(pieces)
            scan_done[slot] = [m_kv[steps - 1], m_prod[steps - 1], m_rep[steps - 1]]
            bg.drain()
            o.claim(act)
            act.after(m_sum[steps - 1])
            o_free.clear()
            for half in range(2):
                o_free.append(act.mark(nc.scalar.copy(flat(o.tensor[:, 2 * half:2 * half + 2, :]), psum[:, OB + half, :])))
            o_ready[0] = o_free[-1]

        ready, o_ready = {}, [None]
        PIECES = 4

        def segment(c, slot, first=False, last=False):
            bg = []
            if not first:
                load_xb(c - 1)
                bg.append(after_scan(c - 1, 1 - slot))
            if not last:
                load_xa(c + 1, None)
                bg.append(before(c + 1, 1 - slot))
            scan(c, slot, Background(*bg), PIECES)

        last = NCH - 1
        assert NCH % 2 == 0
        L.begin(0)
        load_xa(0, None)
        Background(before(0, 0)).drain()
        segment(0, 0, first=True)
        L.finish()
        PER_BODY = CLEARS // (NCH // 2 - 1)
        with nc.Fori(1, NCH // 2) as i:
            L.begin(i)
            clear(i * PER_BODY - PER_BODY, PER_BODY)
            segment(i * 2 - 1, 1)
            segment(i * 2, 0)
            L.finish()
        L.begin(NCH // 2)
        segment(last, 1, last=True)
        load_xb(last)
        Background(after_scan(last, 1)).drain()
        L.finish()
        nc.sync.wait_ge(s_store, 16 * NCH + 16)
        nc.all_engine_barrier()


def layer1_phase(nc, psum, consts, I, route, x_in, x_out, normed):
    C, D, E, N, KC = 512, 256, 512, 16, 4
    KB, EB, TL, NCH = D // P, E // P, C // P, x_in.shape[0] // C
    Z = route.sizes
    NE, GR, TOP, EX = Z.ne, Z.GROUPS, Z.TOP, Z.EXPERTS
    AX = mybir.AxisListType.X
    with ExitStack() as st:
        sb = lambda name, shape: st.enter_context(nc.sbuf_tensor("c_" + name, shape, F32))
        sem = lambda name: st.enter_context(nc.semaphore("c_" + name))
        L = Lanes(nc, "c", st)
        pe, act, dve, pool, sp = L.pe, L.act, L.dve, L.pool, L.sp
        s_load, s_xa, s_xb, s_store, s_normed = sem("load"), sem("xa"), sem("xb"), sem("store"), sem("normed")
        W_in, W_dt, W_out = sb("W_in", [P, KB, 2 * E]), sb("W_dt", [P, EB, E]), sb("W_out", [P, EB, D])
        PARTS, QUAD = 3, 32
        BP = PARTS * QUAD
        W_B = sb("W_B", [P, EB, BP])
        W_router, iota = sb("W_router", [P, KB, NE]), sb("iota", [P, 32])
        spread = st.enter_context(nc.sbuf_tensor("c_spread", [BP, N, P], BF16))
        chunk_mask = sb("chunk_mask", [P, NCH + 1])
        col_pack = sb("cols", [P, EB, N + KC + 3])
        A = col_pack[:, :, 0:N]
        conv_w = col_pack[:, :, N:N + KC]
        b_conv, b_dt, skip = (col_pack[:, :, N + KC + i:N + KC + i + 1] for i in range(3))
        tri, ones = route.tri, route.ones
        ident, neghalf = consts["ident"], consts["neghalf"]

        xs, dt, dtx = ([sb(f"{n}{i}", [P, EB, C]) for i in range(2)] for n in ("xs", "dt", "dtx"))
        gate = [sb(f"gate{i}", [P, TL, E]) for i in range(2)]
        B = [st.enter_context(nc.sbuf_tensor(f"c_B{i}", [BP, C], BF16)) for i in range(2)]
        B_part, B_rest = st.enter_context(nc.sbuf_tensor("c_B_part", [BP, C], BF16)), sb("B_rest", [BP, C])
        NR = 4
        Brep = sb("Brep", [P, N, C])
        dbx, hs = sb("dbx", [P, NR, C]), sb("hs", [P, NR, C])
        carry = sb("carry", [P, EB, N])
        xa, xb, xn = sb("xa", [P, TL, D]), sb("xb", [P, TL, D]), sb("xn", [P, TL, D])
        hn, xT = Shared(sb("hn", [P, TL, D])), Shared(sb("xT", [P, KB, C]))
        yT = Shared(sb("yT", [P, EB, C]))
        pre = sb("pre", [P, EB, C + KC - 1])
        tmp = sb("tmp", [P, 2, C])
        stats, mv = sb("stats", [P, TL, 6]), sb("mv", [P, TL, 2])
        ve, rstd = sb("ve", [P, TL]), sb("rstd", [P, TL])
        at_pick = sb("at_pick", [P, TL * GR, TOP, EX])
        R = router_buffers(nc, st, "c", GR, EX, TOP)

        loaded = load(nc, s_load, [(W_in[:, :, :], I["c_W_in"]), (W_dt[:, :, :], I["c_W_dt"]), (W_out[:, :, :], I["c_W_out"]),
                                   (W_B[:, :, :], I["c_W_B"]), (Brep[0:BP, 0:N * P // C, :], I["state_spread"]), (chunk_mask[:, :], I["chunk_mask"]),
                                   (col_pack[:, :, :], I["c_cols"]), (W_router[:, :, :], I["d_router"]), (iota[:, :], I["iota"]),
                                   (tri[:, :], I["tri"])])
        nc.vector.memset(carry[:, :, :], 0.0)
        nc.vector.memset(pre[:, :, C:C + KC - 1], 0.0)
        nc.vector.memset(route.ahead[:, TL, :], 0.0)
        nc.vector.memset(ones[:, :], 1.0)
        nc.sync.wait_ge(s_load, loaded)
        nc.sync.sem_inc(s_store, 16)
        nc.sync.sem_inc(s_normed, 16)
        nc.all_engine_barrier()
        with nc.semaphore("c_setup") as s_setup:
            nc.scalar.copy(spread[:, :, :].rearrange("k n p -> k (n p)"), Brep[0:BP, 0:N * P // C, :].rearrange("k a c -> k (a c)"))
            nc.scalar.activation(A, A, ACT.Exp).then_inc(s_setup, 1)
            nc.vector.wait_ge(s_setup, 1)
            nc.vector.tensor_scalar(A, A, -1.0, None, ALU.mult)
            nc.vector.tensor_scalar(col_pack[:, :, N:N + KC + 1], col_pack[:, :, N:N + KC + 1], 0.5, None, ALU.mult)
            L.prime()
            nc.all_engine_barrier()

        chunks = lambda ap: ap.rearrange("(c t p) d -> p c t d", p=P, t=TL)
        chunks_in, chunks_out, chunks_normed = chunks(x_in), chunks(x_out), chunks(normed)
        chunk_of = lambda view, c: view[:, bass.ds(c, 1), :, :].rearrange("p a t d -> p (a t) d")
        flat = lambda ap: ap.rearrange("p a b -> p (a b)")
        G, BR, DA, YB = Banks(psum, 0, 2), Banks(psum, 2, 1), Banks(psum, 3, 3), 6
        ready, scan_done, y_read = {}, [[], []], [[], []]
        next_mask = sb("next_mask", [P, 2])
        pre_written, pre_read, tmp_read = [], [None] * EB, {}
        xa_read, y_free = [None], {}
        m_ahead = [None]

        def layer_norm(src, dst):
            for t in range(TL):
                m = dve.mark(nc.vector.bn_stats(stats[:, t, :], src[:, t, :]))
            dve.after_alone(m)
            for t in range(TL):
                m = dve.mark(nc.vector.bn_aggr(mv[:, t, :], stats[:, t, :]))
            yield
            dve.after(m)
            m = dve.mark(nc.vector.tensor_scalar(ve[:, :], mv[:, :, 1], EPS_LN, None, ALU.add))
            pool.after(m)
            m = pool.mark(nc.gpsimd.tensor_tensor(rstd[:, :], ve[:, :], neghalf[:, 0:TL], ALU.pow))
            yield
            dve.after(m)
            for t in range(TL):
                m = dve.mark(nc.vector.tensor_scalar(dst[:, t, :], src[:, t, :], mv[:, t, 0:1], rstd[:, t:t + 1], ALU.subtract, ALU.mult))
            yield
            return m

        def transposed(src, dst, blocks):
            marks = []
            for kb in range(blocks):
                i, bank = G.take(pe)
                for t in range(TL):
                    m = nc.tensor.transpose(bank[:, t * P:(t + 1) * P], src[:, t, kb * P:(kb + 1) * P], ident[:, :])
                m = pe.mark(m)
                yield
                act.after(m)
                m = act.mark(nc.scalar.copy(dst[:, kb, :], bank))
                G.freed[i] = m
                marks.append(m)
            return marks

        def load_xa(c):
            sp.after(xa_read[0])
            nc.sync.dma_start(xa[:, :, :], chunk_of(chunks_in, c)).then_inc(s_xa, 16)

        def load_xb(c):
            sp.engine.wait_ge(s_store, c * 16 + 16)
            nc.sync.dma_start(xb[:, :, :], chunk_of(chunks_in, c)).then_inc(s_xb, 16)

        def before(c, slot):
            xs_, dt_, dtx_, gate_ = xs[slot], dt[slot], dtx[slot], gate[slot]
            dve.after(*pre_written, *pre_read)
            m_pre = dve.mark(nc.vector.tensor_scalar(pre[:, :, 0:KC - 1], pre[:, :, C:C + KC - 1], chunk_mask[:, bass.ds(c, 1)], None, ALU.mult))
            pre_written.clear()
            dve.engine.wait_ge(s_xa, c * 16 + 16)
            hn.claim(dve)
            m = yield from layer_norm(xa, hn.tensor)
            xa_read[0] = m
            pe.after(m)
            xT.claim(act)
            marks = yield from transposed(hn.tensor, xT.tensor, KB)
            hn.readers = marks
            x_T = xT.tensor
            yield
            pe.after(*marks)
            dve.after(*scan_done[slot])
            act.after(m_pre, *scan_done[slot])
            m_xs, m_in = {}, {}
            for e in range(EB + 1):
                if e < EB:
                    i, bank = G.take(pe)
                    m = pe.mark(matmuls(nc, bank, [(W_in[:, kb, e * P:(e + 1) * P], x_T[:, kb, :]) for kb in range(KB)]))
                    yield
                    act.after(m, pre_read[e])
                    m_in[e] = act.mark(nc.scalar.copy(pre[:, e, KC - 1:KC - 1 + C], bank))
                    G.freed[i] = m_in[e]
                    pre_written.append(m_in[e])
                q = e - 1
                if q < 0:
                    continue
                dve.after(m_in[q], m_pre)
                m = dve.mark(nc.vector.tensor_scalar(dtx_[:, q, :], pre[:, q, KC - 1:KC - 1 + C], conv_w[:, q, KC - 1:KC], b_conv[:, q, :], ALU.mult, ALU.add))
                yield
                for j in range(KC - 1):
                    dve.after(m)
                    m = dve.mark(nc.vector.scalar_tensor_tensor(out=dtx_[:, q, :], in0=pre[:, q, j:j + C], scalar=conv_w[:, q, j:j + 1],
                                                                in1=dtx_[:, q, :], op0=ALU.mult, op1=ALU.add))
                    yield
                pre_read[q] = m
                act.after(m, tmp_read.get(q % 2))
                m = act.mark(nc.scalar.activation(tmp[:, q % 2, :], dtx_[:, q, :], ACT.Tanh))
                yield
                dve.after(m)
                m_xs[q] = dve.mark(nc.vector.scalar_tensor_tensor(out=xs_[:, q, :], in0=tmp[:, q % 2, :], scalar=1.0, in1=dtx_[:, q, :],
                                                                  op0=ALU.add, op1=ALU.mult))
                tmp_read[q % 2] = m_xs[q]
            act.after(*y_read[slot])
            for t in range(TL):
                i, bank = G.take(pe)
                m = pe.mark(matmuls(nc, bank, [(x_T[:, kb, t * P:(t + 1) * P], W_in[:, kb, E:2 * E]) for kb in range(KB)]))
                yield
                act.after(m)
                m = act.mark(nc.scalar.activation(gate_[:, t, :], bank, ACT.Tanh, scale=0.5))
                yield
                dve.after(m)
                m_gate = dve.mark(nc.vector.scalar_tensor_tensor(out=gate_[:, t, :], in0=gate_[:, t, :], scalar=1.0, in1=bank,
                                                                 op0=ALU.add, op1=ALU.mult))
                G.freed[i] = m_gate
            xT.readers = [m_gate]
            pe.after(m_xs[EB - 1])
            i, bank = G.take(pe)
            m = pe.mark(matmuls(nc, bank[0:BP, :], [(W_B[:, e, :], xs_[:, e, :]) for e in range(EB)]))
            yield
            act.after(m)
            m = act.mark(nc.scalar.copy(B[slot][:, :], bank[0:BP, :]))
            yield
            dve.after(m)
            m = dve.mark(nc.vector.tensor_tensor(B_rest[:, :], bank[0:BP, :], B[slot][:, :], ALU.subtract))
            G.freed[i] = m
            yield
            act.after(m)
            m = act.mark(nc.scalar.copy(B_part[:, :], B_rest[:, :]))
            yield
            dve.after(m)
            m_rest = dve.mark(nc.vector.tensor_tensor(B_rest[:, :], B_rest[:, :], B_part[:, :], ALU.subtract))
            act.after(m)
            act.mark(nc.scalar.copy(B[slot][QUAD:2 * QUAD, :], B_part[QUAD:2 * QUAD, :]))
            yield
            act.after(m_rest)
            m_B = act.mark(nc.scalar.copy(B[slot][2 * QUAD:BP, :], B_rest[2 * QUAD:BP, :]))
            yield
            nc.scalar.preload_act_table_set("natural_log_exp_and_others")
            m_l, m_dtx, m_skip = {}, {}, {}
            for e in range(EB):
                i, bank = G.take(pe)
                for k in range(EB):
                    m = nc.tensor.matmul(bank, W_dt[:, k, e * P:(e + 1) * P], xs_[:, k, :], start=(k == 0), stop=(k == EB - 1))
                    if k % 2:
                        m = pe.mark(m)
                        yield
                act.after(m, tmp_read.get(e % 2))
                m_z = act.mark(nc.scalar.activation(dt_[:, e, :], bank, ACT.Identity, bias=b_dt[:, e, :]))
                G.freed[i] = m_z
                act.after(m_z)
                m = act.mark(nc.scalar.activation(tmp[:, e % 2, :], dt_[:, e, :], ACT.Abs))
                yield
                act.after(m)
                m = act.mark(nc.scalar.activation(tmp[:, e % 2, :], tmp[:, e % 2, :], ACT.Exp, scale=-1.0))
                yield
                act.after(m)
                m = act.mark(nc.scalar.activation(tmp[:, e % 2, :], tmp[:, e % 2, :], ACT.Ln, bias=1.0))
                yield
                dve.after(m)
                m_l[e] = dve.mark(nc.vector.scalar_tensor_tensor(out=dt_[:, e, :], in0=dt_[:, e, :], scalar=0.0, in1=tmp[:, e % 2, :],
                                                                 op0=ALU.max, op1=ALU.add))
                tmp_read[e % 2] = m_l[e]
                yield
                dve.after(m_l[e])
                m_dtx[e] = dve.mark(nc.vector.tensor_tensor(dtx_[:, e, :], dt_[:, e, :], xs_[:, e, :], ALU.mult))
                yield
            for e in range(EB):
                dve.after(m_dtx[e])
                m_skip[e] = dve.mark(nc.vector.tensor_scalar(xs_[:, e, :], xs_[:, e, :], skip[:, e, :], None, ALU.mult))
                yield
            ready[slot] = {"B": m_B, "dt": m_l, "dtx": m_dtx, "skip": m_skip, "gate": m_gate}

        def after_scan(c, slot):
            y_T = yT.tensor
            yT.claim(act)
            pe.after(*ready.get(("y", slot), []))
            marks = yield from transposed(gate[slot], y_T, EB)
            y_read[slot] = marks
            yield
            pe.after(*marks)
            dve.engine.wait_ge(s_xb, c * 16 + 16)
            for half in range(2):
                i, bank = G.take(pe)
                for t in range(2):
                    at = (2 * half + t) * P
                    m = matmuls(nc, bank[:, t * D:(t + 1) * D], [(y_T[:, e, at:at + P], W_out[:, e, :]) for e in range(EB)])
                m = pe.mark(m)
                yield
                dve.after(m)
                part = flat(xb[:, 2 * half:2 * half + 2, :])
                m = dve.mark(nc.vector.tensor_tensor(part, part, bank, ALU.add))
                G.freed[i] = m
            yield
            sp.after(m)
            nc.sync.dma_start(chunk_of(chunks_out, c), xb[:, :, :]).then_inc(s_store, 16)
            dve.after(m)
            dve.engine.wait_ge(s_normed, c * 16 + 16)
            m = yield from layer_norm(xb, xn)
            sp.after(m)
            nc.sync.dma_start(chunk_of(chunks_normed, c), xn[:, :, :]).then_inc(s_normed, 16)
            pe.after(m)
            marks = yield from transposed(xn, y_T, KB)
            yield
            pe.after(*marks)
            m = yield from router(nc, L, G, y_T, W_router, R, iota, GR, EX, TOP)
            chosen = R["chosen"][:, :, :].rearrange("p (t g) e -> p t (g e)", t=TL)
            part = bass.ds(c * TL, TL)
            dve.mark(nc.vector.tensor_copy(route.picks[:, part, :].rearrange("p t k -> p (t k)"), flat(R["index_f"][:, :, :])))
            dve.mark(nc.vector.tensor_scalar(route.weights[:, part, :].rearrange("p t (g k) -> p (t g) k", g=GR), R["best"][:, :, 0:TOP], 0.5, None, ALU.mult))
            ahead = route.ahead
            dve.after(m, m_ahead[0])
            m = dve.mark(nc.vector.tensor_copy(ahead[:, 0, :], ahead[:, TL, :]))
            for t in range(TL):
                dve.after(m)
                m = dve.mark(nc.vector.tensor_tensor(ahead[:, t + 1, :], ahead[:, t, :], chosen[:, t, :], ALU.add))
            m_ahead[0] = m
            yield
            pe.after(m)
            i, bank = G.take(pe)
            ranks = bank[:, 0:TL * NE]
            m_rank = pe.mark(matmuls(nc, ranks, [(tri[:, :], R["chosen"][:, :, :].rearrange("p r e -> p (r e)")),
                                                 (ones[:, :], ahead[:, 0:TL, :].rearrange("p t e -> p (t e)"))]))
            yT.readers = [m_rank]
            yield
            dve.after(m_rank)
            m = dve.mark(nc.vector.tensor_tensor(
                at_pick[:, :, :, :], R["onehot"][:, :, :, :],
                ranks.rearrange("p (r e) -> p r e", e=EX).unsqueeze(2).broadcast_to([P, TL * GR, TOP, EX]), ALU.mult))
            G.freed[i] = m
            yield
            dve.after(m)
            dve.mark(nc.vector.tensor_reduce(route.ranks[:, part, :].rearrange("p t k -> p (t k)"), at_pick[:, :, :, :].rearrange("p r s e -> p (r s) e"), AX, ALU.add))

        steps = EB * N
        assert steps % NR == 0
        m_rep, m_da, m_dbx, m_scan, m_sum, m_kept, m_y, bank_of = ({} for _ in range(8))
        PIECES, AHEAD, SETTLE = 1.5, 2, 6

        def scans(chunks):
            done_of, count = {}, len(chunks)
            for g in range(count * steps + AHEAD + SETTLE):
                j = min(g // steps, count - 1)
                s = g - j * steps
                if s == 0:
                    if j > 0:
                        background.drain()
                    c, slot, stages = chunks[j]
                    done_of[j] = ready.get(slot, {"B": None, "dt": {}, "dtx": {}, "skip": {}, "gate": None})
                    pe.after(done_of[j]["B"])
                    act.after(m_kept.get(g - 1 - steps))
                    m_mask = act.mark(nc.scalar.copy(next_mask[:, slot:slot + 1], chunk_mask[:, bass.ds(c + 1, 1)]))
                    act.after(m_mask)
                if s == SETTLE:
                    background = Background(*stages())
                if g < count * steps:
                    (e, n), slot, done = divmod(s, N), chunks[j][1], done_of[j]
                    if e == 0:
                        i, bank = BR.take(pe)
                        m = pe.mark(matmuls(nc, bank, [(spread[:, n, :], B[slot][:, :])]))
                        act.after(m, m_dbx.get(g - N))
                        m_rep[n] = act.mark(nc.scalar.copy(Brep[:, n, :], bank))
                        BR.freed[i] = m_rep[n]
                    pool.after(m_rep[n], done["dtx"].get(e), m_scan.get(g - NR))
                    m_dbx[g] = pool.mark(nc.gpsimd.tensor_tensor(dbx[:, g % NR, :], dtx[slot][:, e, :], Brep[:, n, :], ALU.mult))
                    act.after(done["dt"].get(e))
                    bank_of[g] = DA.take(act)
                    m_da[g] = act.mark(nc.scalar.activation(bank_of[g][1], dt[slot][:, e, :], ACT.Exp, scale=A[:, e, n:n + 1]))
                q = g - AHEAD
                if 0 <= q < count * steps:
                    e, n = divmod(q % steps, N)
                    dve.after(m_da[q], m_dbx[q], m_sum.get(q - NR), m_kept.get(q - NR), m_kept.get(q - steps))
                    m_scan[q] = dve.mark(nc.vector.tensor_tensor_scan(hs[:, q % NR, :], bank_of[q][1], dbx[:, q % NR, :], carry[:, e, n:n + 1],
                                                                      ALU.mult, ALU.add))
                    DA.freed[bank_of[q][0]] = m_scan[q]
                q = g - AHEAD - 1
                if 0 <= q < count * steps:
                    (e, n), slot, done = divmod(q % steps, N), chunks[q // steps][1], done_of[q // steps]
                    act.after(m_scan[q])
                    m_kept[q] = act.mark(nc.scalar.activation(carry[:, e, n:n + 1], hs[:, q % NR, C - 1:C], ACT.Copy, scale=next_mask[:, slot:slot + 1]))
                    pe.after(m_scan[q])
                    if n == 0:
                        pe.after(y_free.get(e % 2), done["skip"].get(e))
                        for t in range(TL):
                            nc.tensor.matmul(psum[:, YB + e % 2, t * P:(t + 1) * P], xs[slot][:, e, t * P:(t + 1) * P], ident[:, :],
                                             is_transpose=True, start=(t == 0), stop=False, skip_group_check=True)
                    for t in range(TL):
                        last = nc.tensor.matmul(psum[:, YB + e % 2, t * P:(t + 1) * P], hs[:, q % NR, t * P:(t + 1) * P], ident[:, :],
                                                is_transpose=True, start=False, stop=(n == N - 1 and t == TL - 1), skip_group_check=True)
                    m_sum[q] = pe.mark(last)
                q = g - AHEAD - 3
                if 0 <= q < count * steps and q % N == N - 1:
                    e, slot, done = q % steps // N, chunks[q // steps][1], done_of[q // steps]
                    dve.after(m_sum[q], done["gate"])
                    m_y[e] = dve.mark(nc.vector.scalar_tensor_tensor(
                        out=gate[slot][:, :, e * P:(e + 1) * P], in0=psum[:, YB + e % 2, :].rearrange("p (t d) -> p t d", t=TL), scalar=0.5,
                        in1=gate[slot][:, :, e * P:(e + 1) * P], op0=ALU.mult, op1=ALU.mult))
                    y_free[e % 2] = m_y[e]
                    if e == EB - 1:
                        scan_done[slot] = [m_dbx[q], m_da[q], m_sum[q]]
                        ready[("y", slot)] = [m_y[e]]
                if g < count * steps and s >= SETTLE:
                    background.pull(PIECES)
            background.drain()
            for marks in (m_rep, m_da, m_dbx, m_scan, m_sum, m_kept, m_y, y_free):
                marks.clear()

        def stages(c, slot, first=False, last=False):
            def make():
                if not first:
                    load_xb(c - 1)
                    yield after_scan(c - 1, 1 - slot)
                if not last:
                    load_xa(c + 1)
                    yield before(c + 1, 1 - slot)
            return make

        last = NCH - 1
        assert NCH % 2 == 0
        L.begin(0)
        load_xa(0)
        Background(before(0, 0)).drain()
        scans([(0, 0, stages(0, 0, first=True))])
        L.finish()
        with nc.Fori(1, NCH // 2) as i:
            L.begin(i)
            scans([(i * 2 - 1, 1, stages(i * 2 - 1, 1)), (i * 2, 0, stages(i * 2, 0))])
            L.finish()
        L.begin(NCH // 2)
        scans([(last, 1, stages(last, 1, last=True))])
        load_xb(last)
        Background(after_scan(last, 1)).drain()
        L.finish()
        nc.sync.wait_ge(s_store, 16 * NCH + 16)
        nc.sync.wait_ge(s_normed, 16 * NCH + 16)
        nc.all_engine_barrier()


def router(nc, L, G, xT, W_router, R, iota, groups, experts, top):
    TL, KB = 4, 2
    NE = groups * experts
    pe, act, dve = L.pe, L.act, L.dve
    rows = TL * groups
    i, bank = G.take(pe)
    for t in range(TL):
        m = matmuls(nc, bank[:, t * NE:(t + 1) * NE], [(xT[:, kb, t * P:(t + 1) * P], W_router[:, kb, :]) for kb in range(KB)])
    m = pe.mark(m)
    yield
    logits = bank[:, 0:TL * NE].rearrange("p (r e) -> p r e", r=rows)
    dve.after(m)
    m = dve.mark(nc.vector.tensor_reduce(R["peak"][:, :], logits, mybir.AxisListType.X, ALU.max))
    dve.after(m)
    m = dve.mark(nc.vector.tensor_tensor(R["prob"][:, :, :], logits, R["peak"][:, :].unsqueeze(2).broadcast_to([P, rows, experts]), ALU.subtract))
    G.freed[i] = m
    yield
    act.after(m)
    m = act.mark(nc.scalar.activation(R["prob"][:, :, :], R["prob"][:, :, :], ACT.Exp))
    yield
    dve.after(m)
    m = dve.mark(nc.vector.tensor_reduce(R["total"][:, :], R["prob"][:, :, :], mybir.AxisListType.X, ALU.add))
    dve.after(m)
    m = dve.mark(nc.vector.reciprocal(R["total"][:, :], R["total"][:, :]))
    dve.after(m)
    m = dve.mark(nc.vector.tensor_tensor(R["prob"][:, :, :], R["prob"][:, :, :], R["total"][:, :].unsqueeze(2).broadcast_to([P, rows, experts]), ALU.mult))
    yield
    dve.after_alone(m)
    for r in range(rows):
        m = dve.mark(nc.vector.max(R["best"][:, r, :], R["prob"][:, r, :]))
        if r == rows // 2 - 1:
            yield
    yield
    dve.after_alone(m)
    for r in range(rows):
        m = dve.mark(nc.vector.max_index(R["index"][:, r, :], R["best"][:, r, :], R["prob"][:, r, :]))
        if r == rows // 2 - 1:
            yield
    yield
    dve.after(m)
    m = dve.mark(nc.vector.tensor_copy(R["index_f"][:, :, :], R["index"][:, :, 0:top]))
    dve.after(m)
    m = dve.mark(nc.vector.tensor_tensor(R["onehot"][:, :, :, :], iota[:, 0:experts].unsqueeze(1).unsqueeze(1).broadcast_to([P, rows, top, experts]),
                                         R["index_f"][:, :, :].unsqueeze(3).broadcast_to([P, rows, top, experts]), ALU.is_equal))
    dve.after(m)
    yield
    return dve.mark(nc.vector.tensor_reduce(R["chosen"][:, :, :], R["onehot"][:, :, :, :].rearrange("p r s e -> p r e s"), mybir.AxisListType.X, ALU.add))


def router_buffers(nc, st, name, groups, experts, top):
    rows = 4 * groups
    shapes = {"peak": [P, rows], "total": [P, rows], "prob": [P, rows, experts], "best": [P, rows, 8], "index_f": [P, rows, top],
              "onehot": [P, rows, top, experts], "chosen": [P, rows, experts]}
    R = {n: st.enter_context(nc.sbuf_tensor(f"{name}_{n}", s, F32)) for n, s in shapes.items()}
    R["mv"] = st.enter_context(nc.sbuf_tensor(f"{name}_router_mv", [P, 4, 2], F32))
    R["rstd"] = st.enter_context(nc.sbuf_tensor(f"{name}_router_rstd", [P, 4], F32))
    R["index"] = st.enter_context(nc.sbuf_tensor(f"{name}_index", [P, rows, 8], mybir.dt.uint32))
    return R


class SortedExperts:
    GROUPS, EXPERTS, TOP, SLOTS, UNROLL, RING = 2, 32, 2, 256, 8, 4

    def __init__(self, tokens):
        self.picks = self.GROUPS * self.TOP
        self.ne = self.GROUPS * self.EXPERTS
        self.tiles = tokens * self.picks // self.SLOTS + self.ne
        assert self.tiles % self.UNROLL == 0 and self.tiles + self.RING <= 2 * P and self.UNROLL % self.RING == 0
        self.rows = (self.tiles + self.RING) * self.SLOTS


CLEARS = 28


def clear_sorted_rows(nc, zeros, sorted_x, sem, first, count):
    view = sorted_x.rearrange("(a n p) d -> a p n d", p=P, a=CLEARS)
    for a in range(count):
        nc.sync.dma_start(view[bass.ds(first + a, 1), :, :, :].rearrange("a p n d -> p (a n) d"),
                          zeros[:, :].unsqueeze(1).broadcast_to([P, view.shape[2], view.shape[3]])).then_inc(sem, 16)


class Route:

    def __init__(self, nc, st, tokens):
        self.sizes = SortedExperts(tokens)
        sb = lambda name, shape: st.enter_context(nc.sbuf_tensor("route_" + name, shape, F32))
        self.picks, self.weights, self.ranks, self.rows = (sb(n, [P, tokens // P, self.sizes.picks]) for n in ("picks", "weights", "ranks", "rows"))
        self.ahead = sb("ahead", [P, 5, self.sizes.ne])
        self.tri, self.ones = sb("tri", [P, P]), sb("ones", [P, P])


def sorted_experts_phase(nc, psum, consts, I, route, x_in, normed, out, sorted_x, sorted_y, expert_list):
    Z = route.sizes
    C, D = 512, 256
    KB, TL, TT = D // P, C // P, x_in.shape[0] // P
    NCH, PK, NE, E, TOP, GR, SL = TT // TL, Z.picks, Z.ne, Z.EXPERTS, Z.TOP, Z.GROUPS, Z.SLOTS
    U32, I32, AX = mybir.dt.uint32, mybir.dt.int32, mybir.AxisListType.X
    flat = lambda ap: ap.rearrange("p a b -> p (a b)")
    chunk_of = lambda ap, c: ap.rearrange("(c t p) d -> p c t d", p=P, t=TL)[:, bass.ds(c, 1), :, :].rearrange("p a t d -> p (a t) d")
    picks, weights, ranks, rows, ones = route.picks, route.weights, route.ranks, route.rows, route.ones
    before = route.ahead[:, TL, :]
    with ExitStack() as st:
        sb = lambda name, shape, dt=F32: st.enter_context(nc.sbuf_tensor("d_" + name, shape, dt))
        s_load = st.enter_context(nc.semaphore("d_load"))
        iota, tile_no = sb("iota", [P, 32]), sb("tile_no", [P, 2])
        base, ends, in_tiles, work = (sb(n, [P, NE]) for n in ("base", "ends", "in_tiles", "work"))
        whole = sb("whole", [P, NE], I32)
        e_col, e_int = sb("e_col", [P, 2]), sb("e_int", [P, 2], I32)
        e_row = sb("e_row", [1, 2 * P], I32)
        loaded = load(nc, s_load, [(iota[:, :], I["iota"]), (tile_no[:, :], I["tile_no"])])
        nc.sync.wait_ge(s_load, loaded)
        nc.all_engine_barrier()

        with nc.semaphore("d_place") as s_place, nc.semaphore("d_list") as s_list:
            steps = [0]

            def then(instruction):
                steps[0] += 1
                instruction.then_inc(s_place, 1)
                nc.vector.wait_ge(s_place, steps[0])
            counts = psum[:, 0, 0:NE]
            then(nc.tensor.matmul(counts, ones[:, :], before, start=True, stop=True))
            then(nc.vector.tensor_scalar(work[:, :], counts, float(SL - 1), None, ALU.add))
            then(nc.vector.tensor_copy(whole[:, :], work[:, :]))
            then(nc.vector.tensor_scalar(whole[:, :], whole[:, :], SL.bit_length() - 1, None, ALU.arith_shift_right))
            then(nc.vector.tensor_copy(in_tiles[:, :], whole[:, :]))
            then(nc.vector.tensor_tensor_scan(ends[:, :], ones[:, 0:NE], in_tiles[:, :], 0.0, ALU.mult, ALU.add))
            then(nc.vector.tensor_tensor(base[:, :], ends[:, :], in_tiles[:, :], ALU.subtract))
            then(nc.vector.tensor_scalar(base[:, :], base[:, :], float(SL), None, ALU.mult))
            for j in range(2):
                then(nc.vector.tensor_scalar(work[:, :], ends[:, :], tile_no[:, j:j + 1], None, ALU.is_le))
                then(nc.vector.tensor_reduce(e_col[:, j:j + 1], work[:, :], AX, ALU.add))
            then(nc.vector.tensor_scalar(e_col[:, :], e_col[:, :], float(NE - 1), None, ALU.min))
            then(nc.vector.tensor_copy(e_int[:, :], e_col[:, :]))
            nc.sync.wait_ge(s_place, steps[0])
            with nc.allow_non_contiguous_dma(reason="256 expert numbers, once"):
                for j in range(2):
                    nc.sync.dma_start(expert_list[j * P:(j + 1) * P].rearrange("(p a) -> p a", a=1), e_int[:, j:j + 1]).then_inc(s_list, 16)
            nc.sync.wait_ge(s_list, 32)
            nc.sync.dma_start(e_row[:, :], expert_list.rearrange("(a n) -> a n", a=1)).then_inc(s_list, 16)
            nc.sync.wait_ge(s_list, 48)
            nc.all_engine_barrier()

        with ExitStack() as s2:
            sb2 = lambda name, shape, dt=F32: s2.enter_context(nc.sbuf_tensor("d2_" + name, shape, dt))
            L = Lanes(nc, "d2", s2)
            onehot, start = sb2("onehot", [P, TL * GR, TOP, E]), sb2("start", [P, TL * PK])
            hn = [sb2(f"hn{i}", [P, TL, D]) for i in range(2)]
            to_row = [sb2(f"to_row{i}", [P, TL * PK], U32) for i in range(2)]
            s_hn, s_sent = ([s2.enter_context(nc.semaphore(f"d2_{n}{i}")) for i in range(2)] for n in ("hn", "sent"))
            L.prime()
            per_chunk = 16 * TL * PK

            def fetch_hn(slot, c):
                nc.sync.dma_start(hn[slot][:, :, :], chunk_of(normed, c)).then_inc(s_hn[slot], 16)

            def rows_of(c, slot):
                dve = L.dve
                part = bass.ds(c * TL, TL)
                by_group = lambda ap: ap[:, part, :].rearrange("p t (g k) -> p (t g) k", g=GR)
                base_of = base[:, :].rearrange("p (g e) -> p g e", g=GR).unsqueeze(2).broadcast_to([P, GR, TOP, E])
                m = dve.mark(nc.vector.tensor_tensor(
                    onehot[:, :, :, :], iota[:, 0:E].unsqueeze(1).unsqueeze(1).broadcast_to([P, TL * GR, TOP, E]),
                    by_group(picks).unsqueeze(3).broadcast_to([P, TL * GR, TOP, E]), ALU.is_equal))
                dve.after(m)
                for t in range(TL):
                    mine = onehot[:, t * GR:(t + 1) * GR, :, :]
                    m = dve.mark(nc.vector.tensor_tensor(mine, mine, base_of, ALU.mult))
                dve.after(m)
                m = dve.mark(nc.vector.tensor_reduce(start[:, :], onehot[:, :, :, :].rearrange("p r s e -> p (r s) e"), AX, ALU.add))
                dve.after(m)
                m = dve.mark(nc.vector.tensor_tensor(start[:, :], start[:, :], ranks[:, part, :].rearrange("p t k -> p (t k)"), ALU.add))
                dve.after(m)
                dve.mark(nc.vector.tensor_copy(rows[:, part, :].rearrange("p t k -> p (t k)"), start[:, :]))
                m = dve.mark(nc.vector.tensor_copy(to_row[slot][:, :], start[:, :]))
                dve.after(m)
                return m

            def scatter(c, slot, turn, m_rows):
                L.pool.after(m_rows)
                L.pool.engine.wait_ge(s_hn[slot], turn * 16)
                nc.gpsimd.sem_inc(L.pool.pause, 1)
                for t in range(TL):
                    for k in range(PK):
                        nc.gpsimd.indirect_dma_start(out=sorted_x, out_offset=bass.IndirectOffsetOnAxis(ap=to_row[slot][:, t * PK + k:t * PK + k + 1], axis=0),
                                                     in_=hn[slot][:, t, :], in_offset=None, bounds_check=Z.rows - 1).then_inc(s_sent[slot], 16)

            fetch_hn(0, 0)
            nc.all_engine_barrier()
            L.begin(0)
            m_rows = rows_of(0, 0)
            fetch_hn(1, 1)
            scatter(0, 0, 1, m_rows)
            L.finish()
            with nc.Fori(1, NCH // 2) as i:
                L.begin(i)
                for c, slot, turn in ((i * 2 - 1, 1, i), (i * 2, 0, i + 1)):
                    if slot == 0:
                        nc.vector.wait_ge(s_sent[0], i * per_chunk)
                    m_rows = rows_of(c, slot)
                    scatter(c, slot, turn, m_rows)
                    nc.sync.wait_ge(s_sent[1 - slot], i * per_chunk)
                    nc.sync.sem_inc(L.sp.pause, 1)
                    fetch_hn(1 - slot, c + 1)
                    if slot == 1:
                        continue
                nc.vector.wait_ge(s_sent[1], i * per_chunk)
                L.finish()
            L.begin(NCH // 2)
            m_rows = rows_of(NCH - 1, 1)
            scatter(NCH - 1, 1, NCH // 2, m_rows)
            for slot in range(2):
                nc.gpsimd.wait_ge(s_sent[slot], NCH // 2 * per_chunk)
            L.finish()
            nc.all_engine_barrier()

        with ExitStack() as s3:
            sb3 = lambda name, shape: s3.enter_context(nc.sbuf_tensor("d3_" + name, shape, F32))
            L = Lanes(nc, "d3", s3)
            RN, UN, HB = Z.RING, Z.UNROLL, SL // P
            xs, w, ys = sb3("xs", [P, RN, HB, D]), sb3("w", [P, RN, 2 * KB * P + D]), sb3("ys", [P, RN, HB, D])
            xT, hg = sb3("xT", [P, 3, KB, SL]), sb3("hg", [P, 3, SL])
            s_x, s_w, s_y = ([s3.enter_context(nc.semaphore(f"d3_{n}{i}")) for i in range(RN)] for n in "xwy")
            rows_in = sorted_x.rearrange("(j h p) d -> j p h d", p=P, h=HB)
            rows_out = sorted_y.rearrange("(j h p) d -> j p h d", p=P, h=HB)
            weights_in = I["d_experts"]

            def fetch(j, slot):
                e = nc.sync.value_load(e_row[0:1, bass.ds(j, 1)], min_val=0, max_val=NE - 1)
                nc.sync.dma_start(w[:, slot, :], weights_in[bass.ds(e, 1), :, :].rearrange("a p n -> p (a n)")).then_inc(s_w[slot], 16)
                nc.sync.dma_start(xs[:, slot, :, :], rows_in[bass.ds(j, 1), :, :, :].rearrange("a p h d -> p (a h) d")).then_inc(s_x[slot], 16)
            L.prime()
            for slot in range(RN):
                fetch(slot, slot)
                nc.sync.sem_inc(s_y[slot], 16)
            nc.all_engine_barrier()
            TB, GU, DN = Banks(psum, 0, 2), Banks(psum, 2, 3), Banks(psum, 5, 3)
            pe, act, dve, pool, sp = L.pe, L.act, L.dve, L.pool, L.sp
            w_gate = lambda slot, kb: w[:, slot, kb * P:(kb + 1) * P]
            w_up = lambda slot, kb: w[:, slot, (KB + kb) * P:(KB + kb + 1) * P]
            w_down = lambda slot: w[:, slot, 2 * KB * P:]
            with nc.Fori(0, Z.tiles // UN) as i:
                L.begin(i)
                for b in (TB, GU, DN):
                    b.begin()
                m_xT, m_gu, m_h, m_dn = {}, {}, {}, {}
                uses = UN // RN
                for s in range(UN + 2):
                    if s < UN:
                        slot, use = s % RN, s // RN
                        pe.engine.wait_ge(s_x[slot], i * (16 * uses) + 16 * (use + 1))
                        b, bank = TB.take(pe)
                        for kb in range(KB):
                            for h in range(HB):
                                m = nc.tensor.transpose(bank[:, kb * SL + h * P:kb * SL + (h + 1) * P], xs[:, slot, h, kb * P:(kb + 1) * P], consts["ident"][:, :])
                        m = pe.mark(m)
                        act.after(m, m_gu.get(s - 3))
                        m_xT[s] = act.mark(nc.scalar.copy(xT[:, s % 3, :, :].rearrange("p k c -> p (k c)"), bank))
                        TB.freed[b] = m_xT[s]
                    q = s - 1
                    if 0 <= q < UN:
                        slot, use = q % RN, q // RN
                        pe.engine.wait_ge(s_w[slot], i * (16 * uses) + 16 * (use + 1))
                        b, bank = GU.take(pe)
                        pe.after(m_xT[q])
                        for half, wt in enumerate((w_gate, w_up)):
                            m = matmuls(nc, bank[:, half * SL:(half + 1) * SL], [(wt(slot, kb), xT[:, q % 3, kb, :]) for kb in range(KB)])
                        m_gu[q] = pe.mark(m)
                        act.after(m_gu[q], m_dn.get(q - 3))
                        m = act.mark(nc.scalar.activation(hg[:, q % 3, :], bank[:, 0:SL], ACT.Silu))
                        dve.after(m)
                        m_h[q] = dve.mark(nc.vector.tensor_tensor(hg[:, q % 3, :], hg[:, q % 3, :], bank[:, SL:2 * SL], ALU.mult))
                        GU.freed[b] = m_h[q]
                    q = s - 2
                    if 0 <= q < UN:
                        slot, use = q % RN, q // RN
                        b, bank = DN.take(pe)
                        pe.after(m_h[q])
                        for h in range(HB):
                            m = nc.tensor.matmul(bank[:, h * D:(h + 1) * D], hg[:, q % 3, h * P:(h + 1) * P], w_down(slot), start=True, stop=True)
                        m_dn[q] = pe.mark(m)
                        dve.after(m_dn[q])
                        dve.engine.wait_ge(s_y[slot], i * (16 * uses) + 16 * (use + 1))
                        m = dve.mark(nc.vector.tensor_copy(ys[:, slot, :, :].rearrange("p h d -> p (h d)"), bank))
                        DN.freed[b] = m
                        sp.after(m_dn[q])
                        fetch(i * UN + q + RN, slot)
                        sp.after(m)
                        nc.sync.dma_start(rows_out[bass.ds(i * UN + q, 1), :, :, :].rearrange("a p h d -> p (a h) d"), ys[:, slot, :, :]).then_inc(s_y[slot], 16)
                L.finish()
            for slot in range(RN):
                nc.sync.wait_ge(s_y[slot], 16 * (Z.tiles // RN + 1))
                nc.sync.wait_ge(s_x[slot], 16 * (Z.tiles // RN + 1))
                nc.sync.wait_ge(s_w[slot], 16 * (Z.tiles // RN + 1))
            nc.all_engine_barrier()

        with ExitStack() as s4:
            L = Lanes(nc, "d4", s4)
            NS = 4
            sb4 = lambda name, shape, dt=F32: s4.enter_context(nc.sbuf_tensor("d4_" + name, shape, dt))
            got, x = ([sb4(f"{n}{i}", s) for i in range(NS)] for n, s in (("got", [P, TL * PK, D]), ("x", [P, TL, D])))
            from_row = sb4("from_row", [P, TT * PK], U32)
            s_got = [[s4.enter_context(nc.semaphore(f"d4_got{i}_{t}")) for t in range(TL)] for i in range(NS)]
            s_x, s_out = ([s4.enter_context(nc.semaphore(f"d4_{n}{i}")) for i in range(NS)] for n in ("x", "out"))
            out_view = out.rearrange("b t d -> (b t) d")
            L.prime()
            for slot in range(NS):
                nc.sync.sem_inc(s_out[slot], 16)
            nc.vector.tensor_copy(from_row[:, :], flat(rows[:, :, :]))
            nc.all_engine_barrier()
            pool, dve, sp = L.pool, L.dve, L.sp
            to_read = sb4("to_read", [P, NS * TL * PK], U32)
            with nc.Fori(0, NCH // NS) as i:
                L.begin(i)
                m_rows = dve.mark(nc.vector.tensor_copy(to_read[:, :], from_row[:, bass.ds(i * (NS * TL * PK), NS * TL * PK)]))
                for slot in range(NS):
                    c = i * NS + slot
                    sp.engine.wait_ge(s_out[slot], i * 16 + 16)
                    nc.sync.sem_inc(sp.pause, 1)
                    nc.sync.dma_start(x[slot][:, :, :], chunk_of(x_in, c)).then_inc(s_x[slot], 16)
                pool.after_alone(m_rows)
                for slot in range(NS):
                    for t in range(TL):
                        for k in range(PK):
                            at = (slot * TL + t) * PK + k
                            nc.gpsimd.indirect_dma_start(out=got[slot][:, t * PK + k, :], out_offset=None, in_=sorted_y,
                                                         in_offset=bass.IndirectOffsetOnAxis(ap=to_read[:, at:at + 1], axis=0),
                                                         bounds_check=Z.tiles * SL - 1).then_inc(s_got[slot][t], 16)
                for slot in range(NS):
                    c = i * NS + slot
                    dve.engine.wait_ge(s_x[slot], i * 16 + 16)
                    for t in range(TL):
                        dve.engine.wait_ge(s_got[slot][t], i * (16 * PK) + 16 * PK)
                        for k in range(PK):
                            m = dve.mark(nc.vector.scalar_tensor_tensor(out=x[slot][:, t, :], in0=got[slot][:, t * PK + k, :],
                                                                        scalar=weights[:, bass.ds(c * TL + t, 1), k:k + 1].rearrange("p a b -> p (a b)"),
                                                                        in1=x[slot][:, t, :], op0=ALU.mult, op1=ALU.add))
                            dve.after(m)
                    sp.after(m)
                    nc.sync.dma_start(chunk_of(out_view, c), x[slot][:, :, :]).then_inc(s_out[slot], 16)
                L.finish()
            for slot in range(NS):
                nc.sync.wait_ge(s_out[slot], 16 * (NCH // NS) + 16)
            nc.all_engine_barrier()


def build(nc, I, out, phases="ACD"):
    with ExitStack() as st:
        T, D = out.shape[0] * out.shape[1], out.shape[2]
        consts = {"ident": st.enter_context(nc.sbuf_tensor("ident", [P, P], F32)),
                  "neghalf": st.enter_context(nc.sbuf_tensor("neghalf", [P, 4], F32))}
        psum = st.enter_context(nc.psum_tensor("psum", [P, 8, 512], F32))
        x2, x3, normed = (nc.dram_tensor(n, (T, D), F32).ap() for n in ("x2", "x3", "normed"))
        Z = SortedExperts(T)
        sorted_x = nc.dram_tensor("sorted_x", (Z.rows, D), F32).ap()
        sorted_y = nc.dram_tensor("sorted_y", (Z.tiles * Z.SLOTS, D), F32).ap()
        expert_list = nc.dram_tensor("expert_list", (2 * P,), mybir.dt.int32).ap()
        s_clear = st.enter_context(nc.semaphore("s_clear"))
        zeros = st.enter_context(nc.sbuf_tensor("zeros", [P, D], F32))
        nc.vector.memset(zeros[:, :], 0.0)
        nc.all_engine_barrier()
        clear = lambda first, count: clear_sorted_rows(nc, zeros, sorted_x, s_clear, first, count)
        if "A" in phases:
            layer0_phase(nc, psum, consts, I, I["L0_attn_x"], x2, clear)
        else:
            with nc.semaphore("ld0") as q:
                nc.sync.dma_start(x2, I["L0_attn_x"].rearrange("b t d -> (b t) d")).then_inc(q, 16)
                nc.sync.dma_start(consts["ident"][:, :], I["ident"]).then_inc(q, 16)
                nc.sync.wait_ge(q, 32)
                nc.vector.memset(consts["neghalf"][:, :], -0.5)
                nc.all_engine_barrier()
                if "D" in phases:
                    clear(0, CLEARS)
                else:
                    nc.sync.sem_inc(s_clear, 16 * CLEARS)
        if phases == "A":
            dump_x(nc, x2, out)
            return
        route = Route(nc, st, T)
        layer1_phase(nc, psum, consts, I, route, x2, x3, normed)
        nc.sync.wait_ge(s_clear, 16 * CLEARS)
        nc.all_engine_barrier()
        if "D" in phases:
            sorted_experts_phase(nc, psum, consts, I, route, x3, normed, out, sorted_x, sorted_y, expert_list)
        else:
            dump_x(nc, x3, out)


def dump_x(nc, x, out):
    with nc.semaphore("s_out") as s_out:
        nc.sync.dma_start(out.rearrange("b t d -> (b t) d"), x).then_inc(s_out, 16)
        nc.sync.wait_ge(s_out, 16)


def shape_constants():
    import numpy as np
    dk, per_seq, chunks = 16, 4, 16
    p = np.arange(P)
    same = (p[:, None] // dk == p[None, :] // dk)
    spread = np.stack([same & (p[:, None] % dk == v) for v in range(dk)], axis=1)
    mask = np.tile((np.arange(chunks + 1) % per_seq != 0)[None, :], (P, 1))
    part_rows = np.concatenate([np.eye(32, dk, dtype=np.float32)] * 3)
    state_spread = np.repeat(part_rows[:, :, None], P, axis=2).reshape(96, -1, 512)
    tile_no = p[:, None] + P * np.arange(2)[None, :]
    return {"tri": (p[:, None] < p[None, :]).astype(np.float32), "tile_no": tile_no.astype(np.float32),
            "iota": np.tile(np.arange(32, dtype=np.float32), (P, 1)), "state_spread": state_spread, "ident": np.eye(P, dtype=np.float32), "spread": spread.astype(np.float32),
            "head_of": (p[:, None] // dk == np.arange(P // dk)[None, :]).astype(np.float32), "chunk_mask": mask.astype(np.float32)}


def by_rows(w):
    return w.reshape(-1, P, w.shape[-1]).transpose(1, 0, 2)


def layouts(i):
    import numpy as np
    i = {k: np.asarray(v) for k, v in i.items()}
    a = {n: i["L0_attn_" + n] for n in ("Wr", "Wk", "Wv", "Wg", "Wo", "wA")}
    a["w1"], a["w2"] = i["L0_attn_ffn_w1"], i["L0_attn_ffn_w2"]
    d = {"a_" + k: by_rows(v) for k, v in a.items()}
    d["a_cols"] = np.stack([i["L0_attn_" + n].reshape(-1, P).T for n in A_COLS], axis=1)
    c = {n: i["L1_attn_" + n] for n in ("W_in", "W_dt", "W_out", "W_x", "W_conv", "A_log", "b_conv", "b_dt", "D")}
    d["c_W_in"], d["c_W_dt"], d["c_W_out"] = (by_rows(c[n].T) for n in ("W_in", "W_dt", "W_out"))
    w_b = by_rows(c["W_x"][c["W_x"].shape[0] // 2:].T)
    d["c_W_B"] = np.concatenate([w_b, np.zeros_like(w_b)] * 3, axis=2)
    rows = np.concatenate([c["A_log"], c["W_conv"][:, 0, :]] + [c[n][:, None] for n in ("b_conv", "b_dt", "D")], axis=1)
    d["c_cols"] = by_rows(rows)
    experts = []
    for g in "01":
        for n in ("wg", "wu"):
            a = i[f"L1_ffn_{n}{g}"]
            experts.append(a.reshape(a.shape[0], -1, P, P).transpose(0, 2, 1, 3).reshape(a.shape[0], P, -1))
        experts.append(i[f"L1_ffn_wd{g}"])
    d["d_experts"] = np.concatenate([np.concatenate(experts[0:3], axis=2), np.concatenate(experts[3:6], axis=2)])
    d["d_router"] = by_rows(np.concatenate([i["L1_ffn_router_w0"], i["L1_ffn_router_w1"]], axis=1))
    up = np.concatenate([i["L0_ffn_shared_up"], i["L0_ffn_routed_up"]])
    down = np.concatenate([i["L0_ffn_shared_down"], i["L0_ffn_routed_down"]])
    d["b_up"] = up.reshape(up.shape[0], P, -1, P).transpose(3, 0, 2, 1)
    d["b_down"] = down.transpose(2, 0, 1)
    d["b_router"] = by_rows(i["L0_ffn_router_w"].T)
    d["a_gn_w"], d["a_gn_b"] = i["L0_attn_gn_w"].reshape(-1), i["L0_attn_gn_b"].reshape(-1)
    d["L0_attn_wB"] = i["L0_attn_wB"]
    d["L0_attn_x"] = i["L0_attn_x"]
    return d


def kernel(**inputs):
    import numpy as _np
    import concourse.bacc as _bacc
    from concourse import mybir as _mybir
    from concourse.bass_utils import run_bass_kernel_spmd as _run

    nc = _bacc.Bacc("TRN2", target_bir_lowering=False, num_devices=1)
    nc.disable_value_cache = True
    arrays, aps = {}, {}
    for name, a in list(layouts(inputs).items()) + list(shape_constants().items()):
        a = _np.ascontiguousarray(a)
        arrays[f"in_{name}"] = a
        aps[name] = nc.dram_tensor(f"in_{name}", a.shape, _mybir.dt.from_np(a.dtype), kind="ExternalInput").ap()
    out = nc.dram_tensor("out_x", inputs["L0_attn_x"].shape, _mybir.dt.float32, kind="ExternalOutput").ap()
    build(nc, aps, out)
    r = _run(nc, [arrays], core_ids=[0])
    return r.results[0]["out_x"]
```

```python
from contextlib import ExitStack

import concourse.bass as bass
from concourse import mybir

P = 128
ALU = mybir.AluOpType
ACT = mybir.ActivationFunctionType
F32 = mybir.dt.float32
EPS_LN = 1e-5
EPS_RMS = 1e-6
EPS_GN = 1e-5
LANE_STEP = 2048


A_COLS = ("mu_r", "mu_k", "mu_v", "mu_w", "mu_g", "ln1_w", "ln2_w", "w0", "u", "gn_w", "gn_b")


class Mark:

    def __init__(self, lane, ordinal, body):
        self.lane, self.ordinal, self.body = lane, ordinal, body


class Lane:

    def __init__(self, nc, engine, name, stack):
        self.engine = engine
        self.sem = stack.enter_context(nc.semaphore(name))
        self.pause = stack.enter_context(nc.semaphore(name + "_pause"))
        self.base, self.count, self.waited, self.body = 0, 0, {}, 0

    def begin(self, base, body):
        self.base, self.count, self.waited, self.body = base, 0, {}, body

    def mark(self, instruction):
        self.count += 1
        instruction.then_inc(self.sem, 1)
        return Mark(self, self.count, self.body)

    def after(self, *marks):
        for m in marks:
            if m is None or m.body != self.body or self.waited.get(m.lane, 0) >= m.ordinal:
                continue
            self.waited[m.lane] = m.ordinal
            self.engine.wait_ge(m.lane.sem, m.lane.base + m.ordinal)

    def after_alone(self, *marks):
        self.after(*marks)
        self.engine.sem_inc(self.pause, 1)

    def finish(self):
        assert self.count < LANE_STEP
        if self.count:
            self.engine.wait_ge(self.sem, self.base + self.count)
        self.engine.sem_inc(self.sem, LANE_STEP - self.count)


class Lanes:

    def __init__(self, nc, phase, stack):
        self.pe = Lane(nc, nc.tensor, f"{phase}_pe", stack)
        self.act = Lane(nc, nc.scalar, f"{phase}_act", stack)
        self.dve = Lane(nc, nc.vector, f"{phase}_dve", stack)
        self.pool = Lane(nc, nc.gpsimd, f"{phase}_pool", stack)
        self.sp = Lane(nc, nc.sync, f"{phase}_sp", stack)
        self.all = [self.pe, self.act, self.dve, self.pool, self.sp]
        self.bodies = 0

    def begin(self, index):
        self.bodies += 1
        for lane in self.all:
            lane.begin(index * LANE_STEP + 1, self.bodies)
        for lane in self.all:
            for other in self.all:
                if other is not lane:
                    lane.engine.wait_ge(other.sem, other.base)
        self.sp.engine.sem_inc(self.sp.pause, 1)

    def prime(self):
        for lane in self.all:
            lane.engine.sem_inc(lane.sem, 1)

    def finish(self):
        for lane in self.all:
            lane.finish()


class Banks:

    def __init__(self, tensor, first, count):
        self.tensor, self.first, self.count, self.turn = tensor, first, count, 0
        self.freed = [None] * count

    def begin(self):
        self.turn, self.freed = 0, [None] * self.count

    def take(self, lane):
        i = self.turn % self.count
        self.turn += 1
        assert self.freed[i] != "held"
        lane.after(self.freed[i])
        self.freed[i] = "held"
        return i, self.tensor[:, self.first + i, :]


class Shared:

    def __init__(self, tensor):
        self.tensor, self.readers = tensor, []

    def claim(self, *lanes):
        for lane in lanes:
            lane.after(*self.readers)
        self.readers = []


class Background:

    def __init__(self, *streams):
        self.streams = [[rate, 0.0, list(stages)] for rate, stages in streams]

    def pull(self):
        for stream in self.streams:
            stream[1] += stream[0]
            while stream[1] >= 1 and stream[2]:
                stream[1] -= 1
                self.advance(stream[2])

    @staticmethod
    def advance(stages):
        try:
            next(stages[0])
        except StopIteration:
            stages.pop(0)

    def drain(self, until=lambda: False):
        while any(stages for _, _, stages in self.streams) and not until():
            for _, _, stages in self.streams:
                if stages:
                    self.advance(stages)


def abreast(*stages):
    stages = list(stages)
    while stages:
        for stage in list(stages):
            try:
                next(stage)
            except StopIteration:
                stages.remove(stage)
            yield


def load(nc, sem, pairs):
    for dst, src in pairs:
        nc.sync.dma_start(dst, src).then_inc(sem, 16)
    return 16 * len(pairs)


def matmuls(nc, out, pairs):
    for n, (lhsT, rhs) in enumerate(pairs):
        last = nc.tensor.matmul(out, lhsT, rhs, start=(n == 0), stop=(n == len(pairs) - 1))
    return last


def layer0_phase(nc, psum, consts, I, x_in, x_out):
    C, D, H, DK, LORA, F = 512, 256, 16, 16, 64, 1024
    E, SH, TOP = 16, 2, 4
    KB, TL, HP, FB = D // P, C // P, P // DK, F // P
    NCH = x_in.shape[0] * x_in.shape[1] // C
    AX = mybir.AxisListType.X
    with ExitStack() as st:
        sb = lambda name, shape, dt=F32: st.enter_context(nc.sbuf_tensor("a_" + name, shape, dt))
        sem = lambda name: st.enter_context(nc.semaphore("a_" + name))
        L = Lanes(nc, "a", st)
        pe, act, dve, pool, sp = L.pe, L.act, L.dve, L.pool, L.sp
        s_load, s_xa = sem("load"), sem("xa")
        s_xb, s_store = ([sem(f"{n}{i}") for i in range(2)] for n in ("xb", "store"))
        W = {n: sb(n, [P, KB, D]) for n in ("Wr", "Wk", "Wv", "Wg", "Wo")}
        wA, wB = sb("wA", [P, KB, LORA]), sb("wB", [LORA, D])
        w1, w2 = sb("w1", [P, KB, F]), sb("w2", [P, FB, D])
        head_of = sb("head_of", [P, HP])
        chunk_mask = sb("chunk_mask", [P, NCH + 1])
        col_pack = sb("cols", [P, len(A_COLS), KB])
        cols = {n: col_pack[:, i, :] for i, n in enumerate(A_COLS)}
        gn_w, gn_b = sb("gn_w", [P, D]), sb("gn_b", [P, D])
        eps_gn = sb("eps_gn", [P, 1])
        W_up, W_down = sb("W_up", [P, SH + E, KB, P]), sb("W_down", [P, SH + E, D])
        W_router, iota = sb("W_router", [P, KB, E]), sb("iota", [P, 32])
        ident, neghalf = consts["ident"], consts["neghalf"]

        rkvd = [sb(f"rkvd{i}", [P, 4, KB, C]) for i in range(2)]
        gate, bonus = ([sb(f"{n}{i}", [P, TL, D]) for i in range(2)] for n in ("gate", "bonus"))
        mv = [sb(f"mv{i}", [P, TL, 2]) for i in range(2)]
        rstd = [sb(f"rstd{i}", [P, TL]) for i in range(2)]
        NR = 3
        NV = 8
        kv, prod = sb("kv", [P, NV, C]), sb("prod", [P, NR, C])
        v_rows = nc.dram_tensor("v_rows", (2, D, C), F32).ap()
        s_vout, s_vrep = sem("vout"), [sem(f"vrep{i}") for i in range(NV)]
        S = sb("S", [P, NR, C + 1])
        carry = sb("carry", [P, KB * DK])
        o = Shared(sb("o", [P, TL, D]))
        xa, x1 = sb("xa", [P, TL, D]), sb("x1", [P, TL, D])
        xb = [sb(f"xb{i}", [P, TL, D]) for i in range(2)]
        hn, bgT = Shared(sb("hn", [P, TL, D])), Shared(sb("bgT", [P, KB, C]))
        hn_before, xx = Shared(sb("hn_before", [P, TL, D])), Shared(sb("xx", [P, KB, C]))
        hT = Shared(sb("hT", [P, KB, C + 1]))
        xm = [Shared(sb(f"xm{i}", [P, KB, C])) for i in range(2)]
        NH = 3
        hidden = sb("hidden", [P, NH, C])
        lora = Shared(sb("lora", [LORA, C]))
        stats = [sb(f"stats{i}", [P, TL, 6]) for i in range(2)]
        ve, ms, rms = ([sb(f"{n}{i}", [P, TL]) for i in range(2)] for n in ("ve", "ms", "rms"))
        ssq = sb("ssq", [P, TL])
        heads = sb("heads", [P, TL * H])
        bon = sb("bon", [P, TL * H])
        gates = sb("gates", [P, TL, E])
        R = router_buffers(nc, st, "a", 1, E, TOP)

        pairs = [(W[n][:, :, :], I["a_" + n]) for n in W]
        pairs += [(wA[:, :, :], I["a_wA"]), (wB[:, :], I["L0_attn_wB"]), (w1[:, :, :], I["a_w1"]), (w2[:, :, :], I["a_w2"]),
                  (head_of[:, :], I["head_of"]), (chunk_mask[:, :], I["chunk_mask"]),
                  (ident[:, :], I["ident"]), (col_pack[:, :, :], I["a_cols"]), (gn_w[:, :], I["a_gn_w"].partition_broadcast(P)),
                  (gn_b[:, :], I["a_gn_b"].partition_broadcast(P)), (W_up[:, :, :, :], I["b_up"]), (W_down[:, :, :], I["b_down"]),
                  (W_router[:, :, :], I["b_router"]), (iota[:, :], I["iota"])]
        loaded = load(nc, s_load, pairs)
        nc.vector.memset(neghalf[:, :], -0.5)
        nc.vector.memset(eps_gn[:, :], EPS_GN)
        nc.vector.memset(carry[:, :], 0.0)
        nc.vector.memset(hT.tensor[:, :, C], 0.0)
        nc.vector.wait_ge(s_load, loaded)
        nc.vector.tensor_scalar(gn_w[:, :], gn_w[:, :], 0.5, None, ALU.mult)
        nc.vector.tensor_scalar(gn_b[:, :], gn_b[:, :], 0.5, None, ALU.mult)
        nc.sync.wait_ge(s_load, loaded)
        for slot in range(2):
            nc.sync.sem_inc(s_store[slot], 16)
        L.prime()
        nc.all_engine_barrier()

        chunks_in = x_in.rearrange("b (c t p) d -> p (b c) t d", p=P, t=TL)
        chunks_out = x_out.rearrange("(c t p) d -> p c t d", p=P, t=TL)
        chunk_of = lambda view, c: view[:, bass.ds(c, 1), :, :].rearrange("p a t d -> p (a t) d")
        GB, OB, DN, G = Banks(psum, 0, 2), 2, Banks(psum, 4, 2), Banks(psum, 6, 2)
        o_free, o_parts = [None], {}
        scan_done = [[], []]
        post_done, mv_read = [[], []], [[], []]
        xa_read, hid_read, hid_turn = [None], {}, [0]
        x1_read = []
        mv_free, gate_free = [True, True], [True, True]
        gated, summed, stored = [[], []], [[], []], set()
        flat = lambda ap: ap.rearrange("p a b -> p (a b)")

        def transposed(G, src, dst, scale=None):
            marks = []
            for kb in range(KB):
                i, bank = G.take(pe)
                for t in range(TL):
                    m = nc.tensor.transpose(bank[:, t * P:(t + 1) * P], src[:, t, kb * P:(kb + 1) * P], ident[:, :])
                m = pe.mark(m)
                yield
                act.after(m)
                if scale is None:
                    m = act.mark(nc.scalar.copy(dst(kb), bank))
                else:
                    m = act.mark(nc.scalar.activation(dst(kb), bank, ACT.Copy, scale=scale(kb)))
                G.freed[i] = m
                marks.append(m)
            return marks

        def variance(src, mvb, stats, ve):
            for t in range(TL):
                m = dve.mark(nc.vector.bn_stats(stats[:, t, :], src[:, t, :]))
            dve.after_alone(m)
            for t in range(TL):
                m = dve.mark(nc.vector.bn_aggr(mvb[:, t, :], stats[:, t, :]))
            yield
            dve.after(m)
            return dve.mark(nc.vector.tensor_scalar(ve[:, :], mvb[:, :, 1], EPS_LN, None, ALU.add))

        def inverse_root(dst, src, m):
            pool.after(m)
            return pool.mark(nc.gpsimd.tensor_tensor(dst, src, neghalf[:, 0:TL], ALU.pow))

        def load_xa(c):
            sp.after(xa_read[0])
            nc.sync.dma_start(xa[:, :, :], chunk_of(chunks_in, c)).then_inc(s_xa, 16)

        def load_xb(c, slot, turn):
            sp.engine.wait_ge(s_store[slot], turn * 16)
            nc.sync.dma_start(xb[slot][:, :, :], chunk_of(chunks_in, c)).then_inc(s_xb[slot], 16)

        def before(c, slot):
            rT, kT, vT, dT = (rkvd[slot][:, i] for i in range(4))
            done = {}
            h = hT.tensor
            hT.claim(dve, act)
            prev = dve.mark(nc.vector.tensor_scalar(h[:, :, 0], h[:, :, C], chunk_mask[:, bass.ds(c, 1)], None, ALU.mult))
            dve.engine.wait_ge(s_xa, c * 16 + 16)
            while not mv_free[slot]:
                yield
            mv_free[slot] = False
            dve.after(*mv_read[slot])
            pool.after(*mv_read[slot])
            m = yield from variance(xa, mv[slot], stats[0], ve[0])
            m = inverse_root(rstd[slot][:, :], ve[0][:, :], m)
            yield
            dve.after(m)
            m = dve.mark(nc.vector.tensor_tensor(ms[0][:, :], rstd[slot][:, :], rstd[slot][:, :], ALU.mult))
            dve.after(m)
            m = dve.mark(nc.vector.tensor_tensor(ms[0][:, :], ms[0][:, :], mv[slot][:, :, 1], ALU.mult))
            dve.after(m)
            m = dve.mark(nc.vector.tensor_scalar(ms[0][:, :], ms[0][:, :], EPS_RMS, None, ALU.add))
            m = inverse_root(rms[0][:, :], ms[0][:, :], m)
            yield
            dve.after(m)
            m = dve.mark(nc.vector.tensor_tensor(ms[0][:, :], rms[0][:, :], rstd[slot][:, :], ALU.mult))
            dve.after(m)
            hn_before.claim(dve)
            for t in range(TL):
                m = dve.mark(nc.vector.tensor_scalar(hn_before.tensor[:, t, :], xa[:, t, :], mv[slot][:, t, 0:1], ms[0][:, t:t + 1], ALU.subtract, ALU.mult))
            xa_read[0] = m
            yield
            pe.after(m)
            act.after(prev)
            marks = yield from transposed(GB, hn_before.tensor, lambda kb: h[:, kb, 1:C + 1], lambda kb: cols["ln1_w"][:, kb:kb + 1])
            hn_before.readers = marks
            yield
            xx.claim(dve)
            x_x = xx.tensor
            for kb in range(KB):
                dve.after(marks[kb])
                m = dve.mark(nc.vector.tensor_tensor(x_x[:, kb, :], h[:, kb, 0:C], h[:, kb, 1:C + 1], ALU.subtract))
            yield
            dve.after(m)
            act.after(*scan_done[slot])
            for n, mu in enumerate(("mu_w", "mu_g", "mu_v", "mu_k", "mu_r")):
                buf = xm[n % 2]
                buf.claim(dve)
                for kb in range(KB):
                    m = dve.mark(nc.vector.scalar_tensor_tensor(out=buf.tensor[:, kb, :], in0=x_x[:, kb, :], scalar=cols[mu][:, kb:kb + 1],
                                                                in1=h[:, kb, 1:C + 1], op0=ALU.mult, op1=ALU.add))
                if mu == "mu_r":
                    hT.readers = [m]
                    xx.readers = [m]
                yield
                pe.after(m)
                if mu == "mu_w":
                    i, bank = GB.take(pe)
                    m = pe.mark(matmuls(nc, bank[0:LORA, :], [(wA[:, kb, :], buf.tensor[:, kb, :]) for kb in range(KB)]))
                    buf.readers = [m]
                    yield
                    lora.claim(act)
                    act.after(m)
                    m = act.mark(nc.scalar.activation(lora.tensor[:, :], bank[0:LORA, :], ACT.Tanh))
                    GB.freed[i] = m
                    yield
                    pe.after(m)
                    for ob in range(KB):
                        i, bank = GB.take(pe)
                        m = pe.mark(matmuls(nc, bank, [(wB[:, ob * P:(ob + 1) * P], lora.tensor[:, :])]))
                        lora.readers = [m]
                        yield
                        act.after(m)
                        m = act.mark(nc.scalar.activation(dT[:, ob, :], bank, ACT.Exp, bias=cols["w0"][:, ob:ob + 1]))
                        GB.freed[i] = m
                        act.after(m)
                        done["d"] = act.mark(nc.scalar.activation(dT[:, ob, :], dT[:, ob, :], ACT.Exp, scale=-1.0))
                    continue
                if mu == "mu_g":
                    while not gate_free[slot]:
                        yield
                    gate_free[slot] = False
                    for half in range(2):
                        i, bank = GB.take(pe)
                        for t in range(2):
                            at = (2 * half + t) * P
                            m = matmuls(nc, bank[:, t * D:(t + 1) * D], [(buf.tensor[:, kb, at:at + P], W["Wg"][:, kb, :]) for kb in range(KB)])
                        m = pe.mark(m)
                        buf.readers = [m]
                        yield
                        act.after(m, *post_done[slot])
                        part = flat(gate[slot][:, 2 * half:2 * half + 2, :])
                        m = act.mark(nc.scalar.activation(part, bank, ACT.Tanh, scale=0.5))
                        yield
                        dve.after(m)
                        done["g"] = dve.mark(nc.vector.scalar_tensor_tensor(out=part, in0=part, scalar=1.0, in1=bank, op0=ALU.add, op1=ALU.mult))
                        GB.freed[i] = done["g"]
                    continue
                dst, w = {"mu_k": (kT, W["Wk"]), "mu_v": (vT, W["Wv"]), "mu_r": (rT, W["Wr"])}[mu]
                for ob in range(KB):
                    i, bank = GB.take(pe)
                    m = pe.mark(matmuls(nc, bank, [(w[:, kb, ob * P:(ob + 1) * P], buf.tensor[:, kb, :]) for kb in range(KB)]))
                    buf.readers = [m]
                    yield
                    act.after(m)
                    done[mu[-1]] = act.mark(nc.scalar.copy(dst[:, ob, :], bank))
                    GB.freed[i] = done[mu[-1]]
                if mu == "mu_v":
                    sp.after(done["v"])
                    nc.sync.dma_start(v_rows[slot].rearrange("(k p) t -> p k t", p=P), vT).then_inc(s_vout, 16)
                    stored.add(slot)
            ruk = xm[1]
            ruk.claim(dve)
            dve.after(done["r"], done["k"], *post_done[slot])
            for kb in range(KB):
                m = dve.mark(nc.vector.scalar_tensor_tensor(out=ruk.tensor[:, kb, :], in0=rT[:, kb, :], scalar=cols["u"][:, kb:kb + 1],
                                                            in1=kT[:, kb, :], op0=ALU.mult, op1=ALU.mult))
            yield
            pe.after(m)
            i, bank = GB.take(pe)
            for t in range(TL):
                for kb in range(KB):
                    m = matmuls(nc, bank[:, (t * KB + kb) * HP:(t * KB + kb + 1) * HP], [(ruk.tensor[:, kb, t * P:(t + 1) * P], head_of[:, :])])
            m = pe.mark(m)
            ruk.readers = [m]
            yield
            act.after(m)
            m_bon = act.mark(nc.scalar.copy(bon[:, :], bank[:, 0:TL * H]))
            GB.freed[i] = m_bon
            pe.after(done["v"])
            for half in range(2):
                i, bank = GB.take(pe)
                for t in range(2):
                    for kb in range(KB):
                        at = (2 * half + t) * P
                        m = nc.tensor.transpose(bank[:, t * D + kb * P:t * D + (kb + 1) * P], vT[:, kb, at:at + P], ident[:, :])
                m = pe.mark(m)
                yield
                dve.after(m, m_bon)
                HH = TL * H // 2
                m = dve.mark(nc.vector.tensor_tensor(
                    flat(bonus[slot][:, 2 * half:2 * half + 2, :]).rearrange("p (h v) -> p h v", v=DK), bank.rearrange("p (h v) -> p h v", v=DK),
                    bon[:, half * HH:(half + 1) * HH].unsqueeze(2).broadcast_to([P, HH, DK]), ALU.mult))
                GB.freed[i] = m
            done["b"] = m
            ready[slot] = done

        def two_layer(blocks, up_pairs, down):
            banks = [DN.take(pe) for _ in range(2)]
            m_hidden = {}
            for f in range(blocks + 1):
                if f < blocks:
                    i, bank = G.take(pe)
                    m = pe.mark(matmuls(nc, bank, up_pairs(f)))
                    yield
                    r = hid_turn[0] % NH
                    act.after(m, hid_read.get(r))
                    m_hidden[f] = (act.mark(nc.scalar.activation(hidden[:, r, :], bank, ACT.Gelu)), r)
                    hid_turn[0] += 1
                    G.freed[i] = m_hidden[f][0]
                q = f - 1
                if q >= 0:
                    mh, r = m_hidden[q]
                    pe.after(mh)
                    for t in range(TL):
                        m = nc.tensor.matmul(banks[t // 2][1][:, (t % 2) * D:(t % 2 + 1) * D], hidden[:, r, t * P:(t + 1) * P], down(q),
                                             start=(q == 0 and t % 2 == 0), stop=(q == blocks - 1 and t % 2 == 1), skip_group_check=True)
                    hid_read[r] = pe.mark(m)
                    yield
            return banks, hid_read[r]

        def add_sums(xb, banks, m):
            dve.after(m)
            for half, (i, bank) in enumerate(banks):
                part = flat(xb[:, 2 * half:2 * half + 2, :])
                m = dve.mark(nc.vector.tensor_tensor(part, part, bank, ALU.add))
                DN.freed[i] = m
            return m

        def head_norm(slot, turn):
            ot = o.tensor
            by_head = flat(ot[:, :, :]).rearrange("p (h v) -> p h v", v=DK)
            wide = lambda ap: ap.unsqueeze(2).broadcast_to([P, TL * H, DK])
            dve.engine.wait_ge(s_xb[slot], turn * 16)
            dve.after(*x1_read)
            for t in range(TL):
                m_xn = dve.mark(nc.vector.tensor_scalar(x1[:, t, :], xb[slot][:, t, :], mv[slot][:, t, 0:1], rstd[slot][:, t:t + 1], ALU.subtract, ALU.mult))
            mv_read[slot], mv_free[slot] = [m_xn], True
            yield
            dve.after(o_ready[0])
            m = dve.mark(nc.vector.tensor_tensor(flat(ot[:, :, :]), flat(ot[:, :, :]), flat(bonus[slot][:, :, :]), ALU.add))
            dve.after(m)
            m = dve.mark(nc.vector.tensor_reduce(heads[:, :], by_head, AX, ALU.add))
            dve.after(m)
            m = dve.mark(nc.vector.tensor_scalar(heads[:, :], heads[:, :], 1.0 / DK, None, ALU.mult))
            dve.after(m)
            m = dve.mark(nc.vector.tensor_tensor(by_head, by_head, wide(heads[:, :]), ALU.subtract))
            yield
            hn_before.claim(act)
            act.after(m)
            m = act.mark(nc.scalar.activation(flat(hn_before.tensor[:, :, :]), flat(ot[:, :, :]), ACT.Square))
            yield
            dve.after(m)
            m = dve.mark(nc.vector.tensor_reduce(heads[:, :], flat(hn_before.tensor[:, :, :]).rearrange("p (h v) -> p h v", v=DK), AX, ALU.add))
            hn_before.readers = [m]
            yield
            nc.scalar.preload_act_table_set("natural_log_exp_and_others")
            act.after(m)
            m = act.mark(nc.scalar.activation(heads[:, :], heads[:, :], ACT.Ln, scale=1.0 / DK, bias=eps_gn[:, 0:1]))
            act.after(m)
            m = act.mark(nc.scalar.activation(heads[:, :], heads[:, :], ACT.Exp, scale=-0.5))
            yield
            dve.after(m)
            m = dve.mark(nc.vector.tensor_tensor(by_head, by_head, wide(heads[:, :]), ALU.mult))
            over_tiles = lambda row: row[:, :].unsqueeze(1).broadcast_to([P, TL, D])
            for operand, op in ((over_tiles(gn_w), ALU.mult), (over_tiles(gn_b), ALU.add), (gate[slot][:, :, :], ALU.mult)):
                pool.after(m)
                m = pool.mark(nc.gpsimd.tensor_tensor(ot[:, :, :], ot[:, :, :], operand, op))
                yield
            post_done[slot], gate_free[slot] = [m], True
            gated[slot] = [m, m_xn]

        def feed_forward(slot):
            xb_, ot = xb[slot], o.tensor
            while not gated[slot]:
                yield
            m, m_xn = gated[slot]
            gated[slot] = []
            pe.after(m)
            bgT.claim(act)
            oT = bgT.tensor
            marks = yield from transposed(G, ot, lambda kb: oT[:, kb, :])
            o.readers = marks
            pe.after(*marks)
            dve.after(m_xn)
            for half in range(2):
                i, bank = G.take(pe)
                for t in range(2):
                    at = (2 * half + t) * P
                    m = matmuls(nc, bank[:, t * D:(t + 1) * D], [(oT[:, kb, at:at + P], W["Wo"][:, kb, :]) for kb in range(KB)])
                m = pe.mark(m)
                bgT.readers = [m]
                yield
                dve.after(m)
                part = flat(x1[:, 2 * half:2 * half + 2, :])
                m_x1 = dve.mark(nc.vector.tensor_tensor(part, part, bank, ALU.add))
                G.freed[i] = m_x1
            yield
            hn.claim(act)
            act.after(m_x1)
            for t in range(TL):
                m = act.mark(nc.scalar.activation(hn.tensor[:, t, :], x1[:, t, :], ACT.Square, accum_out=ssq[:, t:t + 1]))
            hn.readers = [m]
            yield
            dve.after(m)
            m = dve.mark(nc.vector.tensor_scalar(ms[1][:, :], ssq[:, :], 1.0 / D, EPS_RMS, ALU.mult, ALU.add))
            m = inverse_root(rms[1][:, :], ms[1][:, :], m)
            m_res = dve.mark(nc.vector.tensor_tensor(flat(xb_[:, :, :]), flat(xb_[:, :, :]), flat(x1[:, :, :]), ALU.add))
            yield
            hn.claim(dve)
            dve.after(m)
            for t in range(TL):
                m = dve.mark(nc.vector.tensor_scalar(hn.tensor[:, t, :], x1[:, t, :], rms[1][:, t:t + 1], None, ALU.mult))
            x1_read[:] = [m_res, m]
            yield
            pe.after(m)
            bgT.claim(act)
            h2T = bgT.tensor
            marks = yield from transposed(G, hn.tensor, lambda kb: h2T[:, kb, :], lambda kb: cols["ln2_w"][:, kb:kb + 1])
            hn.readers = marks
            pe.after(*marks)
            yield
            banks, m = yield from two_layer(FB, lambda f: [(w1[:, kb, f * P:(f + 1) * P], h2T[:, kb, :]) for kb in range(KB)], lambda f: w2[:, f, :])
            bgT.readers = [m]
            dve.after(m_res)
            summed[slot] = [add_sums(xb_, banks, m)]
            yield

        def experts(c, slot):
            xb_ = xb[slot]
            dve.after(*summed[slot])
            m = yield from variance(xb_, R["mv"], stats[1], ve[1])
            m = inverse_root(R["rstd"][:, :], ve[1][:, :], m)
            yield
            dve.after(m)
            hn.claim(dve)
            for t in range(TL):
                m = dve.mark(nc.vector.tensor_scalar(hn.tensor[:, t, :], xb_[:, t, :], R["mv"][:, t, 0:1], R["rstd"][:, t:t + 1], ALU.subtract, ALU.mult))
            yield
            pe.after(m)
            bgT.claim(act)
            xT = bgT.tensor
            marks = yield from transposed(G, hn.tensor, lambda kb: xT[:, kb, :])
            hn.readers = marks
            pe.after(*marks)
            yield
            up_of = lambda e: [(W_up[:, e, kb, :], xT[:, kb, :]) for kb in range(KB)]
            m_done = {}

            def weigh():
                m = yield from router(nc, L, G, xT, W_router, R, iota, 1, E, TOP)
                dve.after(m)
                m_done["gates"] = dve.mark(nc.vector.tensor_tensor(gates[:, :, :], R["chosen"][:, :, :], R["prob"][:, :, :], ALU.mult))
                yield

            def shared():
                banks, m = yield from two_layer(SH, up_of, lambda e: W_down[:, e, :])
                m_done["shared"] = add_sums(xb_, banks, m)
            yield from abreast(weigh(), shared())
            m_gates, m = m_done["gates"], m_done["shared"]
            m_acc = {t: m for t in range(TL)}
            dve.after(m_gates)
            m_hidden = {}
            for e in range(E + 1):
                if e < E:
                    i, bank = G.take(pe)
                    m = pe.mark(matmuls(nc, bank, up_of(SH + e)))
                    yield
                    r = hid_turn[0] % NH
                    act.after(m, hid_read.get(r))
                    m_hidden[e] = (act.mark(nc.scalar.activation(hidden[:, r, :], bank, ACT.Gelu)), r)
                    hid_turn[0] += 1
                    G.freed[i] = m_hidden[e][0]
                q = e - 1
                if q < 0:
                    continue
                mh, r = m_hidden[q]
                pe.after(mh)
                for half in range(2):
                    i, bank = DN.take(pe)
                    for t in (2 * half, 2 * half + 1):
                        m = nc.tensor.matmul(bank[:, (t % 2) * D:(t % 2 + 1) * D], hidden[:, r, t * P:(t + 1) * P], W_down[:, SH + q, :], start=True, stop=True)
                    hid_read[r] = pe.mark(m)
                    yield
                    dve.after(hid_read[r])
                    for t in (2 * half, 2 * half + 1):
                        dve.after(m_acc[t])
                        m_acc[t] = dve.mark(nc.vector.scalar_tensor_tensor(out=xb_[:, t, :], in0=bank[:, (t % 2) * D:(t % 2 + 1) * D],
                                                                           scalar=gates[:, t, q:q + 1], in1=xb_[:, t, :], op0=ALU.mult, op1=ALU.add))
                    DN.freed[i] = m_acc[2 * half + 1]
            bgT.readers = [hid_read[r]]
            sp.after(m_acc[TL - 1])
            nc.sync.dma_start(chunk_of(chunks_out, c), xb_[:, :, :]).then_inc(s_store[slot], 16)

        steps = KB * DK
        MAIN_RATE, SIDE_RATE, SETTLE, LEAD = 3.0, 1.3, 2, 6
        assert steps % NV == 0

        def scans(chunks):
            m_kv, m_scan, m_prod, m_sum, m_kept, m_first, m_start = ({} for _ in range(7))
            done_of, total = {}, len(chunks) * steps

            def fetch_channel(g, s, slot):
                hb, v = divmod(s, DK)
                sp.after(m_scan.get(g - NV))
                rows = v_rows[slot].rearrange("(b h v) t -> b h v t", b=KB, v=DK)[hb, :, v, :]
                nc.sync.dma_start(kv[:, g % NV, :], rows.unsqueeze(1).broadcast_to([HP, DK, C])).then_inc(s_vrep[s % NV], 16)
            for g in range(total + SETTLE):
                j = min(g // steps, len(chunks) - 1)
                s = g - j * steps
                if s == 0:
                    c, slot, prepare = chunks[j]
                    if j > 0:
                        background.drain(until=lambda: slot in stored)
                    stored.discard(slot)
                    sp.engine.wait_ge(s_vout, c * 16 + 16)
                    for k in range(LEAD):
                        fetch_channel(g + k, k, slot)
                    if j > 0:
                        background.drain()
                    streams = prepare()
                    done = done_of[j] = ready.get(slot, {})
                    pool.after(done.get("k"))
                    dve.after(done.get("d"), done.get("r"))
                if s == SETTLE:
                    background = Background(*streams)
                if g < total:
                    (hb, v), slot = divmod(s, DK), chunks[j][1]
                    if v == 0:
                        dve.after(m_kept.get(g - steps + DK - 1))
                        m_start[g // DK] = dve.mark(nc.vector.tensor_scalar(carry[:, s:s + DK], carry[:, s:s + DK], chunk_mask[:, bass.ds(chunks[j][0], 1)], None, ALU.mult))
                    if s + LEAD < steps:
                        fetch_channel(g + LEAD, s + LEAD, slot)
                    act.after(m_prod.get(g - NR), m_kept.get(g - NR), m_start[g // DK])
                    m_first[g] = act.mark(nc.scalar.copy(S[:, g % NR, 0:1], carry[:, s:s + 1]))
                    pool.engine.wait_ge(s_vrep[s % NV], chunks[j][0] * (16 * steps // NV) + 16 * (s // NV + 1))
                    m_kv[g] = pool.mark(nc.gpsimd.tensor_tensor(kv[:, g % NV, :], rkvd[slot][:, 1, hb, :], kv[:, g % NV, :], ALU.mult))
                q = g - 1
                if 0 <= q < total:
                    hb, slot = q % steps // DK, chunks[q // steps][1]
                    dve.after(m_kv[q], m_first[q], m_prod.get(q - NR), m_kept.get(q - NR))
                    m_scan[q] = dve.mark(nc.vector.tensor_tensor_scan(S[:, q % NR, 1:C + 1], rkvd[slot][:, 3, hb, :], kv[:, q % NV, :],
                                                                      S[:, q % NR, 0:1], ALU.mult, ALU.add))
                    act.after(m_scan[q])
                    m_kept[q] = act.mark(nc.scalar.copy(carry[:, q % steps:q % steps + 1], S[:, q % NR, C:C + 1]))
                    dve.after(m_scan[q], m_sum.get(q - NR))
                    m_prod[q] = dve.mark(nc.vector.tensor_tensor(prod[:, q % NR, :], rkvd[slot][:, 0, hb, :], S[:, q % NR, 0:C], ALU.mult))
                q = g - 2
                if 0 <= q < total:
                    hb, v = divmod(q % steps, DK)
                    pe.after(m_prod[q])
                    if q % steps == 0:
                        pe.after(*o_free)
                    for t in range(TL):
                        at = (t % 2) * D + hb * P + v
                        m = nc.tensor.matmul(psum[:, OB + t // 2, at:at + (HP - 1) * DK + 1:DK], prod[:, q % NR, t * P:(t + 1) * P], head_of[:, :],
                                             start=True, stop=True)
                    m_sum[q] = pe.mark(m)
                    if q % steps == steps - 1:
                        slot = chunks[q // steps][1]
                        scan_done[slot] = [m_kv[q], m_prod[q]]
                        o.claim(act)
                        act.after(m_sum[q])
                        o_free[:] = [act.mark(nc.scalar.copy(flat(o.tensor[:, 2 * half:2 * half + 2, :]), psum[:, OB + half, :])) for half in range(2)]
                        o_ready[0] = o_free[-1]
                if g < total and s >= SETTLE:
                    background.pull()
            background.drain()

        ready, o_ready = {}, [None]

        def stages(c, slot, i, first=False, last=False, second=False):
            def prepare():
                side, main = [], []
                if not first:
                    load_xb(c - 1, 1 - slot, i)
                    side.append(head_norm(1 - slot, i))
                    if not second:
                        main.append(experts(c - 2, slot))
                    main.append(feed_forward(1 - slot))
                if not last:
                    load_xa(c + 1)
                    side.append(before(c + 1, 1 - slot))
                return (MAIN_RATE, main), (SIDE_RATE, side)
            return prepare

        last, half = NCH - 1, NCH // 2
        assert NCH % 2 == 0

        def body(i, second=False):
            L.begin(i)
            scans([(i * 2 - 1, 1, stages(i * 2 - 1, 1, i, second=second)), (i * 2, 0, stages(i * 2, 0, i))])
            L.finish()
        L.begin(0)
        load_xa(0)
        Background((1, [before(0, 0)])).drain()
        scans([(0, 0, stages(0, 0, 0, first=True))])
        L.finish()
        body(1, second=True)
        with nc.Fori(2, half) as i:
            body(i)
        L.begin(half)
        scans([(last, 1, stages(last, 1, half, last=True))])
        load_xb(last, 1, half)
        Background((1, [experts(last - 1, 0), feed_forward(1), experts(last, 1)]), (1, [head_norm(1, half)])).drain()
        L.finish()
        for slot in range(2):
            nc.sync.wait_ge(s_store[slot], 16 * half + 16)
        nc.all_engine_barrier()


def layer1_phase(nc, psum, consts, I, route, x_in, x_out, normed):
    C, D, E, N, KC = 512, 256, 512, 16, 4
    KB, EB, TL, NCH = D // P, E // P, C // P, x_in.shape[0] // C
    Z = route.sizes
    NE, GR, TOP, EX = Z.ne, Z.GROUPS, Z.TOP, Z.EXPERTS
    AX = mybir.AxisListType.X
    with ExitStack() as st:
        sb = lambda name, shape: st.enter_context(nc.sbuf_tensor("c_" + name, shape, F32))
        sem = lambda name: st.enter_context(nc.semaphore("c_" + name))
        L = Lanes(nc, "c", st)
        pe, act, dve, pool, sp = L.pe, L.act, L.dve, L.pool, L.sp
        s_load, s_xa, s_xb, s_store, s_normed = sem("load"), sem("xa"), sem("xb"), sem("store"), sem("normed")
        W_in, W_dt, W_out = sb("W_in", [P, KB, 2 * E]), sb("W_dt", [P, EB, E]), sb("W_out", [P, EB, D])
        W_B = sb("W_B", [P, EB, N])
        W_router, iota = sb("W_router", [P, KB, NE]), sb("iota", [P, 32])
        chunk_mask = sb("chunk_mask", [P, NCH + 1])
        col_pack = sb("cols", [P, EB, N + KC + 3])
        A = col_pack[:, :, 0:N]
        conv_w = col_pack[:, :, N:N + KC]
        b_conv, b_dt, skip = (col_pack[:, :, N + KC + i:N + KC + i + 1] for i in range(3))
        tri, ones = route.tri, route.ones
        ident, neghalf = consts["ident"], consts["neghalf"]

        xs, dt, dtx = ([sb(f"{n}{i}", [P, EB, C]) for i in range(2)] for n in ("xs", "dt", "dtx"))
        gate = [sb(f"gate{i}", [P, TL, E]) for i in range(2)]
        B = [sb(f"B{i}", [N, C]) for i in range(2)]
        NB = 4
        b_rows = nc.dram_tensor("b_rows", (2, N, C), F32).ap()
        s_bout, s_brep = sem("bout"), [sem(f"brep{i}") for i in range(N // NB)]
        NR = 4
        Brep = sb("Brep", [P, N, C])
        da, dbx, hs = (sb(n, [P, NR, C]) for n in ("da", "dbx", "hs"))
        carry = sb("carry", [P, EB, N])
        xa, xb, xn = sb("xa", [P, TL, D]), sb("xb", [P, TL, D]), sb("xn", [P, TL, D])
        hn, xT = Shared(sb("hn", [P, TL, D])), Shared(sb("xT", [P, KB, C]))
        yT = Shared(sb("yT", [P, EB, C]))
        pre = sb("pre", [P, EB, C + KC - 1])
        tmp = sb("tmp", [P, 2, C])
        norm_buffers = [[sb(f"{n}{i}", [P, TL, *w]) for n, w in (("stats", [6]), ("mv", [2]), ("ve", []), ("rstd", []))] for i in range(2)]
        at_pick = sb("at_pick", [P, TL * GR, TOP, EX])
        place = sb("place", [P, TL, GR, TOP])
        tokens = st.enter_context(nc.sbuf_tensor("c_tokens", [P, NCH * TL], mybir.dt.int32))
        to_entry = st.enter_context(nc.sbuf_tensor("c_to_entry", [P, TL * Z.picks], mybir.dt.uint32))
        numbers = st.enter_context(nc.sbuf_tensor("c_numbers", [P, TL], mybir.dt.int32))
        s_listed = sem("listed")
        R = router_buffers(nc, st, "c", GR, EX, TOP)

        loaded = load(nc, s_load, [(W_in[:, :, :], I["c_W_in"]), (W_dt[:, :, :], I["c_W_dt"]), (W_out[:, :, :], I["c_W_out"]),
                                   (W_B[:, :, :], I["c_W_B"]), (chunk_mask[:, :], I["chunk_mask"]),
                                   (col_pack[:, :, :], I["c_cols"]), (W_router[:, :, :], I["d_router"]), (iota[:, :], I["iota"]),
                                   (tri[:, :], I["tri"])])
        nc.vector.memset(carry[:, :, :], 0.0)
        nc.vector.memset(pre[:, :, C:C + KC - 1], 0.0)
        nc.vector.memset(route.ahead[:, TL, :], 0.0)
        nc.gpsimd.dma_start(tokens[:, :], I["tokens"]).then_inc(s_listed, 16)
        nc.gpsimd.wait_ge(s_listed, 16)
        nc.vector.memset(ones[:, :], 1.0)
        nc.sync.wait_ge(s_load, loaded)
        nc.sync.sem_inc(s_store, 16)
        nc.sync.sem_inc(s_normed, 16)
        nc.all_engine_barrier()
        with nc.semaphore("c_setup") as s_setup:
            nc.scalar.activation(A, A, ACT.Exp).then_inc(s_setup, 1)
            nc.vector.wait_ge(s_setup, 1)
            nc.vector.tensor_scalar(A, A, -1.0, None, ALU.mult)
            nc.vector.tensor_scalar(col_pack[:, :, N:N + KC + 1], col_pack[:, :, N:N + KC + 1], 0.5, None, ALU.mult)
            L.prime()
            nc.all_engine_barrier()

        chunks = lambda ap: ap.rearrange("(c t p) d -> p c t d", p=P, t=TL)
        chunks_in, chunks_out, chunks_normed = chunks(x_in), chunks(x_out), chunks(normed)
        chunk_of = lambda view, c: view[:, bass.ds(c, 1), :, :].rearrange("p a t d -> p (a t) d")
        flat = lambda ap: ap.rearrange("p a b -> p (a b)")
        G, GA, YB = Banks(psum, 0, 3), Banks(psum, 3, 3), 6
        ready, scan_done, y_read = {}, [[], []], [[], []]
        pre_written, pre_read, tmp_read = [], [None] * EB, {}
        xa_read, y_free, gate_free, stored = [None], {}, [True, True], set()
        per_chunk = 16 * TL * Z.picks
        m_ahead = [None]

        def layer_norm(src, dst, stats, mv, ve, rstd):
            for t in range(TL):
                m = dve.mark(nc.vector.bn_stats(stats[:, t, :], src[:, t, :]))
            dve.after_alone(m)
            for t in range(TL):
                m = dve.mark(nc.vector.bn_aggr(mv[:, t, :], stats[:, t, :]))
            yield
            dve.after(m)
            m = dve.mark(nc.vector.tensor_scalar(ve[:, :], mv[:, :, 1], EPS_LN, None, ALU.add))
            pool.after(m)
            m = pool.mark(nc.gpsimd.tensor_tensor(rstd[:, :], ve[:, :], neghalf[:, 0:TL], ALU.pow))
            yield
            dve.after(m)
            for t in range(TL):
                m = dve.mark(nc.vector.tensor_scalar(dst[:, t, :], src[:, t, :], mv[:, t, 0:1], rstd[:, t:t + 1], ALU.subtract, ALU.mult))
            yield
            return m

        def transposed(G, src, dst, blocks):
            marks = []
            for kb in range(blocks):
                i, bank = G.take(pe)
                for t in range(TL):
                    m = nc.tensor.transpose(bank[:, t * P:(t + 1) * P], src[:, t, kb * P:(kb + 1) * P], ident[:, :])
                m = pe.mark(m)
                yield
                act.after(m)
                m = act.mark(nc.scalar.copy(dst[:, kb, :], bank))
                G.freed[i] = m
                marks.append(m)
            return marks

        def load_xa(c):
            sp.after(xa_read[0])
            nc.sync.dma_start(xa[:, :, :], chunk_of(chunks_in, c)).then_inc(s_xa, 16)

        def load_xb(c):
            sp.engine.wait_ge(s_store, c * 16 + 16)
            nc.sync.dma_start(xb[:, :, :], chunk_of(chunks_in, c)).then_inc(s_xb, 16)

        def before(c, slot):
            xs_, dt_, dtx_, gate_ = xs[slot], dt[slot], dtx[slot], gate[slot]
            dve.after(*pre_written, *pre_read)
            m_pre = dve.mark(nc.vector.tensor_scalar(pre[:, :, 0:KC - 1], pre[:, :, C:C + KC - 1], chunk_mask[:, bass.ds(c, 1)], None, ALU.mult))
            pre_written.clear()
            dve.engine.wait_ge(s_xa, c * 16 + 16)
            hn.claim(dve)
            m = yield from layer_norm(xa, hn.tensor, *norm_buffers[0])
            xa_read[0] = m
            pe.after(m)
            xT.claim(act)
            marks = yield from transposed(G, hn.tensor, xT.tensor, KB)
            hn.readers = marks
            x_T = xT.tensor
            yield
            pe.after(*marks)
            dve.after(*scan_done[slot])
            act.after(m_pre, *scan_done[slot])
            m_xs, m_gate = {}, {}

            def inner(e):
                i, bank = G.take(pe)
                m = pe.mark(matmuls(nc, bank, [(W_in[:, kb, e * P:(e + 1) * P], x_T[:, kb, :]) for kb in range(KB)]))
                yield
                act.after(m, pre_read[e])
                m = act.mark(nc.scalar.copy(pre[:, e, KC - 1:KC - 1 + C], bank))
                G.freed[i] = m
                pre_written.append(m)
                yield
                dve.after(m, m_pre)
                m = dve.mark(nc.vector.tensor_scalar(dtx_[:, e, :], pre[:, e, KC - 1:KC - 1 + C], conv_w[:, e, KC - 1:KC], b_conv[:, e, :], ALU.mult, ALU.add))
                for j in range(KC - 1):
                    yield
                    dve.after(m)
                    m = dve.mark(nc.vector.scalar_tensor_tensor(out=dtx_[:, e, :], in0=pre[:, e, j:j + C], scalar=conv_w[:, e, j:j + 1],
                                                                in1=dtx_[:, e, :], op0=ALU.mult, op1=ALU.add))
                pre_read[e] = m
                yield
                act.after(m, tmp_read.get(e % 2))
                m = act.mark(nc.scalar.activation(tmp[:, e % 2, :], dtx_[:, e, :], ACT.Tanh))
                yield
                dve.after(m)
                m_xs[e] = dve.mark(nc.vector.scalar_tensor_tensor(out=xs_[:, e, :], in0=tmp[:, e % 2, :], scalar=1.0, in1=dtx_[:, e, :],
                                                                  op0=ALU.add, op1=ALU.mult))
                tmp_read[e % 2] = m_xs[e]

            def gates(tiles):
                for t in tiles:
                    i, bank = G.take(pe)
                    m = pe.mark(matmuls(nc, bank, [(x_T[:, kb, t * P:(t + 1) * P], W_in[:, kb, E:2 * E]) for kb in range(KB)]))
                    yield
                    act.after(m, *y_read[slot])
                    m = act.mark(nc.scalar.activation(gate_[:, t, :], bank, ACT.Tanh, scale=0.5))
                    yield
                    dve.after(m)
                    m_gate[t] = dve.mark(nc.vector.scalar_tensor_tensor(out=gate_[:, t, :], in0=gate_[:, t, :], scalar=1.0, in1=bank,
                                                                        op0=ALU.add, op1=ALU.mult))
                    G.freed[i] = m_gate[t]
                    yield
            yield from abreast(inner(0), inner(1))
            while not gate_free[slot]:
                yield
            gate_free[slot] = False
            yield from abreast(inner(2), gates(range(0, 2)), inner(3))
            pe.after(m_xs[EB - 1])
            i, bank = G.take(pe)
            m = pe.mark(matmuls(nc, bank[0:N, :], [(W_B[:, e, :], xs_[:, e, :]) for e in range(EB)]))
            yield
            act.after(m)
            m = act.mark(nc.scalar.copy(B[slot][:, :], bank[0:N, :]))
            G.freed[i] = m
            sp.after(m)
            nc.sync.dma_start(b_rows[slot], B[slot][:, :]).then_inc(s_bout, 16)
            stored.add(slot)
            yield
            yield from gates(range(2, TL))
            xT.readers = list(m_gate.values())
            nc.scalar.preload_act_table_set("natural_log_exp_and_others")
            m_l, m_dtx, m_skip = {}, {}, {}

            def step_size(e):
                i, bank = G.take(pe)
                for k in range(EB):
                    m = nc.tensor.matmul(bank, W_dt[:, k, e * P:(e + 1) * P], xs_[:, k, :], start=(k == 0), stop=(k == EB - 1))
                    if k % 2:
                        m = pe.mark(m)
                        yield
                act.after(m, tmp_read.get(e % 2))
                m_z = act.mark(nc.scalar.activation(dt_[:, e, :], bank, ACT.Identity, bias=b_dt[:, e, :]))
                G.freed[i] = m_z
                act.after(m_z)
                m = act.mark(nc.scalar.activation(tmp[:, e % 2, :], dt_[:, e, :], ACT.Abs))
                yield
                act.after(m)
                m = act.mark(nc.scalar.activation(tmp[:, e % 2, :], tmp[:, e % 2, :], ACT.Exp, scale=-1.0))
                yield
                act.after(m)
                m = act.mark(nc.scalar.activation(tmp[:, e % 2, :], tmp[:, e % 2, :], ACT.Ln, bias=1.0))
                yield
                dve.after(m)
                m_l[e] = dve.mark(nc.vector.scalar_tensor_tensor(out=dt_[:, e, :], in0=dt_[:, e, :], scalar=0.0, in1=tmp[:, e % 2, :],
                                                                 op0=ALU.max, op1=ALU.add))
                tmp_read[e % 2] = m_l[e]
                yield
                dve.after(m_l[e])
                m_dtx[e] = dve.mark(nc.vector.tensor_tensor(dtx_[:, e, :], dt_[:, e, :], xs_[:, e, :], ALU.mult))
                yield
            for e in range(0, EB, 2):
                yield from abreast(step_size(e), step_size(e + 1))
            for e in range(EB):
                dve.after(m_dtx[e])
                m_skip[e] = dve.mark(nc.vector.tensor_scalar(xs_[:, e, :], xs_[:, e, :], skip[:, e, :], None, ALU.mult))
                yield
            ready[slot] = {"dt": m_l, "dtx": m_dtx, "skip": m_skip, "gate": m_gate[TL - 1]}

        def after_scan(c, slot):
            y_T = yT.tensor
            yT.claim(act)
            pe.after(*ready.get(("y", slot), []))
            marks = yield from transposed(GA, gate[slot], y_T, EB)
            y_read[slot] = marks
            gate_free[slot] = True
            yield
            pe.after(*marks)
            dve.engine.wait_ge(s_xb, c * 16 + 16)
            for half in range(2):
                i, bank = GA.take(pe)
                for t in range(2):
                    at = (2 * half + t) * P
                    m = matmuls(nc, bank[:, t * D:(t + 1) * D], [(y_T[:, e, at:at + P], W_out[:, e, :]) for e in range(EB)])
                m = pe.mark(m)
                yield
                dve.after(m)
                part = flat(xb[:, 2 * half:2 * half + 2, :])
                m = dve.mark(nc.vector.tensor_tensor(part, part, bank, ALU.add))
                GA.freed[i] = m
            yield
            sp.after(m)
            nc.sync.dma_start(chunk_of(chunks_out, c), xb[:, :, :]).then_inc(s_store, 16)
            dve.after(m)
            dve.engine.wait_ge(s_normed, c * 16 + 16)
            m = yield from layer_norm(xb, xn, *norm_buffers[1])
            sp.after(m)
            nc.sync.dma_start(chunk_of(chunks_normed, c), xn[:, :, :]).then_inc(s_normed, 16)
            pe.after(m)
            marks = yield from transposed(GA, xn, y_T, KB)
            yield
            pe.after(*marks)
            m = yield from router(nc, L, GA, y_T, W_router, R, iota, GR, EX, TOP)
            chosen = R["chosen"][:, :, :].rearrange("p (t g) e -> p t (g e)", t=TL)
            part = bass.ds(c * TL, TL)
            dve.mark(nc.vector.tensor_copy(route.picks[:, part, :].rearrange("p t k -> p (t k)"), flat(R["index_f"][:, :, :])))
            dve.mark(nc.vector.tensor_scalar(route.weights[:, part, :].rearrange("p t (g k) -> p (t g) k", g=GR), R["best"][:, :, 0:TOP], 0.5, None, ALU.mult))
            ahead = route.ahead
            dve.after(m, m_ahead[0])
            m = dve.mark(nc.vector.tensor_copy(ahead[:, 0, :], ahead[:, TL, :]))
            for t in range(TL):
                dve.after(m)
                m = dve.mark(nc.vector.tensor_tensor(ahead[:, t + 1, :], ahead[:, t, :], chosen[:, t, :], ALU.add))
            m_ahead[0] = m
            yield
            pe.after(m)
            i, bank = GA.take(pe)
            ranks = bank[:, 0:TL * NE]
            m_rank = pe.mark(matmuls(nc, ranks, [(tri[:, :], R["chosen"][:, :, :].rearrange("p r e -> p (r e)")),
                                                 (ones[:, :], ahead[:, 0:TL, :].rearrange("p t e -> p (t e)"))]))
            yT.readers = [m_rank]
            yield
            dve.after(m_rank)
            m = dve.mark(nc.vector.tensor_tensor(
                at_pick[:, :, :, :], R["onehot"][:, :, :, :],
                ranks.rearrange("p (r e) -> p r e", e=EX).unsqueeze(2).broadcast_to([P, TL * GR, TOP, EX]), ALU.mult))
            GA.freed[i] = m
            yield
            dve.after(m)
            m = dve.mark(nc.vector.tensor_reduce(flat(place[:, :, :, :].rearrange("p t g k -> p t (g k)")), at_pick[:, :, :, :].rearrange("p r s e -> p (r s) e"), AX, ALU.add))
            dve.after(m)
            dve.mark(nc.vector.tensor_copy(route.ranks[:, part, :].rearrange("p t k -> p (t k)"), flat(place[:, :, :, :].rearrange("p t g k -> p t (g k)"))))
            m = dve.mark(nc.vector.scalar_tensor_tensor(out=place[:, :, :, :].rearrange("p t g k -> p (t g) k"), in0=R["index_f"][:, :, :], scalar=float(Z.capacity),
                                                        in1=place[:, :, :, :].rearrange("p t g k -> p (t g) k"), op0=ALU.mult, op1=ALU.add))
            for g in range(1, GR):
                dve.after(m)
                m = dve.mark(nc.vector.tensor_scalar(place[:, :, g, :], place[:, :, g, :], float(g * EX * Z.capacity), None, ALU.add))
            yield
            dve.after(m)
            dve.engine.wait_ge(s_listed, c * per_chunk + 16)
            dve.mark(nc.vector.tensor_copy(to_entry[:, :], flat(place[:, :, :, :].rearrange("p t g k -> p t (g k)"))))
            m = dve.mark(nc.vector.tensor_copy(numbers[:, :], tokens[:, part]))
            yield
            pool.after_alone(m)
            for t in range(TL):
                for k in range(Z.picks):
                    at = t * Z.picks + k
                    nc.gpsimd.indirect_dma_start(out=route.lists, out_offset=bass.IndirectOffsetOnAxis(ap=to_entry[:, at:at + 1], axis=0),
                                                 in_=numbers[:, t:t + 1], in_offset=None, bounds_check=Z.entries - 1).then_inc(s_listed, 16)
                    yield

        steps = EB * N
        m_da, m_dbx, m_scan, m_sum, m_kept, m_y = ({} for _ in range(6))
        AFTER_RATE, BEFORE_RATE, AHEAD, SETTLE = 0.5, 1.3, 2, 5

        def scans(chunks):
            done_of, count = {}, len(chunks)
            for g in range(count * steps + AHEAD + SETTLE):
                j = min(g // steps, count - 1)
                s = g - j * steps
                if s == 0:
                    c, slot, prepare = chunks[j]
                    if j > 0:
                        background.drain(until=lambda: slot in stored)
                    stored.discard(slot)
                    sp.engine.wait_ge(s_bout, c * 16 + 16)
                    for k in range(N // NB):
                        sp.after(m_dbx.get(g - N + (k + 1) * NB - 1))
                        nc.sync.dma_start(Brep[:, k * NB:(k + 1) * NB, :], b_rows[slot, k * NB:(k + 1) * NB, :].partition_broadcast(P)).then_inc(s_brep[k], 16)
                    if j > 0:
                        background.drain()
                    streams = prepare()
                    done_of[j] = ready.get(slot, {"dt": {}, "dtx": {}, "skip": {}, "gate": None})
                if s == SETTLE:
                    background = Background(*streams)
                if g < count * steps:
                    (e, n), slot, done = divmod(s, N), chunks[j][1], done_of[j]
                    if e == 0 and n % NB == 0:
                        pool.engine.wait_ge(s_brep[n // NB], chunks[j][0] * 16 + 16)
                    pool.after(done["dtx"].get(e), m_scan.get(g - NR))
                    m_dbx[g] = pool.mark(nc.gpsimd.tensor_tensor(dbx[:, g % NR, :], dtx[slot][:, e, :], Brep[:, n, :], ALU.mult))
                    act.after(done["dt"].get(e))
                    act.after(m_scan.get(g - NR))
                    m_da[g] = act.mark(nc.scalar.activation(da[:, g % NR, :], dt[slot][:, e, :], ACT.Exp, scale=A[:, e, n:n + 1]))
                q = g - AHEAD
                if 0 <= q < count * steps:
                    e, n = divmod(q % steps, N)
                    if n == 0:
                        dve.after(m_kept.get(q - steps + N - 1))
                        m_carry = dve.mark(nc.vector.tensor_scalar(carry[:, e, :], carry[:, e, :], chunk_mask[:, bass.ds(chunks[q // steps][0], 1)], None, ALU.mult))
                        dve.after(m_carry)
                    dve.after(m_da[q], m_dbx[q], m_sum.get(q - NR), m_kept.get(q - NR))
                    m_scan[q] = dve.mark(nc.vector.tensor_tensor_scan(hs[:, q % NR, :], da[:, q % NR, :], dbx[:, q % NR, :], carry[:, e, n:n + 1],
                                                                      ALU.mult, ALU.add))
                q = g - AHEAD - 1
                if 0 <= q < count * steps:
                    (e, n), slot, done = divmod(q % steps, N), chunks[q // steps][1], done_of[q // steps]
                    act.after(m_scan[q])
                    m_kept[q] = act.mark(nc.scalar.copy(carry[:, e, n:n + 1], hs[:, q % NR, C - 1:C]))
                    pe.after(m_scan[q])
                    if n == 0:
                        pe.after(y_free.get(e % 2), done["skip"].get(e))
                        for t in range(TL):
                            nc.tensor.matmul(psum[:, YB + e % 2, t * P:(t + 1) * P], xs[slot][:, e, t * P:(t + 1) * P], ident[:, :],
                                             is_transpose=True, start=(t == 0), stop=False, skip_group_check=True)
                    for t in range(TL):
                        last = nc.tensor.matmul(psum[:, YB + e % 2, t * P:(t + 1) * P], hs[:, q % NR, t * P:(t + 1) * P], ident[:, :],
                                                is_transpose=True, start=False, stop=(n == N - 1 and t == TL - 1), skip_group_check=True)
                    m_sum[q] = pe.mark(last)
                q = g - AHEAD - 3
                if 0 <= q < count * steps and q % N == N - 1:
                    e, slot, done = q % steps // N, chunks[q // steps][1], done_of[q // steps]
                    dve.after(m_sum[q], done["gate"])
                    m_y[e] = dve.mark(nc.vector.scalar_tensor_tensor(
                        out=gate[slot][:, :, e * P:(e + 1) * P], in0=psum[:, YB + e % 2, :].rearrange("p (t d) -> p t d", t=TL), scalar=0.5,
                        in1=gate[slot][:, :, e * P:(e + 1) * P], op0=ALU.mult, op1=ALU.mult))
                    y_free[e % 2] = m_y[e]
                    if e == EB - 1:
                        scan_done[slot] = [m_dbx[q], m_da[q], m_sum[q]]
                        ready[("y", slot)] = [m_y[e]]
                if g < count * steps and s >= SETTLE:
                    background.pull()
            background.drain()
            for marks in (m_da, m_dbx, m_scan, m_sum, m_kept, m_y, y_free):
                marks.clear()

        def stages(c, slot, first=False, last=False):
            def prepare():
                streams = []
                if not first:
                    load_xb(c - 1)
                    streams.append((AFTER_RATE, [after_scan(c - 1, 1 - slot)]))
                if not last:
                    load_xa(c + 1)
                    streams.append((BEFORE_RATE, [before(c + 1, 1 - slot)]))
                return streams
            return prepare

        last = NCH - 1
        assert NCH % 2 == 0
        L.begin(0)
        load_xa(0)
        Background((1, [before(0, 0)])).drain()
        scans([(0, 0, stages(0, 0, first=True))])
        L.finish()
        with nc.Fori(1, NCH // 2) as i:
            L.begin(i)
            scans([(i * 2 - 1, 1, stages(i * 2 - 1, 1)), (i * 2, 0, stages(i * 2, 0))])
            L.finish()
        L.begin(NCH // 2)
        scans([(last, 1, stages(last, 1, last=True))])
        load_xb(last)
        Background((1, [after_scan(last, 1)])).drain()
        L.finish()
        nc.sync.wait_ge(s_store, 16 * NCH + 16)
        nc.sync.wait_ge(s_normed, 16 * NCH + 16)
        nc.sync.wait_ge(s_listed, NCH * per_chunk + 16)
        nc.all_engine_barrier()


def router(nc, L, G, xT, W_router, R, iota, groups, experts, top):
    TL, KB = 4, 2
    NE = groups * experts
    pe, act, dve = L.pe, L.act, L.dve
    rows = TL * groups
    i, bank = G.take(pe)
    for t in range(TL):
        m = matmuls(nc, bank[:, t * NE:(t + 1) * NE], [(xT[:, kb, t * P:(t + 1) * P], W_router[:, kb, :]) for kb in range(KB)])
    m = pe.mark(m)
    act.after(m)
    m = act.mark(nc.scalar.copy(R["prob"][:, :, :].rearrange("p r e -> p (r e)"), bank[:, 0:TL * NE]))
    G.freed[i] = m
    yield
    dve.after(m)
    m = dve.mark(nc.vector.tensor_reduce(R["peak"][:, :], R["prob"][:, :, :], mybir.AxisListType.X, ALU.max))
    dve.after(m)
    m = dve.mark(nc.vector.tensor_tensor(R["prob"][:, :, :], R["prob"][:, :, :], R["peak"][:, :].unsqueeze(2).broadcast_to([P, rows, experts]), ALU.subtract))
    yield
    act.after(m)
    m = act.mark(nc.scalar.activation(R["prob"][:, :, :], R["prob"][:, :, :], ACT.Exp))
    yield
    dve.after(m)
    m = dve.mark(nc.vector.tensor_reduce(R["total"][:, :], R["prob"][:, :, :], mybir.AxisListType.X, ALU.add))
    dve.after(m)
    m = dve.mark(nc.vector.reciprocal(R["total"][:, :], R["total"][:, :]))
    dve.after(m)
    m = dve.mark(nc.vector.tensor_tensor(R["prob"][:, :, :], R["prob"][:, :, :], R["total"][:, :].unsqueeze(2).broadcast_to([P, rows, experts]), ALU.mult))
    yield
    dve.after_alone(m)
    for r in range(rows):
        m = dve.mark(nc.vector.max(R["best"][:, r, :], R["prob"][:, r, :]))
        if r == rows // 2 - 1:
            yield
    yield
    dve.after_alone(m)
    for r in range(rows):
        m = dve.mark(nc.vector.max_index(R["index"][:, r, :], R["best"][:, r, :], R["prob"][:, r, :]))
        if r == rows // 2 - 1:
            yield
    yield
    dve.after(m)
    m = dve.mark(nc.vector.tensor_copy(R["index_f"][:, :, :], R["index"][:, :, 0:top]))
    dve.after(m)
    m = dve.mark(nc.vector.tensor_tensor(R["onehot"][:, :, :, :], iota[:, 0:experts].unsqueeze(1).unsqueeze(1).broadcast_to([P, rows, top, experts]),
                                         R["index_f"][:, :, :].unsqueeze(3).broadcast_to([P, rows, top, experts]), ALU.is_equal))
    dve.after(m)
    yield
    return dve.mark(nc.vector.tensor_reduce(R["chosen"][:, :, :], R["onehot"][:, :, :, :].rearrange("p r s e -> p r e s"), mybir.AxisListType.X, ALU.add))


def router_buffers(nc, st, name, groups, experts, top):
    rows = 4 * groups
    shapes = {"peak": [P, rows], "total": [P, rows], "prob": [P, rows, experts], "best": [P, rows, 8], "index_f": [P, rows, top],
              "onehot": [P, rows, top, experts], "chosen": [P, rows, experts]}
    R = {n: st.enter_context(nc.sbuf_tensor(f"{name}_{n}", s, F32)) for n, s in shapes.items()}
    R["mv"] = st.enter_context(nc.sbuf_tensor(f"{name}_router_mv", [P, 4, 2], F32))
    R["rstd"] = st.enter_context(nc.sbuf_tensor(f"{name}_router_rstd", [P, 4], F32))
    R["index"] = st.enter_context(nc.sbuf_tensor(f"{name}_index", [P, rows, 8], mybir.dt.uint32))
    return R


class SortedExperts:
    GROUPS, EXPERTS, TOP, SLOTS, UNROLL, RING = 2, 32, 2, 256, 24, 8

    def __init__(self, tokens):
        self.picks = self.GROUPS * self.TOP
        self.ne = self.GROUPS * self.EXPERTS
        self.capacity = tokens
        self.tiles = tokens * self.picks // self.SLOTS + self.ne
        assert self.tiles % self.UNROLL == 0 and self.tiles + self.RING <= 2 * P and self.UNROLL % self.RING == 0
        whole = P * 256
        self.entries = -(-(self.ne * self.capacity + 2 * P * self.SLOTS) // whole) * whole


class Route:

    def __init__(self, nc, st, tokens, lists):
        Z = self.sizes = SortedExperts(tokens)
        self.lists = lists
        sb = lambda name, shape: st.enter_context(nc.sbuf_tensor("route_" + name, shape, F32))
        self.picks, self.weights, self.ranks, self.rows = (sb(n, [P, tokens // P, Z.picks]) for n in ("picks", "weights", "ranks", "rows"))
        self.ahead = sb("ahead", [P, 5, Z.ne])
        self.tri, self.ones = sb("tri", [P, P]), sb("ones", [P, P])


def sorted_experts_phase(nc, psum, consts, I, route, x_in, normed, out, sorted_y, tile_list):
    Z = route.sizes
    C, D = 512, 256
    KB, TL, TT = D // P, C // P, x_in.shape[0] // P
    NCH, PK, NE, E, TOP, GR, SL = TT // TL, Z.picks, Z.ne, Z.EXPERTS, Z.TOP, Z.GROUPS, Z.SLOTS
    U32, I32, AX = mybir.dt.uint32, mybir.dt.int32, mybir.AxisListType.X
    flat = lambda ap: ap.rearrange("p a b -> p (a b)")
    chunk_of = lambda ap, c: ap.rearrange("(c t p) d -> p c t d", p=P, t=TL)[:, bass.ds(c, 1), :, :].rearrange("p a t d -> p (a t) d")
    picks, weights, ranks, rows, ones = route.picks, route.weights, route.ranks, route.rows, route.ones
    before = route.ahead[:, TL, :]
    with ExitStack() as st:
        sb = lambda name, shape, dt=F32: st.enter_context(nc.sbuf_tensor("d_" + name, shape, dt))
        s_load = st.enter_context(nc.semaphore("d_load"))
        iota, tile_no = sb("iota", [P, 32]), sb("tile_no", [P, 2])
        base, ends, in_tiles, work = (sb(n, [P, NE]) for n in ("base", "ends", "in_tiles", "work"))
        whole = sb("whole", [P, NE], I32)
        firsts, of_col, of_int = sb("firsts", [P, 2]), sb("of_col", [P, 4]), sb("of_int", [P, 4], I32)
        of_tile = sb("of_tile", [1, 4 * P], I32)
        loaded = load(nc, s_load, [(iota[:, :], I["iota"]), (tile_no[:, :], I["tile_no"])])
        nc.sync.wait_ge(s_load, loaded)
        nc.all_engine_barrier()

        with nc.semaphore("d_place") as s_place, nc.semaphore("d_list") as s_list:
            steps = [0]

            def then(instruction):
                steps[0] += 1
                instruction.then_inc(s_place, 1)
                nc.vector.wait_ge(s_place, steps[0])
            counts = psum[:, 0, 0:NE]
            then(nc.tensor.matmul(counts, ones[:, :], before, start=True, stop=True))
            then(nc.vector.tensor_scalar(work[:, :], counts, float(SL - 1), None, ALU.add))
            then(nc.vector.tensor_copy(whole[:, :], work[:, :]))
            then(nc.vector.tensor_scalar(whole[:, :], whole[:, :], SL.bit_length() - 1, None, ALU.arith_shift_right))
            then(nc.vector.tensor_copy(in_tiles[:, :], whole[:, :]))
            then(nc.vector.tensor_tensor_scan(ends[:, :], ones[:, 0:NE], in_tiles[:, :], 0.0, ALU.mult, ALU.add))
            then(nc.vector.tensor_tensor(base[:, :], ends[:, :], in_tiles[:, :], ALU.subtract))
            then(nc.vector.tensor_scalar(base[:, :], base[:, :], float(SL), None, ALU.mult))
            for j in range(2):
                then(nc.vector.tensor_scalar(work[:, :], ends[:, :], tile_no[:, j:j + 1], None, ALU.is_le))
                then(nc.vector.tensor_reduce(of_col[:, j:j + 1], work[:, :], AX, ALU.add))
                then(nc.vector.tensor_tensor(work[:, :], work[:, :], in_tiles[:, :], ALU.mult))
                then(nc.vector.tensor_reduce(firsts[:, j:j + 1], work[:, :], AX, ALU.add))
            then(nc.vector.tensor_scalar(of_col[:, 0:2], of_col[:, 0:2], float(NE - 1), None, ALU.min))
            then(nc.vector.tensor_tensor(firsts[:, :], tile_no[:, :], firsts[:, :], ALU.subtract))
            then(nc.vector.scalar_tensor_tensor(out=of_col[:, 2:4], in0=of_col[:, 0:2], scalar=float(Z.capacity // SL), in1=firsts[:, :], op0=ALU.mult, op1=ALU.add))
            then(nc.vector.tensor_copy(of_int[:, :], of_col[:, :]))
            nc.sync.wait_ge(s_place, steps[0])
            with nc.allow_non_contiguous_dma(reason="512 numbers, once"):
                for j in range(4):
                    nc.sync.dma_start(tile_list[j * P:(j + 1) * P].rearrange("(p a) -> p a", a=1), of_int[:, j:j + 1]).then_inc(s_list, 16)
            nc.sync.wait_ge(s_list, 64)
            nc.sync.dma_start(of_tile[:, :], tile_list.rearrange("(a n) -> a n", a=1)).then_inc(s_list, 16)
            nc.sync.wait_ge(s_list, 80)
            nc.all_engine_barrier()

        with ExitStack() as s3:
            sb3 = lambda name, shape: s3.enter_context(nc.sbuf_tensor("d3_" + name, shape, F32))
            L = Lanes(nc, "d3", s3)
            RN, UN, HB = Z.RING, Z.UNROLL, SL // P
            xs, w, ys = sb3("xs", [P, RN, HB, D]), sb3("w", [P, RN, 2 * KB * P + D]), sb3("ys", [P, RN, HB, D])
            xT, hg = sb3("xT", [P, 3, KB, SL]), sb3("hg", [P, 3, SL])
            onehot, start = sb3("onehot", [P, TL * GR, TOP, E]), sb3("start", [P, TL * PK])
            entries = [s3.enter_context(nc.sbuf_tensor(f"d3_entries{i}", [P, HB], I32)) for i in range(RN)]
            s_x, s_w, s_y, s_e = ([s3.enter_context(nc.semaphore(f"d3_{n}{i}")) for i in range(RN)] for n in "xwye")
            entries_in = route.lists.rearrange("(l p h) a -> l p (h a)", p=P, h=HB)
            rows_out = sorted_y.rearrange("(j p h) d -> j p h d", p=P, h=HB)
            weights_in = I["d_experts"]

            def fetch_weights(j, slot):
                e = nc.sync.value_load(of_tile[0:1, bass.ds(j, 1)], min_val=0, max_val=NE - 1)
                nc.sync.dma_start(w[:, slot, :], weights_in[bass.ds(e, 1), :, :].rearrange("a p n -> p (a n)")).then_inc(s_w[slot], 16)

            def fetch_entries(j, slot):
                at = nc.sync.value_load(of_tile[0:1, bass.ds(j + 2 * P, 1)], min_val=0, max_val=Z.entries // SL - 1)
                nc.sync.dma_start(entries[slot][:, :], entries_in[bass.ds(at, 1), :, :].rearrange("a p h -> p (a h)")).then_inc(s_e[slot], 16)

            def gather(slot):
                for h in range(HB):
                    nc.gpsimd.indirect_dma_start(out=xs[:, slot, h, :], out_offset=None, in_=normed,
                                                 in_offset=bass.IndirectOffsetOnAxis(ap=entries[slot][:, h:h + 1], axis=0),
                                                 bounds_check=x_in.shape[0] - 1).then_inc(s_x[slot], 16)

            def rows_of(c):
                part = bass.ds(c * TL, TL)
                by_group = lambda ap: ap[:, part, :].rearrange("p t (g k) -> p (t g) k", g=GR)
                base_of = base[:, :].rearrange("p (g e) -> p g e", g=GR).unsqueeze(2).broadcast_to([P, GR, TOP, E])
                m = dve.mark(nc.vector.tensor_tensor(
                    onehot[:, :, :, :], iota[:, 0:E].unsqueeze(1).unsqueeze(1).broadcast_to([P, TL * GR, TOP, E]),
                    by_group(picks).unsqueeze(3).broadcast_to([P, TL * GR, TOP, E]), ALU.is_equal))
                dve.after(m)
                for t in range(TL):
                    mine = onehot[:, t * GR:(t + 1) * GR, :, :]
                    m = dve.mark(nc.vector.tensor_tensor(mine, mine, base_of, ALU.mult))
                dve.after(m)
                m = dve.mark(nc.vector.tensor_reduce(start[:, :], onehot[:, :, :, :].rearrange("p r s e -> p (r s) e"), AX, ALU.add))
                dve.after(m)
                m = dve.mark(nc.vector.tensor_tensor(start[:, :], start[:, :], ranks[:, part, :].rearrange("p t k -> p (t k)"), ALU.add))
                dve.after(m)
                dve.after(dve.mark(nc.vector.tensor_copy(rows[:, part, :].rearrange("p t k -> p (t k)"), start[:, :])))

            L.prime()
            for slot in range(RN):
                fetch_entries(slot, slot)
                fetch_weights(slot, slot)
                nc.sync.sem_inc(s_y[slot], 16)
            for slot in range(RN):
                nc.gpsimd.wait_ge(s_e[slot], 16)
                nc.gpsimd.sem_inc(L.pool.pause, 1)
                gather(slot)
            nc.all_engine_barrier()
            CB = NCH * UN // Z.tiles
            assert CB * Z.tiles == NCH * UN
            TB, GU, DN = Banks(psum, 0, 2), Banks(psum, 2, 3), Banks(psum, 5, 3)
            pe, act, dve, pool, sp = L.pe, L.act, L.dve, L.pool, L.sp
            w_gate = lambda slot, kb: w[:, slot, kb * P:(kb + 1) * P]
            w_up = lambda slot, kb: w[:, slot, (KB + kb) * P:(KB + kb + 1) * P]
            w_down = lambda slot: w[:, slot, 2 * KB * P:]
            with nc.Fori(0, Z.tiles // UN) as i:
                L.begin(i)
                for b in (TB, GU, DN):
                    b.begin()
                m_xT, m_gu, m_h, m_dn = {}, {}, {}, {}
                uses = UN // RN
                for k in range(CB):
                    rows_of(i * CB + k)
                for s in range(UN + 2):
                    if s < UN:
                        slot, use = s % RN, s // RN
                        pe.engine.wait_ge(s_x[slot], i * (16 * HB * uses) + 16 * HB * (use + 1))
                        b, bank = TB.take(pe)
                        for kb in range(KB):
                            for h in range(HB):
                                m = nc.tensor.transpose(bank[:, kb * SL + h * P:kb * SL + (h + 1) * P], xs[:, slot, h, kb * P:(kb + 1) * P], consts["ident"][:, :])
                        m = pe.mark(m)
                        sp.after(m)
                        fetch_entries(i * UN + s + RN, slot)
                        pool.after(m)
                        pool.engine.wait_ge(s_e[slot], i * (16 * uses) + 16 * (use + 2))
                        nc.gpsimd.sem_inc(pool.pause, 1)
                        gather(slot)
                        act.after(m, m_gu.get(s - 3))
                        m_xT[s] = act.mark(nc.scalar.copy(xT[:, s % 3, :, :].rearrange("p k c -> p (k c)"), bank))
                        TB.freed[b] = m_xT[s]
                    q = s - 1
                    if 0 <= q < UN:
                        slot, use = q % RN, q // RN
                        pe.engine.wait_ge(s_w[slot], i * (16 * uses) + 16 * (use + 1))
                        b, bank = GU.take(pe)
                        pe.after(m_xT[q])
                        for half, wt in enumerate((w_gate, w_up)):
                            m = matmuls(nc, bank[:, half * SL:(half + 1) * SL], [(wt(slot, kb), xT[:, q % 3, kb, :]) for kb in range(KB)])
                        m_gu[q] = pe.mark(m)
                        act.after(m_gu[q], m_dn.get(q - 3))
                        m = act.mark(nc.scalar.activation(hg[:, q % 3, :], bank[:, 0:SL], ACT.Silu))
                        dve.after(m)
                        m_h[q] = dve.mark(nc.vector.tensor_tensor(hg[:, q % 3, :], hg[:, q % 3, :], bank[:, SL:2 * SL], ALU.mult))
                        GU.freed[b] = m_h[q]
                    q = s - 2
                    if 0 <= q < UN:
                        slot, use = q % RN, q // RN
                        b, bank = DN.take(pe)
                        pe.after(m_h[q])
                        for h in range(HB):
                            m = nc.tensor.matmul(bank[:, h * D:(h + 1) * D], hg[:, q % 3, h * P:(h + 1) * P], w_down(slot), start=True, stop=True)
                        m_dn[q] = pe.mark(m)
                        dve.after(m_dn[q])
                        dve.engine.wait_ge(s_y[slot], i * (16 * uses) + 16 * (use + 1))
                        m = dve.mark(nc.vector.tensor_copy(ys[:, slot, :, :].rearrange("p h d -> p (h d)"), bank))
                        DN.freed[b] = m
                        sp.after(m_dn[q])
                        fetch_weights(i * UN + q + RN, slot)
                        sp.after(m)
                        nc.sync.dma_start(rows_out[bass.ds(i * UN + q, 1), :, :, :].rearrange("a p h d -> p (a h) d"), ys[:, slot, :, :]).then_inc(s_y[slot], 16)
                L.finish()
            for slot in range(RN):
                nc.sync.wait_ge(s_y[slot], 16 * (Z.tiles // RN + 1))
                nc.sync.wait_ge(s_x[slot], 16 * HB * (Z.tiles // RN + 1))
                nc.sync.wait_ge(s_e[slot], 16 * (Z.tiles // RN + 1))
                nc.sync.wait_ge(s_w[slot], 16 * (Z.tiles // RN + 1))
            nc.all_engine_barrier()

        with ExitStack() as s4:
            L = Lanes(nc, "d4", s4)
            NS = 4
            sb4 = lambda name, shape, dt=F32: s4.enter_context(nc.sbuf_tensor("d4_" + name, shape, dt))
            got, x = ([sb4(f"{n}{i}", s) for i in range(NS)] for n, s in (("got", [P, TL * PK, D]), ("x", [P, TL, D])))
            from_row = sb4("from_row", [P, TT * PK], U32)
            s_got = [[s4.enter_context(nc.semaphore(f"d4_got{i}_{t}")) for t in range(TL)] for i in range(NS)]
            s_x, s_out = ([s4.enter_context(nc.semaphore(f"d4_{n}{i}")) for i in range(NS)] for n in ("x", "out"))
            out_view = out.rearrange("b t d -> (b t) d")
            L.prime()
            for slot in range(NS):
                nc.sync.sem_inc(s_out[slot], 16)
            nc.vector.tensor_copy(from_row[:, :], flat(rows[:, :, :]))
            nc.all_engine_barrier()
            pool, dve, sp = L.pool, L.dve, L.sp
            to_read = sb4("to_read", [P, NS * TL * PK], U32)
            with nc.Fori(0, NCH // NS) as i:
                L.begin(i)
                m_rows = dve.mark(nc.vector.tensor_copy(to_read[:, :], from_row[:, bass.ds(i * (NS * TL * PK), NS * TL * PK)]))
                for slot in range(NS):
                    c = i * NS + slot
                    sp.engine.wait_ge(s_out[slot], i * 16 + 16)
                    nc.sync.sem_inc(sp.pause, 1)
                    nc.sync.dma_start(x[slot][:, :, :], chunk_of(x_in, c)).then_inc(s_x[slot], 16)
                pool.after_alone(m_rows)
                for slot in range(NS):
                    for t in range(TL):
                        for k in range(PK):
                            at = (slot * TL + t) * PK + k
                            nc.gpsimd.indirect_dma_start(out=got[slot][:, t * PK + k, :], out_offset=None, in_=sorted_y,
                                                         in_offset=bass.IndirectOffsetOnAxis(ap=to_read[:, at:at + 1], axis=0),
                                                         bounds_check=Z.tiles * SL - 1).then_inc(s_got[slot][t], 16)
                for slot in range(NS):
                    c = i * NS + slot
                    dve.engine.wait_ge(s_x[slot], i * 16 + 16)
                    for t in range(TL):
                        dve.engine.wait_ge(s_got[slot][t], i * (16 * PK) + 16 * PK)
                        for k in range(PK):
                            m = dve.mark(nc.vector.scalar_tensor_tensor(out=x[slot][:, t, :], in0=got[slot][:, t * PK + k, :],
                                                                        scalar=weights[:, bass.ds(c * TL + t, 1), k:k + 1].rearrange("p a b -> p (a b)"),
                                                                        in1=x[slot][:, t, :], op0=ALU.mult, op1=ALU.add))
                            dve.after(m)
                    sp.after(m)
                    nc.sync.dma_start(chunk_of(out_view, c), x[slot][:, :, :]).then_inc(s_out[slot], 16)
                L.finish()
            for slot in range(NS):
                nc.sync.wait_ge(s_out[slot], 16 * (NCH // NS) + 16)
            nc.all_engine_barrier()


def build(nc, I, out):
    with ExitStack() as st:
        T, D = out.shape[0] * out.shape[1], out.shape[2]
        consts = {"ident": st.enter_context(nc.sbuf_tensor("ident", [P, P], F32)),
                  "neghalf": st.enter_context(nc.sbuf_tensor("neghalf", [P, 4], F32))}
        psum = st.enter_context(nc.psum_tensor("psum", [P, 8, 512], F32))
        x2, x3, normed = (nc.dram_tensor(n, (T, D), F32).ap() for n in ("x2", "x3", "normed"))
        Z = SortedExperts(T)
        sorted_y = nc.dram_tensor("sorted_y", (Z.tiles * Z.SLOTS, D), F32).ap()
        tile_list = nc.dram_tensor("tile_list", (4 * P,), mybir.dt.int32).ap()
        lists = nc.dram_tensor("lists", (Z.entries, 1), mybir.dt.int32).ap()
        s_clear = st.enter_context(nc.semaphore("s_clear"))
        zeros = st.enter_context(nc.sbuf_tensor("zeros", [P, 256], mybir.dt.int32))
        nc.vector.memset(zeros[:, :], 0)
        nc.all_engine_barrier()
        view = lists.rearrange("(n p k) a -> p n (k a)", p=P, k=zeros.shape[1])
        nc.sync.dma_start(view, zeros[:, :].unsqueeze(1).broadcast_to([P, view.shape[1], zeros.shape[1]])).then_inc(s_clear, 16)
        layer0_phase(nc, psum, consts, I, I["L0_attn_x"], x2)
        nc.sync.wait_ge(s_clear, 16)
        nc.all_engine_barrier()
        route = Route(nc, st, T, lists)
        layer1_phase(nc, psum, consts, I, route, x2, x3, normed)
        sorted_experts_phase(nc, psum, consts, I, route, x3, normed, out, sorted_y, tile_list)


def shape_constants():
    import numpy as np
    dk, per_seq, chunks = 16, 4, 16
    p = np.arange(P)
    mask = np.tile((np.arange(chunks + 1) % per_seq != 0)[None, :], (P, 1))
    tile_no = p[:, None] + P * np.arange(2)[None, :]
    return {"tri": (p[:, None] < p[None, :]).astype(np.float32), "tile_no": tile_no.astype(np.float32),
            "tokens": (p[:, None] + P * np.arange(per_seq * chunks)[None, :]).astype(np.int32),
            "iota": np.tile(np.arange(32, dtype=np.float32), (P, 1)), "ident": np.eye(P, dtype=np.float32),
            "head_of": (p[:, None] // dk == np.arange(P // dk)[None, :]).astype(np.float32), "chunk_mask": mask.astype(np.float32)}


def by_rows(w):
    return w.reshape(-1, P, w.shape[-1]).transpose(1, 0, 2)


def layouts(i):
    import numpy as np
    i = {k: np.asarray(v) for k, v in i.items()}
    a = {n: i["L0_attn_" + n] for n in ("Wr", "Wk", "Wv", "Wg", "Wo", "wA")}
    a["w1"], a["w2"] = i["L0_attn_ffn_w1"], i["L0_attn_ffn_w2"]
    d = {"a_" + k: by_rows(v) for k, v in a.items()}
    d["a_cols"] = np.stack([i["L0_attn_" + n].reshape(-1, P).T for n in A_COLS], axis=1)
    c = {n: i["L1_attn_" + n] for n in ("W_in", "W_dt", "W_out", "W_x", "W_conv", "A_log", "b_conv", "b_dt", "D")}
    d["c_W_in"], d["c_W_dt"], d["c_W_out"] = (by_rows(c[n].T) for n in ("W_in", "W_dt", "W_out"))
    d["c_W_B"] = by_rows(c["W_x"][c["W_x"].shape[0] // 2:].T)
    rows = np.concatenate([c["A_log"], c["W_conv"][:, 0, :]] + [c[n][:, None] for n in ("b_conv", "b_dt", "D")], axis=1)
    d["c_cols"] = by_rows(rows)
    experts = []
    for g in "01":
        for n in ("wg", "wu"):
            a = i[f"L1_ffn_{n}{g}"]
            experts.append(a.reshape(a.shape[0], -1, P, P).transpose(0, 2, 1, 3).reshape(a.shape[0], P, -1))
        experts.append(i[f"L1_ffn_wd{g}"])
    d["d_experts"] = np.concatenate([np.concatenate(experts[0:3], axis=2), np.concatenate(experts[3:6], axis=2)])
    d["d_router"] = by_rows(np.concatenate([i["L1_ffn_router_w0"], i["L1_ffn_router_w1"]], axis=1))
    up = np.concatenate([i["L0_ffn_shared_up"], i["L0_ffn_routed_up"]])
    down = np.concatenate([i["L0_ffn_shared_down"], i["L0_ffn_routed_down"]])
    d["b_up"] = up.reshape(up.shape[0], P, -1, P).transpose(3, 0, 2, 1)
    d["b_down"] = down.transpose(2, 0, 1)
    d["b_router"] = by_rows(i["L0_ffn_router_w"].T)
    d["a_gn_w"], d["a_gn_b"] = i["L0_attn_gn_w"].reshape(-1), i["L0_attn_gn_b"].reshape(-1)
    d["L0_attn_wB"] = i["L0_attn_wB"]
    d["L0_attn_x"] = i["L0_attn_x"]
    return d


def kernel(**inputs):
    import numpy as _np
    import concourse.bacc as _bacc
    from concourse import mybir as _mybir
    from concourse.bass_utils import run_bass_kernel_spmd as _run

    nc = _bacc.Bacc("TRN2", target_bir_lowering=False, num_devices=1)
    nc.disable_value_cache = True
    arrays, aps = {}, {}
    for name, a in list(layouts(inputs).items()) + list(shape_constants().items()):
        a = _np.ascontiguousarray(a)
        arrays[f"in_{name}"] = a
        aps[name] = nc.dram_tensor(f"in_{name}", a.shape, _mybir.dt.from_np(a.dtype), kind="ExternalInput").ap()
    out = nc.dram_tensor("out_x", inputs["L0_attn_x"].shape, _mybir.dt.float32, kind="ExternalOutput").ap()
    build(nc, aps, out)
    r = _run(nc, [arrays], core_ids=[0])
    return r.results[0]["out_x"]
```
